# Optimizing a Trainium2 kernel written in Bass

```python
import numpy as np
import jax
import jax.numpy as jnp

def _softmax(x, axis=-1):
    return jax.nn.softmax(x, axis=axis)

def _gelu(x):
    return jax.nn.gelu(x, approximate=True)

def _silu(x):
    return jax.nn.silu(x)

def _sigmoid(x):
    return jax.nn.sigmoid(x)

def _layernorm(x, axis=-1, eps=1e-05):
    m = jnp.mean(x, axis=axis, keepdims=True)
    v = jnp.var(x, axis=axis, keepdims=True)
    return (x - m) / jnp.sqrt(v + eps)

def _scatter_add(tgt, idx, src, axis=0):
    return tgt.at[idx].add(src)

def _segment_sum(src, seg, n):
    return jax.ops.segment_sum(src, seg, n)
kernel_name = 'mk_perceiver_d2_seqx_r2_d228d8'

def setup_inputs(seed: int=0):
    np.random.seed(seed)
    _w = jnp.asarray

    def _rec_inputs():
        import jax
        import jax.numpy as jnp
        _rk = jax.random.key(seed)
        x = -0.0003929 + 0.9999 * jax.random.normal(jax.random.fold_in(_rk, 1), (8, 64, 512), jnp.float32)
        _lenS = 64 - jax.random.randint(jax.random.fold_in(_rk, 7), (8,), 0, max(1, 64 // 4) + 1, jnp.int32)
        _lenS2 = 1601 - jax.random.randint(jax.random.fold_in(_rk, 8), (8,), 0, max(1, 1601 // 4) + 1, jnp.int32)
        _ctx_2048P = jax.random.normal(jax.random.fold_in(_rk, 11), (8, 16, 1024), jnp.float32)
        _ctx_2048c = jax.random.dirichlet(jax.random.fold_in(_rk, 511), 0.3 * jnp.ones((16,), jnp.float32), (8, 1601))
        _ctx_2048t = jnp.einsum('bsk,bkd->bsd', _ctx_2048c, _ctx_2048P)
        _ctx_2048t = _ctx_2048t * jax.lax.rsqrt(jnp.mean(jnp.square(_ctx_2048t)) + 1e-12) * 0.953939
        ctx_2048 = 4.13588e-05 + 0.999923 * (_ctx_2048t + 0.3 * jax.random.normal(jax.random.fold_in(_rk, 611), (8, 1601, 1024), jnp.float32))
        _validS = jnp.arange(64)[None, :] < _lenS[:, None]
        _validS2 = jnp.arange(1601)[None, :] < _lenS2[:, None]
        _causal = jnp.tril(jnp.ones((64, 64), dtype=bool))
        mask_BxS2_if0 = jnp.where(jnp.ones((8, 1601), dtype=bool), 4, 0).astype(jnp.int32)
        return (x, ctx_2048, mask_BxS2_if0)
    x, ctx_2048, mask_BxS2_if0 = _rec_inputs()

    def _L0_xattn_setup():
        import jax, jax.numpy as jnp
        import numpy as np
        B, L, P = (4, 2048, 512)
        D_MODEL = 512
        D_GLOBAL = 1024
        HEADDIM = 32
        EPSILON = 0.001
        RMS_EPS = 1e-05

        def rmsnorm(x, g, eps=RMS_EPS):
            var = jnp.mean(jnp.square(x), axis=-1, keepdims=True)
            return x * jax.lax.rsqrt(var + eps) * g

        def _hnet_depool(h, h_patch_full, patch_lens):
            h_patch = h_patch_full[..., :D_MODEL]
            bsz, plen = (h_patch.shape[0], h_patch.shape[1])
            seqlen = h.shape[1]
            logp = jnp.full((bsz, plen), -EPSILON, dtype=jnp.float32)
            bidx = jnp.cumsum(patch_lens, axis=1) - 1
            boundary_mask = jnp.zeros((bsz, seqlen), dtype=jnp.int32)
            boundary_mask = boundary_mask.at[jnp.arange(bsz)[:, None], bidx].set(1)
            dt = (-jnp.log(-jnp.expm1(logp))).astype(h_patch.dtype)
            x = h_patch / dt[..., None]
            n_heads = D_MODEL // HEADDIM
            A = -jnp.ones((n_heads,), dtype=jnp.float32)
            bcoef = jnp.exp(logp).astype(h_patch.dtype)
            x4 = x.reshape(bsz, plen, n_heads, HEADDIM)
            a = jnp.exp(dt[:, :, None] * A[None, None, :])
            u = (dt * bcoef)[:, :, None, None] * x4
            a_b = jnp.broadcast_to(a[..., None], u.shape)

            def comb(lft, rgt):
                aL, uL = lft
                aR, uR = rgt
                return (aL * aR, uL * aR + uR)
            _, s = jax.lax.associative_scan(comb, (a_b, u), axis=1)
            depool = s.reshape(bsz, plen, D_MODEL)
            plug = jnp.clip(jnp.cumsum(boundary_mask, axis=1) - 1, 0, plen - 1)
            depool_out = depool[jnp.arange(bsz)[:, None], plug]
            return depool_out + h
        key = jax.random.key(seed)
        k1, k2, k3, k4 = jax.random.split(key, 4)
        embeds = jax.random.normal(k1, (B, L, D_MODEL), dtype=jnp.float32)
        patch_embeds = jax.random.normal(k2, (B, P, D_GLOBAL), dtype=jnp.float32)
        patch_lens = jnp.full((B, P), L // P, dtype=jnp.int64)
        W_in = jax.random.normal(k3, (D_MODEL, D_MODEL), dtype=jnp.float32) * 0.02
        b_in = jnp.zeros((D_MODEL,), dtype=jnp.float32)
        g_res = jnp.ones((D_MODEL,), dtype=jnp.float32)
        g_init = jnp.ones((D_GLOBAL,), dtype=jnp.float32)
        return {'embeds': embeds, 'patch_embeds': patch_embeds, 'patch_lens': patch_lens, 'W_in': W_in, 'b_in': b_in, 'g_res': g_res, 'g_init': g_init}
    _L0_xattn_all = _L0_xattn_setup()
    _L0_xattn_in = {k: v for k, v in _L0_xattn_all.items() if k in ('W_in', 'b_in', 'g_res', 'g_init')}
    del _L0_xattn_all

    def _L0_attn_setup():
        import jax, jax.numpy as jnp
        import numpy as np
        import math
        D_MODEL = 512
        D_STATE = 16
        D_CONV = 4
        D_INNER = 2 * D_MODEL
        DT_RANK = math.ceil(D_MODEL / 16)
        B_SZ, SEQ = (2, 1024)

        def _mamba_forward(x, in_proj_w, conv_w, conv_b, x_proj_w, dt_proj_w, dt_proj_b, A_log, D, out_proj_w):
            B, L, _ = x.shape
            xz = x @ in_proj_w.T
            xp, z = jnp.split(xz, 2, axis=-1)
            xc = jax.lax.conv_general_dilated(xp.transpose(0, 2, 1), conv_w, window_strides=(1,), padding=[(D_CONV - 1, 0)], feature_group_count=D_INNER, dimension_numbers=('NCH', 'OIH', 'NCH'))
            xc = (xc + conv_b[None, :, None]).transpose(0, 2, 1)
            xa = jax.nn.silu(xc)
            dbc = xa @ x_proj_w.T
            dl = dbc[..., :DT_RANK]
            Bm = dbc[..., DT_RANK:DT_RANK + D_STATE]
            Cm = dbc[..., DT_RANK + D_STATE:]
            delta = jax.nn.softplus(dl @ dt_proj_w.T + dt_proj_b)
            A = -jnp.exp(A_log)
            dA = jnp.exp(delta[..., None] * A)
            dBu = (delta * xa)[..., None] * Bm[:, :, None, :]

            def step(h, t):
                dA_t, dBu_t, C_t = t
                h = dA_t * h + dBu_t
                y = jnp.einsum('ben,bn->be', h, C_t)
                return (h, y)
            h0 = jnp.zeros((B, D_INNER, D_STATE), x.dtype)
            _, ys = jax.lax.scan(step, h0, (dA.transpose(1, 0, 2, 3), dBu.transpose(1, 0, 2, 3), Cm.transpose(1, 0, 2)))
            y = ys.transpose(1, 0, 2) + D * xa
            y = y * jax.nn.silu(z)
            return y @ out_proj_w.T
        key = jax.random.key(seed)
        ks = jax.random.split(key, 10)
        dt_init_std = DT_RANK ** (-0.5)
        dt = jnp.exp(jax.random.uniform(ks[0], (D_INNER,)) * (math.log(0.1) - math.log(0.001)) + math.log(0.001))
        dt = jnp.clip(dt, 0.0001, None)
        inv_dt = dt + jnp.log(-jnp.expm1(-dt))
        A = jnp.tile(jnp.arange(1, D_STATE + 1, dtype=jnp.float32), (D_INNER, 1))
        return {'x': jax.random.normal(ks[1], (B_SZ, SEQ, D_MODEL), jnp.float32), 'in_proj_w': jax.random.normal(ks[2], (2 * D_INNER, D_MODEL), jnp.float32) * D_MODEL ** (-0.5), 'conv_w': jax.random.normal(ks[3], (D_INNER, 1, D_CONV), jnp.float32) * D_CONV ** (-0.5), 'conv_b': jnp.zeros((D_INNER,), jnp.float32), 'x_proj_w': jax.random.normal(ks[4], (DT_RANK + 2 * D_STATE, D_INNER), jnp.float32) * D_INNER ** (-0.5), 'dt_proj_w': jax.random.uniform(ks[5], (D_INNER, DT_RANK), jnp.float32, -dt_init_std, dt_init_std), 'dt_proj_b': inv_dt, 'A_log': jnp.log(A), 'D': jnp.ones((D_INNER,), jnp.float32), 'out_proj_w': jax.random.normal(ks[6], (D_MODEL, D_INNER), jnp.float32) * D_INNER ** (-0.5)}
    _L0_attn_all = _L0_attn_setup()
    _L0_attn_in = {k: v for k, v in _L0_attn_all.items() if k in ('in_proj_w', 'conv_w', 'conv_b', 'x_proj_w', 'dt_proj_w', 'dt_proj_b', 'A_log', 'D', 'out_proj_w')}
    del _L0_attn_all

    def _L0_ffn_setup():
        import jax, jax.numpy as jnp
        import numpy as np
        QB = 127.0
        EPS = 1e-05

        def _ste(x, q):
            return x + jax.lax.stop_gradient(q - x)

        def bitlinear(x, W, b):
            w_scale = jnp.clip(jnp.mean(jnp.abs(W)), EPS, None)
            Wq = _ste(W, jnp.clip(jnp.round(W / w_scale), -1.0, 1.0) * w_scale)
            x_scale = jnp.clip(jnp.max(jnp.abs(x), axis=-1, keepdims=True), EPS, None)
            xq = _ste(x, jnp.clip(jnp.round(x * (QB / x_scale)), -QB - 1.0, QB) * (x_scale / QB))
            return jnp.einsum('bnd,hd->bnh', xq, Wq) + b
        key = jax.random.key(seed)
        k0, k1, k2 = jax.random.split(key, 3)
        B, N, D = (8, 2048, 512)
        H = int(D * 4.0)
        x = jax.random.normal(k0, (B, N, D), dtype=jnp.float32)
        W1 = jax.random.normal(k1, (H, D), dtype=jnp.float32) * 0.02
        b1 = jnp.zeros((H,), dtype=jnp.float32)
        W2 = jax.random.normal(k2, (D, H), dtype=jnp.float32) * 0.02
        b2 = jnp.zeros((D,), dtype=jnp.float32)
        return {'x': x, 'W1': W1, 'b1': b1, 'W2': W2, 'b2': b2}
    _L0_ffn_all = _L0_ffn_setup()
    _L0_ffn_in = {k: v for k, v in _L0_ffn_all.items() if k in ('W1', 'b1', 'W2', 'b2')}
    del _L0_ffn_all

    def _L1_xattn_setup():
        import jax, jax.numpy as jnp
        import numpy as np
        B, N, DIM = (8, 2048, 512)
        M, CTX = (128, 1024)
        HEADS, DH = (16, 64)
        INNER = HEADS * DH
        EPS = 1e-06

        def _split_heads(t):
            b, n, _ = t.shape
            return t.reshape(b, n, HEADS, DH).transpose(0, 2, 1, 3)
        key = jax.random.key(seed)
        ks = jax.random.split(key, 6)
        x = jax.random.normal(ks[0], (B, N, DIM), dtype=jnp.float32)
        context = jax.random.normal(ks[1], (B, M, CTX), dtype=jnp.float32)
        Wq = jax.random.normal(ks[2], (DIM, INNER), dtype=jnp.float32) / np.sqrt(DIM)
        Wkv = jax.random.normal(ks[3], (CTX, 2 * INNER), dtype=jnp.float32) / np.sqrt(CTX)
        null_kv = jax.random.normal(ks[4], (2, DH), dtype=jnp.float32) / np.sqrt(2.0)
        Wout = jax.random.normal(ks[5], (INNER, DIM), dtype=jnp.float32) / np.sqrt(INNER)
        ln_scale = jnp.ones((DIM,), dtype=jnp.float32)
        ln_bias = jnp.zeros((DIM,), dtype=jnp.float32)
        return {'x': x, 'context': context, 'Wq': Wq, 'Wkv': Wkv, 'null_kv': null_kv, 'Wout': Wout, 'ln_scale': ln_scale, 'ln_bias': ln_bias}
    _L1_xattn_all = _L1_xattn_setup()
    _L1_xattn_in = {k: v for k, v in _L1_xattn_all.items() if k in ('Wq', 'Wkv', 'null_kv', 'Wout', 'ln_scale', 'ln_bias')}
    del _L1_xattn_all

    def _L1_attn_setup():
        import jax, jax.numpy as jnp
        import numpy as np
        EMBED_DIM = 512
        NUM_HEADS = 8
        HEAD_DIM = EMBED_DIM // NUM_HEADS
        NUM_QUBITS = 8
        CIRCUITS = 4
        DEPTH = 3
        WAVELENGTHS = 16
        SCALING = HEAD_DIM ** (-0.5)
        ERR_MIN = 1e-06
        TWO_PI = 2.0 * np.pi

        def _quantum_encode(x, photonic_phases):
            hd = x.shape[-1]
            norm = jnp.sqrt(jnp.sum(x * x, axis=-1, keepdims=True))
            normed = x / jnp.maximum(norm, 1e-12)
            ch = jnp.arange(hd)
            phases = photonic_phases[ch % WAVELENGTHS, ch]
            return normed * jnp.exp(1j * phases)

        def _entangle(state, gates):
            for depth in range(DEPTH):
                g = gates[depth, :NUM_HEADS - 1]
                theta = g[:, 0][None, None, :, None]
                phi = g[:, 1][None, None, :, None]
                s1 = state[:, :, :-1]
                s2 = state[:, :, 1:]
                cos_t = jnp.cos(theta / 2)
                sin_t = jnp.sin(theta / 2)
                ctrl = jnp.abs(s1) ** 2
                rot = cos_t * s2 + sin_t * jnp.exp(1j * phi) * jnp.conj(s2)
                new = ctrl * rot + (1.0 - ctrl) * s2
                state = jnp.concatenate([new, state[:, :, -1:]], axis=2)
            return state

        def _forward(query, W_qkv, b_qkv, W_out, b_out, quantum_weights, photonic_phases, entanglement_gates, superposition_logits):
            B, S, E = query.shape
            qkv = query @ W_qkv.T + b_qkv
            q, k, v = jnp.split(qkv, 3, axis=-1)
            q = q.reshape(B, S, NUM_HEADS, HEAD_DIM)
            k = k.reshape(B, S, NUM_HEADS, HEAD_DIM)
            v = v.reshape(B, S, NUM_HEADS, HEAD_DIM)
            qq = _quantum_encode(q, photonic_phases)
            kq = _quantum_encode(k, photonic_phases)
            vq = _quantum_encode(v, photonic_phases)
            q_ent = _entangle(qq, entanglement_gates)
            k_ent = _entangle(kq, entanglement_gates)
            coh = jnp.exp(1j * jnp.angle(jnp.sum(vq, axis=2, keepdims=True)))
            sup_w = jax.nn.softmax(superposition_logits)
            final = None
            for c in range(CIRCUITS):
                ratio = 0.5 + 0.3 * jnp.sin(quantum_weights[c, 0, 0])
                qa = jnp.sqrt(ratio) * q_ent
                ka = jnp.sqrt(1.0 - ratio) * k_ent
                pattern = jnp.einsum('bsid,bsjd->bsij', jnp.conj(qa), ka)
                mod = pattern * jnp.exp(1j * quantum_weights[c, 1, :])
                scores = jnp.abs(mod) ** 2 * SCALING
                probs = jax.nn.softmax(scores, axis=-1)
                amps = jnp.sqrt(probs + 1e-12)
                coh_phase = jnp.angle(jnp.sum(scores, axis=-1, keepdims=True))
                w = amps * jnp.cos(coh_phase)
                weighted = jnp.einsum('bsij,bsjd->bsid', w.astype(jnp.complex64), vq)
                co = weighted * coh
                amp = jnp.clip(jnp.abs(co), ERR_MIN, 1.0)
                ph = jnp.mod(jnp.angle(co), TWO_PI)
                corrected = amp * jnp.exp(1j * ph)
                contrib = sup_w[c] * corrected
                final = contrib if final is None else final + contrib
            measured = jnp.real(final).reshape(B, S, E)
            return measured @ W_out.T + b_out
        key = jax.random.key(seed)
        ks = jax.random.split(key, 8)
        B, S, E = (2, 1024, EMBED_DIM)
        return {'query': jax.random.normal(ks[0], (B, S, E), jnp.float32), 'W_qkv': jax.random.normal(ks[1], (3 * E, E), jnp.float32) / np.sqrt(E).astype(np.float32), 'b_qkv': jnp.zeros((3 * E,), jnp.float32), 'W_out': jax.random.normal(ks[2], (E, E), jnp.float32) / np.sqrt(E).astype(np.float32), 'b_out': jnp.zeros((E,), jnp.float32), 'quantum_weights': jax.random.normal(ks[3], (CIRCUITS, NUM_QUBITS, NUM_QUBITS), jnp.float32) * 0.1, 'photonic_phases': jax.random.normal(ks[4], (WAVELENGTHS, E), jnp.float32) * np.float32(np.pi), 'entanglement_gates': jax.random.normal(ks[5], (DEPTH, NUM_HEADS, 4), jnp.float32) * 0.1, 'superposition_logits': jax.random.normal(ks[6], (CIRCUITS,), jnp.float32)}
    _L1_attn_all = _L1_attn_setup()
    _L1_attn_in = {k: v for k, v in _L1_attn_all.items() if k in ('W_qkv', 'b_qkv', 'W_out', 'b_out', 'quantum_weights', 'photonic_phases', 'entanglement_gates', 'superposition_logits')}
    del _L1_attn_all

    def _L1_ffn_setup():
        import math
        import jax, jax.numpy as jnp
        import numpy as np
        D_MODEL = 512
        D_HIDDEN = 1024
        N_EXPERTS = 8
        TOP_K = 2
        CAPACITY_FACTOR = 1.25

        def _moe_forward(x, w_router, w_gate, w_down):
            B, T, D = x.shape
            N = B * T
            xf = x.reshape(N, D)
            logits = xf.astype(jnp.float32) @ w_router.T
            gates = jax.nn.softmax(logits, axis=-1)
            topk_gates, topk_idx = jax.lax.top_k(gates, TOP_K)
            expert_mask = jax.nn.one_hot(topk_idx, N_EXPERTS, dtype=jnp.int32).sum(axis=1)
            capacity = math.ceil(N / N_EXPERTS * CAPACITY_FACTOR)
            position_in_expert = jnp.cumsum(expert_mask, axis=0) - 1
            expert_mask = expert_mask * (position_in_expert < capacity)
            keep = jnp.take_along_axis(expert_mask, topk_idx, axis=1) > 0
            topk_gates = topk_gates * keep
            topk_gates = topk_gates / (topk_gates.sum(axis=-1, keepdims=True) + 1e-06)
            hidden = jax.nn.silu(xf @ w_gate.T)
            combine = (topk_gates[:, :, None] * jax.nn.one_hot(topk_idx, N_EXPERTS, dtype=topk_gates.dtype)).sum(axis=1)
            y = jnp.zeros((N, D), dtype=x.dtype)
            for e in range(N_EXPERTS):
                y = y + combine[:, e:e + 1] * (hidden @ w_down[e].T)
            return y.reshape(B, T, D)
        key = jax.random.key(seed)
        k0, k1, k2, k3 = jax.random.split(key, 4)
        B, T = (2, 1024)
        x = jax.random.normal(k0, (B, T, D_MODEL), dtype=jnp.float32)
        w_router = jax.random.normal(k1, (N_EXPERTS, D_MODEL), dtype=jnp.float32) * 0.02
        w_gate = jax.random.normal(k2, (D_HIDDEN, D_MODEL), dtype=jnp.float32) * 0.02
        w_down = jax.random.normal(k3, (N_EXPERTS, D_MODEL, D_HIDDEN), dtype=jnp.float32) * 0.02
        return {'x': x, 'w_router': w_router, 'w_gate': w_gate, 'w_down': w_down}
    _L1_ffn_all = _L1_ffn_setup()
    _L1_ffn_in = {k: v for k, v in _L1_ffn_all.items() if k in ('w_router', 'w_gate', 'w_down')}
    del _L1_ffn_all
    return {'x': x, 'ctx_2048': ctx_2048, 'mask_BxS2_if0': mask_BxS2_if0, 'L0_xattn_W_in': _L0_xattn_in['W_in'], 'L0_xattn_b_in': _L0_xattn_in['b_in'], 'L0_xattn_g_res': _L0_xattn_in['g_res'], 'L0_xattn_g_init': _L0_xattn_in['g_init'], 'L0_attn_in_proj_w': _L0_attn_in['in_proj_w'], 'L0_attn_conv_w': _L0_attn_in['conv_w'], 'L0_attn_conv_b': _L0_attn_in['conv_b'], 'L0_attn_x_proj_w': _L0_attn_in['x_proj_w'], 'L0_attn_dt_proj_w': _L0_attn_in['dt_proj_w'], 'L0_attn_dt_proj_b': _L0_attn_in['dt_proj_b'], 'L0_attn_A_log': _L0_attn_in['A_log'], 'L0_attn_D': _L0_attn_in['D'], 'L0_attn_out_proj_w': _L0_attn_in['out_proj_w'], 'L0_ffn_W1': _L0_ffn_in['W1'], 'L0_ffn_b1': _L0_ffn_in['b1'], 'L0_ffn_W2': _L0_ffn_in['W2'], 'L0_ffn_b2': _L0_ffn_in['b2'], 'L1_xattn_Wq': _L1_xattn_in['Wq'], 'L1_xattn_Wkv': _L1_xattn_in['Wkv'], 'L1_xattn_null_kv': _L1_xattn_in['null_kv'], 'L1_xattn_Wout': _L1_xattn_in['Wout'], 'L1_xattn_ln_scale': _L1_xattn_in['ln_scale'], 'L1_xattn_ln_bias': _L1_xattn_in['ln_bias'], 'L1_attn_W_qkv': _L1_attn_in['W_qkv'], 'L1_attn_b_qkv': _L1_attn_in['b_qkv'], 'L1_attn_W_out': _L1_attn_in['W_out'], 'L1_attn_b_out': _L1_attn_in['b_out'], 'L1_attn_quantum_weights': _L1_attn_in['quantum_weights'], 'L1_attn_photonic_phases': _L1_attn_in['photonic_phases'], 'L1_attn_entanglement_gates': _L1_attn_in['entanglement_gates'], 'L1_attn_superposition_logits': _L1_attn_in['superposition_logits'], 'L1_ffn_w_router': _L1_ffn_in['w_router'], 'L1_ffn_w_gate': _L1_ffn_in['w_gate'], 'L1_ffn_w_down': _L1_ffn_in['w_down']}

def reference(x, ctx_2048, mask_BxS2_if0, L0_xattn_W_in, L0_xattn_b_in, L0_xattn_g_res, L0_xattn_g_init, L0_attn_in_proj_w, L0_attn_conv_w, L0_attn_conv_b, L0_attn_x_proj_w, L0_attn_dt_proj_w, L0_attn_dt_proj_b, L0_attn_A_log, L0_attn_D, L0_attn_out_proj_w, L0_ffn_W1, L0_ffn_b1, L0_ffn_W2, L0_ffn_b2, L1_xattn_Wq, L1_xattn_Wkv, L1_xattn_null_kv, L1_xattn_Wout, L1_xattn_ln_scale, L1_xattn_ln_bias, L1_attn_W_qkv, L1_attn_b_qkv, L1_attn_W_out, L1_attn_b_out, L1_attn_quantum_weights, L1_attn_photonic_phases, L1_attn_entanglement_gates, L1_attn_superposition_logits, L1_ffn_w_router, L1_ffn_w_gate, L1_ffn_w_down):
    import jax
    import jax.numpy as jnp

    def _L0_xattn_ref(embeds, patch_embeds, patch_lens, W_in, b_in, g_res, g_init):
        import jax, jax.numpy as jnp
        import numpy as np
        B, L, P = (4, 2048, 512)
        D_MODEL = 512
        D_GLOBAL = 1024
        HEADDIM = 32
        EPSILON = 0.001
        RMS_EPS = 1e-05

        def rmsnorm(x, g, eps=RMS_EPS):
            var = jnp.mean(jnp.square(x), axis=-1, keepdims=True)
            return x * jax.lax.rsqrt(var + eps) * g

        def _hnet_depool(h, h_patch_full, patch_lens):
            h_patch = h_patch_full[..., :D_MODEL]
            bsz, plen = (h_patch.shape[0], h_patch.shape[1])
            seqlen = h.shape[1]
            logp = jnp.full((bsz, plen), -EPSILON, dtype=jnp.float32)
            bidx = jnp.cumsum(patch_lens, axis=1) - 1
            boundary_mask = jnp.zeros((bsz, seqlen), dtype=jnp.int32)
            boundary_mask = boundary_mask.at[jnp.arange(bsz)[:, None], bidx].set(1)
            dt = (-jnp.log(-jnp.expm1(logp))).astype(h_patch.dtype)
            x = h_patch / dt[..., None]
            n_heads = D_MODEL // HEADDIM
            A = -jnp.ones((n_heads,), dtype=jnp.float32)
            bcoef = jnp.exp(logp).astype(h_patch.dtype)
            x4 = x.reshape(bsz, plen, n_heads, HEADDIM)
            a = jnp.exp(dt[:, :, None] * A[None, None, :])
            u = (dt * bcoef)[:, :, None, None] * x4
            a_b = jnp.broadcast_to(a[..., None], u.shape)

            def comb(lft, rgt):
                aL, uL = lft
                aR, uR = rgt
                return (aL * aR, uL * aR + uR)
            _, s = jax.lax.associative_scan(comb, (a_b, u), axis=1)
            depool = s.reshape(bsz, plen, D_MODEL)
            plug = jnp.clip(jnp.cumsum(boundary_mask, axis=1) - 1, 0, plen - 1)
            depool_out = depool[jnp.arange(bsz)[:, None], plug]
            return depool_out + h
        h = rmsnorm(embeds, g_res)
        h = jnp.einsum('bld,ed->ble', h, W_in) + b_in
        h_patch = rmsnorm(patch_embeds, g_init)
        return _hnet_depool(h, h_patch, patch_lens)

    def _L0_attn_ref(x, in_proj_w, conv_w, conv_b, x_proj_w, dt_proj_w, dt_proj_b, A_log, D, out_proj_w):
        import jax, jax.numpy as jnp
        import numpy as np
        import math
        D_MODEL = 512
        D_STATE = 16
        D_CONV = 4
        D_INNER = 2 * D_MODEL
        DT_RANK = math.ceil(D_MODEL / 16)
        B_SZ, SEQ = (2, 1024)

        def _mamba_forward(x, in_proj_w, conv_w, conv_b, x_proj_w, dt_proj_w, dt_proj_b, A_log, D, out_proj_w):
            B, L, _ = x.shape
            xz = x @ in_proj_w.T
            xp, z = jnp.split(xz, 2, axis=-1)
            xc = jax.lax.conv_general_dilated(xp.transpose(0, 2, 1), conv_w, window_strides=(1,), padding=[(D_CONV - 1, 0)], feature_group_count=D_INNER, dimension_numbers=('NCH', 'OIH', 'NCH'))
            xc = (xc + conv_b[None, :, None]).transpose(0, 2, 1)
            xa = jax.nn.silu(xc)
            dbc = xa @ x_proj_w.T
            dl = dbc[..., :DT_RANK]
            Bm = dbc[..., DT_RANK:DT_RANK + D_STATE]
            Cm = dbc[..., DT_RANK + D_STATE:]
            delta = jax.nn.softplus(dl @ dt_proj_w.T + dt_proj_b)
            A = -jnp.exp(A_log)
            dA = jnp.exp(delta[..., None] * A)
            dBu = (delta * xa)[..., None] * Bm[:, :, None, :]

            def step(h, t):
                dA_t, dBu_t, C_t = t
                h = dA_t * h + dBu_t
                y = jnp.einsum('ben,bn->be', h, C_t)
                return (h, y)
            h0 = jnp.zeros((B, D_INNER, D_STATE), x.dtype)
            _, ys = jax.lax.scan(step, h0, (dA.transpose(1, 0, 2, 3), dBu.transpose(1, 0, 2, 3), Cm.transpose(1, 0, 2)))
            y = ys.transpose(1, 0, 2) + D * xa
            y = y * jax.nn.silu(z)
            return y @ out_proj_w.T
        return _mamba_forward(x, in_proj_w, conv_w, conv_b, x_proj_w, dt_proj_w, dt_proj_b, A_log, D, out_proj_w)

    def _L0_ffn_ref(x, W1, b1, W2, b2):
        import jax, jax.numpy as jnp
        import numpy as np
        QB = 127.0
        EPS = 1e-05

        def _ste(x, q):
            return x + jax.lax.stop_gradient(q - x)

        def bitlinear(x, W, b):
            w_scale = jnp.clip(jnp.mean(jnp.abs(W)), EPS, None)
            Wq = _ste(W, jnp.clip(jnp.round(W / w_scale), -1.0, 1.0) * w_scale)
            x_scale = jnp.clip(jnp.max(jnp.abs(x), axis=-1, keepdims=True), EPS, None)
            xq = _ste(x, jnp.clip(jnp.round(x * (QB / x_scale)), -QB - 1.0, QB) * (x_scale / QB))
            return jnp.einsum('bnd,hd->bnh', xq, Wq) + b
        h = bitlinear(x, W1, b1)
        h = jax.nn.gelu(h, approximate=False)
        return bitlinear(h, W2, b2)

    def _L1_xattn_ref(x, context, Wq, Wkv, null_kv, Wout, ln_scale, ln_bias):
        import jax, jax.numpy as jnp
        import numpy as np
        B, N, DIM = (8, 2048, 512)
        M, CTX = (128, 1024)
        HEADS, DH = (16, 64)
        INNER = HEADS * DH
        EPS = 1e-06

        def _split_heads(t):
            b, n, _ = t.shape
            return t.reshape(b, n, HEADS, DH).transpose(0, 2, 1, 3)
        scale = DH ** (-0.5)
        b = x.shape[0]
        q = _split_heads(jnp.einsum('bnd,df->bnf', x, Wq))
        kv = jnp.einsum('bmc,cf->bmf', context, Wkv)
        k, v = jnp.split(kv, 2, axis=-1)
        k, v = (_split_heads(k), _split_heads(v))
        nk = jnp.broadcast_to(null_kv[0], (b, HEADS, 1, DH))
        nv = jnp.broadcast_to(null_kv[1], (b, HEADS, 1, DH))
        k = jnp.concatenate((nk, k), axis=-2)
        v = jnp.concatenate((nv, v), axis=-2)
        q = q * scale
        sim = jnp.einsum('bhid,bhjd->bhij', q, k)
        attn = jax.nn.softmax(sim, axis=-1)
        out = jnp.einsum('bhij,bhjd->bhid', attn, v)
        out = out.transpose(0, 2, 1, 3).reshape(b, -1, INNER)
        out = jnp.einsum('bnf,fd->bnd', out, Wout)
        mu = jnp.mean(out, axis=-1, keepdims=True)
        var = jnp.var(out, axis=-1, keepdims=True)
        out = (out - mu) * jax.lax.rsqrt(var + EPS) * ln_scale + ln_bias
        return out

    def _L1_attn_ref(query, W_qkv, b_qkv, W_out, b_out, quantum_weights, photonic_phases, entanglement_gates, superposition_logits):
        import jax, jax.numpy as jnp
        import numpy as np
        EMBED_DIM = 512
        NUM_HEADS = 8
        HEAD_DIM = EMBED_DIM // NUM_HEADS
        NUM_QUBITS = 8
        CIRCUITS = 4
        DEPTH = 3
        WAVELENGTHS = 16
        SCALING = HEAD_DIM ** (-0.5)
        ERR_MIN = 1e-06
        TWO_PI = 2.0 * np.pi

        def _quantum_encode(x, photonic_phases):
            hd = x.shape[-1]
            norm = jnp.sqrt(jnp.sum(x * x, axis=-1, keepdims=True))
            normed = x / jnp.maximum(norm, 1e-12)
            ch = jnp.arange(hd)
            phases = photonic_phases[ch % WAVELENGTHS, ch]
            return normed * jnp.exp(1j * phases)

        def _entangle(state, gates):
            for depth in range(DEPTH):
                g = gates[depth, :NUM_HEADS - 1]
                theta = g[:, 0][None, None, :, None]
                phi = g[:, 1][None, None, :, None]
                s1 = state[:, :, :-1]
                s2 = state[:, :, 1:]
                cos_t = jnp.cos(theta / 2)
                sin_t = jnp.sin(theta / 2)
                ctrl = jnp.abs(s1) ** 2
                rot = cos_t * s2 + sin_t * jnp.exp(1j * phi) * jnp.conj(s2)
                new = ctrl * rot + (1.0 - ctrl) * s2
                state = jnp.concatenate([new, state[:, :, -1:]], axis=2)
            return state

        def _forward(query, W_qkv, b_qkv, W_out, b_out, quantum_weights, photonic_phases, entanglement_gates, superposition_logits):
            B, S, E = query.shape
            qkv = query @ W_qkv.T + b_qkv
            q, k, v = jnp.split(qkv, 3, axis=-1)
            q = q.reshape(B, S, NUM_HEADS, HEAD_DIM)
            k = k.reshape(B, S, NUM_HEADS, HEAD_DIM)
            v = v.reshape(B, S, NUM_HEADS, HEAD_DIM)
            qq = _quantum_encode(q, photonic_phases)
            kq = _quantum_encode(k, photonic_phases)
            vq = _quantum_encode(v, photonic_phases)
            q_ent = _entangle(qq, entanglement_gates)
            k_ent = _entangle(kq, entanglement_gates)
            coh = jnp.exp(1j * jnp.angle(jnp.sum(vq, axis=2, keepdims=True)))
            sup_w = jax.nn.softmax(superposition_logits)
            final = None
            for c in range(CIRCUITS):
                ratio = 0.5 + 0.3 * jnp.sin(quantum_weights[c, 0, 0])
                qa = jnp.sqrt(ratio) * q_ent
                ka = jnp.sqrt(1.0 - ratio) * k_ent
                pattern = jnp.einsum('bsid,bsjd->bsij', jnp.conj(qa), ka)
                mod = pattern * jnp.exp(1j * quantum_weights[c, 1, :])
                scores = jnp.abs(mod) ** 2 * SCALING
                probs = jax.nn.softmax(scores, axis=-1)
                amps = jnp.sqrt(probs + 1e-12)
                coh_phase = jnp.angle(jnp.sum(scores, axis=-1, keepdims=True))
                w = amps * jnp.cos(coh_phase)
                weighted = jnp.einsum('bsij,bsjd->bsid', w.astype(jnp.complex64), vq)
                co = weighted * coh
                amp = jnp.clip(jnp.abs(co), ERR_MIN, 1.0)
                ph = jnp.mod(jnp.angle(co), TWO_PI)
                corrected = amp * jnp.exp(1j * ph)
                contrib = sup_w[c] * corrected
                final = contrib if final is None else final + contrib
            measured = jnp.real(final).reshape(B, S, E)
            return measured @ W_out.T + b_out
        return _forward(query, W_qkv, b_qkv, W_out, b_out, quantum_weights, photonic_phases, entanglement_gates, superposition_logits)

    def _L1_ffn_ref(x, w_router, w_gate, w_down):
        import math
        import jax, jax.numpy as jnp
        import numpy as np
        D_MODEL = 512
        D_HIDDEN = 1024
        N_EXPERTS = 8
        TOP_K = 2
        CAPACITY_FACTOR = 1.25

        def _moe_forward(x, w_router, w_gate, w_down):
            B, T, D = x.shape
            N = B * T
            xf = x.reshape(N, D)
            logits = xf.astype(jnp.float32) @ w_router.T
            gates = jax.nn.softmax(logits, axis=-1)
            topk_gates, topk_idx = jax.lax.top_k(gates, TOP_K)
            expert_mask = jax.nn.one_hot(topk_idx, N_EXPERTS, dtype=jnp.int32).sum(axis=1)
            capacity = math.ceil(N / N_EXPERTS * CAPACITY_FACTOR)
            position_in_expert = jnp.cumsum(expert_mask, axis=0) - 1
            expert_mask = expert_mask * (position_in_expert < capacity)
            keep = jnp.take_along_axis(expert_mask, topk_idx, axis=1) > 0
            topk_gates = topk_gates * keep
            topk_gates = topk_gates / (topk_gates.sum(axis=-1, keepdims=True) + 1e-06)
            hidden = jax.nn.silu(xf @ w_gate.T)
            combine = (topk_gates[:, :, None] * jax.nn.one_hot(topk_idx, N_EXPERTS, dtype=topk_gates.dtype)).sum(axis=1)
            y = jnp.zeros((N, D), dtype=x.dtype)
            for e in range(N_EXPERTS):
                y = y + combine[:, e:e + 1] * (hidden @ w_down[e].T)
            return y.reshape(B, T, D)
        return _moe_forward(x, w_router, w_gate, w_down)
    x = x + _L0_xattn_ref(_layernorm(x, axis=-1), ctx_2048, mask_BxS2_if0, L0_xattn_W_in, L0_xattn_b_in, L0_xattn_g_res, L0_xattn_g_init)
    x = x + _L0_attn_ref(_layernorm(x, axis=-1), L0_attn_in_proj_w, L0_attn_conv_w, L0_attn_conv_b, L0_attn_x_proj_w, L0_attn_dt_proj_w, L0_attn_dt_proj_b, L0_attn_A_log, L0_attn_D, L0_attn_out_proj_w)
    x = x + _L0_ffn_ref(_layernorm(x, axis=-1), L0_ffn_W1, L0_ffn_b1, L0_ffn_W2, L0_ffn_b2)
    x = x + _L1_xattn_ref(_layernorm(x, axis=-1), ctx_2048, L1_xattn_Wq, L1_xattn_Wkv, L1_xattn_null_kv, L1_xattn_Wout, L1_xattn_ln_scale, L1_xattn_ln_bias)
    x = x + _L1_attn_ref(_layernorm(x, axis=-1), L1_attn_W_qkv, L1_attn_b_qkv, L1_attn_W_out, L1_attn_b_out, L1_attn_quantum_weights, L1_attn_photonic_phases, L1_attn_entanglement_gates, L1_attn_superposition_logits)
    x = x + _L1_ffn_ref(_layernorm(x, axis=-1), L1_ffn_w_router, L1_ffn_w_gate, L1_ffn_w_down)
    return x

_drawn_inputs = setup_inputs


def setup_inputs(seed=0):
    import zlib

    import numpy as np

    out = dict(_drawn_inputs(seed))
    spreads = {'L0_xattn_b_in': (0.0, 0.1),
     'L0_xattn_g_res': (1.0, 0.2),
     'L0_xattn_g_init': (1.0, 0.2),
     'L0_attn_conv_b': (0.0, 0.312),
     'L0_attn_D': (1.0, 0.2),
     'L0_ffn_b1': (0.0, 0.382),
     'L0_ffn_b2': (0.0, 0.1),
     'L1_xattn_ln_scale': (1.0, 0.2),
     'L1_xattn_ln_bias': (0.0, 0.1),
     'L1_attn_b_qkv': (0.0, 0.8),
     'L1_attn_b_out': (0.0, 0.1)}
    factors = {'L0_attn_dt_proj_w': 7.115,
     'L0_attn_dt_proj_b': 4.165,
     'L0_attn_A_log': 4.037,
     'L1_xattn_null_kv': 8.0,
     'L1_attn_quantum_weights': 8.0,
     'L1_attn_entanglement_gates': 8.0,
     'L1_attn_superposition_logits': 8.0}
    for name, (base, spread) in spreads.items():
        noise = np.random.default_rng([zlib.crc32(name.encode()), seed]).standard_normal(out[name].shape)
        drawn = base * np.exp(spread * noise) if base else spread * noise
        out[name] = jnp.asarray(drawn.astype(out[name].dtype))
    for name, factor in factors.items():
        out[name] = (out[name] * factor).astype(out[name].dtype)
    return out
```

```python
import math
from contextlib import ExitStack

import numpy as np

import concourse.bass as bass
from concourse import mybir

f32 = mybir.dt.float32
f16 = mybir.dt.float16
bf16 = mybir.dt.bfloat16
i32 = mybir.dt.int32
ALU = mybir.AluOpType
ACT = mybir.ActivationFunctionType
AX = mybir.AxisListType

P = 128
B, S, D = 8, 64, 512
TOK = B * S
NT = TOK // P
DC = D // P
CTX, CW = 1601, 1024
ROUND = 1.5 * 2.0**23
BANK = 512


class Chain:

    def __init__(self, eng, sem):
        self.eng, self.sem, self.n = eng, sem, 0

    def mark(self, ins):
        ins.then_inc(self.sem, 1)
        self.n += 1

    def settle(self):
        self.eng.wait_ge(self.sem, self.n)

    def link(self, ins):
        self.mark(ins)
        self.settle()


class Stage:

    def __init__(self, nc, name):
        self.nc, self.name, self.stack, self.held = nc, name, ExitStack(), []

    def __enter__(self):
        self.stack.__enter__()
        return self

    def __exit__(self, *a):
        self.stack.__exit__(*a)
        if self.held:
            self.nc.clear_and_free_semaphores(self.held)
            self.nc.all_engine_barrier()

    def sb(self, name, shape, dt=f32):
        return self.stack.enter_context(self.nc.sbuf_tensor(f"{self.name}_{name}", shape, dt))

    def ps(self, name, banks=1, dt=f32):
        return self.stack.enter_context(self.nc.psum_tensor(f"{self.name}_{name}", [P, banks * BANK], dt))

    def sem(self, name):
        self.held.append(self.nc.alloc_semaphore(name=f"{self.name}_{name}"))
        return self.held[-1]

    def sems(self, names):
        return [self.sem(n) for n in names.split()]

    def block(self):
        return self.stack.enter_context(self.nc.Block())


def norm_transpose(nc, name, x, xn, xt, ident, eps, rms_eps=None, gain=None, transpose=True):
    with Stage(nc, name) as st:
        stats = st.sb("stats", [P, NT, 6])
        mv = st.sb("mv", [P, NT, 2])
        root = st.sb("root", [P, 2 * NT])
        rstd = st.sb("rstd", [P, 2 * NT])
        square = st.sb("square", [P, D])
        ssum = st.sb("ssum", [P, NT])
        pt = st.ps("pt", DC)
        var_ready, root_ready, xn_ready, xt_in_psum, done, chain, normed, ss_ready, sq_chain = st.sems(
            "var_ready root_ready xn_ready xt_in_psum done chain normed ss_ready sq_chain")
        block = st.block()

        @block.vector
        def _(dve):
            c = Chain(dve, chain)
            for t in range(NT):
                c.mark(nc.vector.bn_stats(stats[:, t, :], x[:, t, :]))
            c.settle()
            for t in range(NT):
                c.mark(nc.vector.bn_aggr(mv[:, t, :], stats[:, t, :]))
            c.settle()
            nc.vector.tensor_scalar(root[:, 0:NT], mv[:, :, 1], eps, None, ALU.add).then_inc(var_ready, 1)
            dve.wait_ge(root_ready, 1)
            c.link(nc.vector.reciprocal(rstd[:, 0:NT], root[:, NT:2 * NT]))
            for t in range(NT):
                nc.vector.tensor_scalar(xn[:, t, :], x[:, t, :], mv[:, t, 0:1], rstd[:, t:t + 1],
                                        ALU.subtract, ALU.mult).then_inc(normed if rms_eps else xn_ready, 1)
            if rms_eps:
                dve.wait_ge(ss_ready, 1)
                c.link(nc.vector.reciprocal(rstd[:, NT:2 * NT], root[:, NT:2 * NT]))
                for t in range(NT):
                    nc.vector.tensor_scalar(xn[:, t, :], xn[:, t, :], rstd[:, NT + t:NT + t + 1], None,
                                            ALU.mult).then_inc(xn_ready, 1)
            if not transpose:
                dve.wait_ge(xn_ready, NT)
                return
            dve.wait_ge(xt_in_psum, 1)
            for k in range(0, DC, 2):
                if gain is None:
                    nc.vector.tensor_copy(xt[:, k, :], pt[:, k * BANK:(k + 1) * BANK]).then_inc(done, 1)
                else:
                    nc.vector.tensor_scalar(xt[:, k, :], pt[:, k * BANK:(k + 1) * BANK], gain[:, k:k + 1],
                                            None, ALU.mult).then_inc(done, 1)
            dve.wait_ge(done, DC)

        @block.scalar
        def _(act):
            act.wait_ge(var_ready, 1)
            nc.scalar.activation(root[:, NT:2 * NT], root[:, 0:NT], ACT.Sqrt).then_inc(root_ready, 1)
            if rms_eps:
                for t in range(NT):
                    act.wait_ge(normed, t + 1)
                    if t:
                        act.wait_ge(sq_chain, t)
                    nc.scalar.activation(square[:, :], xn[:, t, :], ACT.Square,
                                         accum_out=ssum[:, t:t + 1]).then_inc(sq_chain, 1)
                act.wait_ge(sq_chain, NT)
                nc.scalar.activation(root[:, 0:NT], ssum[:, :], ACT.Copy, bias=rms_eps, scale=1.0 / D).then_inc(sq_chain, 1)
                act.wait_ge(sq_chain, NT + 1)
                nc.scalar.activation(root[:, NT:2 * NT], root[:, 0:NT], ACT.Sqrt).then_inc(ss_ready, 1)
            if not transpose:
                return
            act.wait_ge(xt_in_psum, 1)
            for k in range(1, DC, 2):
                if gain is None:
                    nc.scalar.activation(xt[:, k, :], pt[:, k * BANK:(k + 1) * BANK], ACT.Copy).then_inc(done, 1)
                else:
                    nc.scalar.activation(xt[:, k, :], pt[:, k * BANK:(k + 1) * BANK], ACT.Copy,
                                         scale=gain[:, k:k + 1]).then_inc(done, 1)

        @block.tensor
        def _(pe):
            if not transpose:
                return
            for t in range(NT):
                pe.wait_ge(xn_ready, t + 1)
                for k in range(DC):
                    last = nc.tensor.transpose(pt[:, k * BANK + t * P:k * BANK + (t + 1) * P],
                                               xn[:, t, k * P:(k + 1) * P], ident[:, :])
            last.then_inc(xt_in_psum, 1)


COLS = dict(g_res=(0, 4), conv_b=(4, 8), d_skip=(12, 8), dt_b=(20, 8), conv_w=(28, 32))


def col(cols, name, i=0, n=None):
    at, k = COLS[name]
    return cols[:, at + i:at + (k if n is None else i + n)]


def depool_stream(nc, io, k, x, xn, xt):
    norm_transpose(nc, "n0", x, xn, xt, k.ident, 1e-5, rms_eps=1e-5, gain=col(k.cols, "g_res"))
    EPS = 0.001
    dt = -math.log(-math.expm1(-EPS))
    decay = math.exp(-dt)
    bcoef = math.exp(-EPS)
    PT = (CTX + P - 1) // P
    with Stage(nc, "dp") as st:
        lens_i = st.sb("lens_i", [P, PT, B], i32)
        lens = st.sb("lens", [P, PT, B])
        ends = st.sb("ends", [P, PT, B])
        wrap = st.sb("wrap", [P, PT, B])
        w_in = st.sb("w_in", [P, DC, D])
        b_row = st.sb("b_row", [1, D])
        ctx = st.sb("ctx", [P, NT, CW])
        g_init = st.sb("g_init", [P, D])
        upto = st.sb("upto", [P, P])
        place = st.sb("place", [P, S])
        hit = st.sb("hit", [P, PT * B, S], bf16)
        ones_h = st.sb("ones_h", [P, P], bf16)
        keep = st.sb("keep", [S, B, S])
        mark = st.sb("mark", [S, TOK])
        plug = st.sb("plug", [S, TOK])
        rowid = st.sb("rowid", [S, 1])
        pick = st.sb("pick", [S, TOK])
        scan = st.sb("scan", [S, 2, S])
        gather = st.sb("gather", [P, NT, P])
        sq = st.sb("sq", [P, CW])
        ss = st.sb("ss", [P, 4 * NT])
        p_ends, p_hits, p_gat = st.ps("p_ends"), st.ps("p_hits"), st.ps("p_gat")
        p_out = st.ps("p_out", NT)
        ld_lens, ld_w, ready, ends_ready, hit_ready, hits_counted, picked, gat_ready, gat_done, \
            u_ready, out_ready, chain, actc, root_ready, pc = st.sems(
                "ld_lens ld_w ready ends_ready hit_ready hits_counted picked gat_ready gat_done "
                "u_ready out_ready chain actc root_ready pc")
        ld_ctx = [st.sem(f"ld_ctx{t}") for t in range(NT)]
        block = st.block()

        @block.sync
        def _(sp):
            sp.dma_start(lens_i[:, :, :], io.lens).then_inc(ld_lens, 16)
            for t in range(NT):
                sp.dma_start(ctx[:, t, :], io.patches[:, t, :]).then_inc(ld_ctx[t], 16)
            sp.dma_start(w_in[:, :, :], io.w_in).then_inc(ld_w, 16)
            sp.dma_start(b_row[:, :], io.b_in).then_inc(ld_w, 16)
            sp.dma_start(g_init[:, :], io.g_init.partition_broadcast(P)).then_inc(ld_w, 16)

        @block.gpsimd
        def _(g):
            c = Chain(g, pc)
            c.mark(g.memset(upto[:, :], 1.0))
            c.mark(g.memset(ones_h[:, :], 1.0))
            c.mark(g.memset(keep[:, :, :], 1.0))
            c.mark(g.memset(scan[:, :, :], 0.0))
            c.mark(g.memset(gather[:, :, :], 0.0))
            c.mark(g.iota(place[:, :], [[1, S]], base=1, channel_multiplier=0,
                          allow_small_or_imprecise_dtypes=True))
            c.mark(g.iota(rowid[:, :], [[0, 1]], base=0, channel_multiplier=1,
                          allow_small_or_imprecise_dtypes=True))
            c.settle()
            c.mark(g.affine_select(out=upto[:, :], in_=upto[:, :], compare_op=ALU.is_ge, fill=0.0,
                                   base=0, pattern=[[1, P]], channel_multiplier=-1))
            c.mark(g.memset(keep[:, :, 0:1], 0.0))
            power = 0
            while decay**power > 1e-38:
                c.link(g.affine_select(out=scan[:, :, :], in_=scan[:, :, :], compare_op=ALU.not_equal,
                                       fill=decay**power, base=-power, pattern=[[0, 2], [-1, S]],
                                       channel_multiplier=1))
                power += 1
            g.sem_inc(ready, 1)

        @block.vector
        def _(dve):
            c = Chain(dve, chain)
            dve.wait_ge(ld_lens, 16)
            nc.vector.tensor_copy(lens[:, :, :], lens_i[:, :, :]).then_inc(hit_ready, 1)
            dve.wait_ge(root_ready, 1)
            c.link(nc.vector.reciprocal(ss[:, 2 * NT:3 * NT], ss[:, NT:2 * NT]))
            c.link(nc.vector.tensor_scalar(ss[:, 3 * NT:4 * NT], ss[:, 2 * NT:3 * NT], bcoef, None, ALU.mult))
            dve.wait_ge(ld_w, 48)
            for t in range(NT):
                nc.vector.scalar_tensor_tensor(ctx[:, t, 0:D], ctx[:, t, 0:D], ss[:, 3 * NT + t:3 * NT + t + 1],
                                               g_init[:, :], ALU.mult, ALU.mult).then_inc(u_ready, 1)
            dve.wait_ge(ends_ready, 1)
            dve.wait_ge(ready, 1)
            e = p_ends[:, 0:PT * B]
            c.link(nc.vector.tensor_scalar(wrap[:, :, :].rearrange("p a b -> p (a b)"), e, 0.0, float(S),
                                           ALU.is_le, ALU.mult))
            c.link(nc.vector.tensor_tensor(ends[:, :, :].rearrange("p a b -> p (a b)"),
                                           wrap[:, :, :].rearrange("p a b -> p (a b)"), e, ALU.add))
            nc.vector.tensor_tensor(
                hit[:, :, :], ends[:, :, :].rearrange("p a b -> p (a b)").unsqueeze(2).to_broadcast([P, PT * B, S]),
                place[:, :].unsqueeze(1).to_broadcast([P, PT * B, S]), ALU.is_equal).then_inc(hit_ready, 1)
            dve.wait_ge(hits_counted, 1)
            c.link(nc.vector.tensor_scalar(mark[:, :], p_hits[0:S, :], 1.0, None, ALU.min))
            c.link(nc.vector.tensor_tensor_scan(plug[:, :], keep[:, :, :].rearrange("p b s -> p (b s)"), mark[:, :],
                                                0.0, ALU.mult, ALU.add))
            c.link(nc.vector.tensor_scalar(plug[:, :], plug[:, :], -1.0, 0.0, ALU.add, ALU.max))
            nc.vector.tensor_scalar(pick[:, :], plug[:, :], rowid[:, 0:1], None, ALU.is_equal).then_inc(picked, 1)
            dve.wait_ge(gat_ready, 1)
            for h in range(2):
                nc.vector.tensor_copy(gather[h * S:(h + 1) * S, :, h * S:(h + 1) * S],
                                      p_gat[h * S:(h + 1) * S, :].rearrange("p (t h s) -> p t h s", h=2, s=S)[:, :, h, :]
                                      ).then_inc(gat_done, 1)
            for t in range(NT):
                dve.wait_ge(out_ready, t + 1)
                c.mark(nc.vector.tensor_tensor(x[:, t, :], x[:, t, :], p_out[:, t * BANK:(t + 1) * BANK], ALU.add))
            c.settle()

        @block.scalar
        def _(act):
            for t in range(NT):
                act.wait_ge(ld_ctx[t], 16)
                if t:
                    act.wait_ge(actc, t)
                nc.scalar.activation(sq[:, :], ctx[:, t, :], ACT.Square,
                                     accum_out=ss[:, t:t + 1]).then_inc(actc, 1)
            act.wait_ge(actc, NT)
            nc.scalar.activation(ss[:, NT:2 * NT], ss[:, 0:NT], ACT.Copy, bias=1e-5, scale=1.0 / CW).then_inc(actc, 1)
            act.wait_ge(actc, NT + 1)
            nc.scalar.activation(ss[:, NT:2 * NT], ss[:, NT:2 * NT], ACT.Sqrt).then_inc(root_ready, 1)

        @block.tensor
        def _(pe):
            pe.wait_ge(hit_ready, 1)
            pe.wait_ge(ready, 1)
            lt = lens[:, :, :]
            nc.tensor.matmul(p_ends[:, 0:PT * B], upto[:, :], lt.rearrange("p a b -> p (a b)"), start=True, stop=False)
            for j in range(PT - 1):
                rest = PT - 1 - j
                last = nc.tensor.matmul(p_ends[:, (j + 1) * B:PT * B], k.ones[:, :],
                                        lt[:, j:j + 1, :].to_broadcast([P, rest, B]), start=False, stop=(rest == 1))
            last.then_inc(ends_ready, 1)
            pe.wait_ge(hit_ready, 2)
            for j in range(PT):
                last = nc.tensor.matmul(p_hits[:, :], ones_h[:, :],
                                        hit[:, j * B:(j + 1) * B, :].rearrange("p b s -> p (b s)"),
                                        start=(j == 0), stop=(j == PT - 1))
            last.then_inc(hits_counted, 1)
            pe.wait_ge(ld_w, 48)
            for t in range(NT):
                o = p_out[:, t * BANK:(t + 1) * BANK]
                for c in range(DC):
                    nc.tensor.matmul(o, xt[:, c, t * P:(t + 1) * P], w_in[:, c, :], start=(c == 0), stop=False)
                nc.tensor.matmul(o, k.ones[0:1, :], b_row[0:1, :], start=False, stop=False)
            pe.wait_ge(picked, 1)
            nc.tensor.matmul(p_gat[:, :], scan[:, :, :].rearrange("p a b -> p (a b)"), pick[:, :],
                             start=True, stop=True).then_inc(gat_ready, 1)
            pe.wait_ge(gat_done, 2)
            pe.wait_ge(u_ready, NT)
            for t in range(NT):
                nc.tensor.matmul(p_out[:, t * BANK:(t + 1) * BANK], gather[:, t, :], ctx[:, t, 0:D],
                                 start=False, stop=True).then_inc(out_ready, 1)


DI, NS, RANK = 2 * D, 16, 32
EC = DI // P
NQ = 4


def mamba(nc, io, k, x, xn, xt):
    norm_transpose(nc, "n1", x, xn, xt, k.ident, 1e-5)
    conv_b, conv_w = col(k.cols, "conv_b"), col(k.cols, "conv_w").rearrange("p (c j) -> p c j", j=4)
    d_skip, dt_b = col(k.cols, "d_skip"), col(k.cols, "dt_b")
    with Stage(nc, "mb") as keep:
        xa = keep.sb("xa", [P, EC, TOK])
        gate = keep.sb("gate", [P, EC, TOK])
        delta = keep.sb("delta", [P, EC + 1, TOK])
        dbc = keep.sb("dbc", [RANK + 2 * NS, TOK])
        a_neg = keep.sb("a_neg", [P, EC, NS])
        mamba_in(nc, io, k, xt, xa, gate, delta, dbc, a_neg, conv_b, conv_w, dt_b)
        mamba_scan(nc, io, k, xa, delta, dbc, a_neg)
        mamba_out(nc, io, x, xa, gate, delta, d_skip)


def mamba_in(nc, io, k, xt, xa, gate, delta, dbc, a_neg, conv_b, conv_w, dt_b):
    TAPS = 4
    with Stage(nc, "mi") as st:
        w = st.sb("w", [P, DC, 2 * DI])
        w_x = st.sb("w_x", [P, EC, RANK + 2 * NS])
        w_dt = st.sb("w_dt", [RANK, DI])
        a_log = st.sb("a_log", [P, EC, NS])
        pad = [st.sb(f"pad{i}", [P, B, S + TAPS - 1]) for i in range(2)]
        acc = [st.sb(f"acc{i}", [P, B, S]) for i in range(2)]
        v_abs, v_exp, v_one, v_ln, v_inv, v_max = [st.sb(n, [P, 2, TOK]) for n in
                                                   "v_abs v_exp v_one v_ln v_inv v_max".split()]
        proj = st.ps("proj", 4)
        p_dbc = st.ps("p_dbc")
        p_dt = st.ps("p_dt", 2)
        ld_x, ld_dt, ld_a, padded, conv_out, proj_ready, x_copied, gated, xa_ready, dbc_ready, dbc_copied, \
            dt_ready, exp_ready, one_ready, ln_ready, chain, a_chain, v_maxed, v_copied, v_step = st.sems(
                "ld_x ld_dt ld_a padded conv_out proj_ready x_copied gated xa_ready dbc_ready dbc_copied "
                "dt_ready exp_ready one_ready ln_ready chain a_chain v_maxed v_copied v_step")
        ld_wc = [st.sem(f"ld_w{c}") for c in range(DC)]
        block = st.block()

        @block.sync
        def _(sp):
            for c in range(DC):
                sp.dma_start(w[:, c, :], io.in_proj[:, c, :]).then_inc(ld_wc[c], 16)
            sp.dma_start(w_x[:, :, :], io.x_proj).then_inc(ld_x, 16)
            sp.dma_start(w_dt[:, :], io.dt_proj).then_inc(ld_dt, 16)
            sp.dma_start(a_log[:, :, :], io.a_log).then_inc(ld_a, 16)

        @block.gpsimd
        def _(g):
            for i in range(2):
                g.memset(pad[i][:, :, 0:TAPS - 1], 0.0).then_inc(padded, 1)

        @block.tensor
        def _(pe):
            for c in range(DC):
                pe.wait_ge(ld_wc[c], 16)
            for e in range(2 * EC):
                if e >= 4:
                    if e % 2 == 0:
                        pe.wait_ge(x_copied, (e - 4) // 2 + 1)
                    else:
                        pe.wait_ge(gated, (e - 4) // 2 + 1)
                f = (e // 2) * P + (e % 2) * DI
                for c in range(DC):
                    last = nc.tensor.matmul(proj[:, (e % 4) * BANK:(e % 4 + 1) * BANK], w[:, c, f:f + P], xt[:, c, :],
                                            start=(c == 0), stop=(c == DC - 1))
                last.then_inc(proj_ready, 1)
            pe.wait_ge(ld_x, 16)
            for e in range(EC):
                pe.wait_ge(xa_ready, e + 1)
                last = nc.tensor.matmul(p_dbc[0:RANK + 2 * NS, :], w_x[:, e, :], xa[:, e, :],
                                        start=(e == 0), stop=(e == EC - 1))
            last.then_inc(dbc_ready, 1)
            pe.wait_ge(dbc_copied, 1)
            pe.wait_ge(ld_dt, 16)
            for e in range(EC):
                if e >= 2:
                    pe.wait_ge(v_copied, e - 1)
                nc.tensor.matmul(p_dt[:, (e % 2) * BANK:(e % 2 + 1) * BANK], w_dt[:, e * P:(e + 1) * P],
                                 dbc[0:RANK, :], start=True, stop=True).then_inc(dt_ready, 1)

        @block.scalar
        def _(act):
            for e in range(EC):
                act.wait_ge(proj_ready, 2 * e + 1)
                if e < 2:
                    act.wait_ge(padded, 2)
                else:
                    act.wait_ge(conv_out, e - 1)
                nc.scalar.activation(pad[e % 2][:, :, TAPS - 1:], proj[:, (2 * e % 4) * BANK:(2 * e % 4 + 1) * BANK]
                                     .rearrange("p (b s) -> p b s", s=S), ACT.Copy).then_inc(x_copied, 1)
                act.wait_ge(proj_ready, 2 * e + 2)
                o = (2 * e + 1) % 4
                nc.scalar.activation(gate[:, e, :], proj[:, o * BANK:(o + 1) * BANK], ACT.Silu).then_inc(gated, 1)
                act.wait_ge(conv_out, e + 1)
                nc.scalar.activation(xa[:, e, :], acc[e % 2][:, :, :].rearrange("p b s -> p (b s)"),
                                     ACT.Silu).then_inc(xa_ready, 1)
            act.wait_ge(dbc_ready, 1)
            nc.scalar.activation(dbc[:, :], p_dbc[0:RANK + 2 * NS, :], ACT.Copy).then_inc(dbc_copied, 1)
            act.wait_ge(ld_a, 16)
            nc.scalar.activation(a_neg[:, :, :], a_log[:, :, :], ACT.Exp).then_inc(a_chain, 1)
            n = 1
            for e in range(0, EC, 2):
                act.wait_ge(dt_ready, e + 2)
                if e:
                    act.wait_ge(v_step, 2 * e)
                for h in range(2):
                    nc.scalar.activation(v_max[:, h, :], p_dt[:, h * BANK:(h + 1) * BANK], ACT.Identity,
                                         bias=dt_b[:, e + h:e + h + 1]).then_inc(v_copied, 1)
                act.wait_ge(v_copied, e + 2)
                nc.scalar.activation(v_abs[:, :, :], v_max[:, :, :], ACT.Abs).then_inc(a_chain, 1)
                n += 1
                act.wait_ge(a_chain, n)
                nc.scalar.activation(v_exp[:, :, :], v_abs[:, :, :], ACT.Exp, scale=-1.0).then_inc(exp_ready, 1)
                act.wait_ge(one_ready, e // 2 + 1)
                nc.scalar.activation(v_ln[:, :, :], v_one[:, :, :], ACT.Ln).then_inc(a_chain, 1)
                n += 1
                act.wait_ge(a_chain, n)
                nc.scalar.activation(v_inv[:, :, :], v_ln[:, :, :], ACT.Exp, scale=-1.0).then_inc(ln_ready, 1)

        @block.vector
        def _(dve):
            c = Chain(dve, chain)
            for e in range(EC):
                dve.wait_ge(x_copied, e + 1)
                if e >= 2:
                    dve.wait_ge(xa_ready, e - 1)
                o, s = acc[e % 2], pad[e % 2]
                c.link(nc.vector.tensor_scalar(o[:, :, :], s[:, :, 0:S], conv_w[:, e, 0:1], conv_b[:, e:e + 1],
                                               ALU.mult, ALU.add))
                for j in range(1, TAPS):
                    ins = nc.vector.scalar_tensor_tensor(o[:, :, :], s[:, :, j:j + S], conv_w[:, e, j:j + 1],
                                                         o[:, :, :], ALU.mult, ALU.add)
                    if j < TAPS - 1:
                        c.link(ins)
                    else:
                        ins.then_inc(conv_out, 1)
            for e in range(0, EC, 2):
                dve.wait_ge(exp_ready, e // 2 + 1)
                nc.vector.tensor_scalar(v_max[:, :, :], v_max[:, :, :], 0.0, None, ALU.max).then_inc(v_maxed, 1)
                nc.vector.tensor_scalar(v_one[:, :, :], v_exp[:, :, :], 1.0, None, ALU.add).then_inc(one_ready, 1)
                dve.wait_ge(one_ready, e // 2 + 1)
                dve.wait_ge(ln_ready, e // 2 + 1)
                nc.vector.scalar_tensor_tensor(v_exp[:, :, :], v_one[:, :, :], -1.0, v_exp[:, :, :], ALU.add,
                                               ALU.subtract).then_inc(v_step, 1)
                dve.wait_ge(v_step, 4 * (e // 2) + 1)
                nc.vector.tensor_tensor(v_exp[:, :, :], v_exp[:, :, :], v_inv[:, :, :], ALU.mult).then_inc(v_step, 1)
                dve.wait_ge(v_step, 4 * (e // 2) + 2)
                nc.vector.tensor_tensor(v_ln[:, :, :], v_ln[:, :, :], v_exp[:, :, :], ALU.subtract).then_inc(v_step, 1)
                dve.wait_ge(v_step, 4 * (e // 2) + 3)
                dve.wait_ge(v_maxed, e // 2 + 1)
                nc.vector.tensor_tensor(delta[:, e + 1:e + 3, :], v_ln[:, :, :], v_max[:, :, :],
                                        ALU.add).then_inc(v_step, 1)
            dve.wait_ge(a_chain, 1)
            nc.vector.tensor_scalar(a_neg[:, :, :], a_neg[:, :, :], -1.0, None, ALU.mult).then_inc(v_step, 1)


def mamba_scan(nc, io, k, xa, delta, dbc, a_neg):
    with Stage(nc, "ms") as st:
        b_all = st.sb("b_all", [P, NS, TOK])
        c_all = st.sb("c_all", [P, NS, TOK])
        da = [st.sb(f"da{i}", [P, NQ, B, S]) for i in range(2)]
        h = [st.sb(f"h{i}", [P, NQ, TOK]) for i in range(2)]
        hc = [st.sb(f"hc{i}", [P, NQ, TOK]) for i in range(2)]
        du = st.sb("du", [P, TOK])
        p_bc = st.ps("p_bc", 4)
        p_y = st.ps("p_y")
        bc_ready, b_copied, c_copied, first_zero, da_ready, du_ready, h_set, scanned, hc_ready, summed, y_copied = \
            st.sems("bc_ready b_copied c_copied first_zero da_ready du_ready h_set scanned hc_ready summed y_copied")
        block = st.block()
        STEPS = NS // NQ
        flat = "p n t -> p (n t)"

        @block.gpsimd
        def _(g):
            for i in range(2):
                g.memset(da[i][:, :, :, 0:1], 0.0).then_inc(first_zero, 1)
            g.wait_ge(c_copied, NS)
            with g.Fori(0, EC) as e:
                for q in range(STEPS):
                    g.wait_ge(scanned, e * STEPS + (q + 3))
                    g.wait_ge(summed, e * STEPS + (q + 1))
                    g.tensor_tensor(hc[q % 2][:, :, :], h[q % 2][:, :, :], c_all[:, q * NQ:(q + 1) * NQ, :],
                                    ALU.mult).then_inc(hc_ready, 1)

        @block.tensor
        def _(pe):
            for n in range(2 * NS):
                if n >= 4:
                    pe.wait_ge(b_copied if n % 2 == 0 else c_copied, (n - 4) // 2 + 1)
                r = RANK + n // 2 + (n % 2) * NS
                nc.tensor.matmul(p_bc[:, (n % 4) * BANK:(n % 4 + 1) * BANK],
                                 k.ident[0:RANK + 2 * NS, r:r + 1].to_broadcast([RANK + 2 * NS, P]), dbc[:, :],
                                 start=True, stop=True).then_inc(bc_ready, 1)
            nc.tensor.matmul(p_y[:, :], k.ident[0:RANK + 2 * NS, :], dbc[:, :], start=True, stop=True)\
                .then_inc(summed, 2)
            with pe.Fori(0, EC) as e:
                pe.wait_ge(y_copied, e + 1)
                for q in range(STEPS):
                    pe.wait_ge(hc_ready, e * STEPS + (q + 3))
                    for n in range(NQ):
                        last = nc.tensor.matmul(p_y[:, :], k.ident[:, :], hc[q % 2][:, n, :],
                                                start=(q == 0 and n == 0), stop=(q == STEPS - 1 and n == NQ - 1))
                    last.then_inc(summed, 1)

        @block.scalar
        def _(act):
            for n in range(NS):
                act.wait_ge(bc_ready, 2 * n + 2)
                o = (2 * n + 1) % 4
                nc.scalar.activation(c_all[:, n, :], p_bc[:, o * BANK:(o + 1) * BANK], ACT.Copy)\
                    .then_inc(c_copied, 1)
            act.wait_ge(first_zero, 2)
            with act.Fori(0, EC) as e:
                for q in range(STEPS):
                    act.wait_ge(scanned, e * STEPS + (q + 1))
                    for n in range(NQ):
                        ins = nc.scalar.activation(
                            da[q % 2][:, n, :, 1:],
                            delta[:, bass.ds(e + 1, 1), :].rearrange("p a (b s) -> p (a b) s", s=S)[:, :, 1:],
                            ACT.Exp, scale=a_neg[:, bass.ds(e, 1), q * NQ + n:q * NQ + n + 1]
                            .rearrange("p a n -> p (a n)"))
                    ins.then_inc(da_ready, 1)
                    if q == 1:
                        act.wait_ge(summed, e * STEPS + 2)
                        act.wait_ge(du_ready, e + 1)
                        nc.scalar.activation(delta[:, bass.ds(e, 1), :].rearrange("p a t -> p (a t)"), p_y[:, :],
                                             ACT.Copy).then_inc(y_copied, 1)
            act.wait_ge(summed, EC * STEPS + 2)
            nc.scalar.activation(delta[:, EC, :], p_y[:, :], ACT.Copy).then_inc(y_copied, 1)

        @block.vector
        def _(dve):
            dve.sem_inc(scanned, 2)
            dve.sem_inc(hc_ready, 2)
            dve.sem_inc(h_set, 1)
            for n in range(NS):
                dve.wait_ge(bc_ready, 2 * n + 1)
                o = (2 * n) % 4
                nc.vector.tensor_copy(b_all[:, n, :], p_bc[:, o * BANK:(o + 1) * BANK]).then_inc(b_copied, 1)
            dve.wait_ge(b_copied, NS)
            with dve.Fori(0, EC) as e:
                dve.wait_ge(h_set, e * STEPS + 1)
                nc.vector.tensor_tensor(du[:, :], delta[:, bass.ds(e + 1, 1), :].rearrange("p a t -> p (a t)"),
                                        xa[:, bass.ds(e, 1), :].rearrange("p a t -> p (a t)"),
                                        ALU.mult).then_inc(du_ready, 1)
                dve.wait_ge(du_ready, e + 1)
                for q in range(STEPS):
                    dve.wait_ge(hc_ready, e * STEPS + (q + 1))
                    nc.vector.tensor_tensor(h[q % 2][:, :, :], b_all[:, q * NQ:(q + 1) * NQ, :],
                                            du[:, :].unsqueeze(1).to_broadcast([P, NQ, TOK]),
                                            ALU.mult).then_inc(h_set, 1)
                    dve.wait_ge(h_set, e * STEPS + (q + 2))
                    dve.wait_ge(da_ready, e * STEPS + (q + 1))
                    hf = h[q % 2][:, :, :].rearrange(flat)
                    nc.vector.tensor_tensor_scan(hf, da[q % 2][:, :, :, :].rearrange("p n b s -> p (n b s)"), hf,
                                                 0.0, ALU.mult, ALU.add).then_inc(scanned, 1)


def mamba_out(nc, io, x, xa, gate, delta, d_skip):
    with Stage(nc, "mo") as st:
        w = st.sb("w", [P, EC, D])
        p_out = st.ps("p_out", NT)
        skipped, gated, out_ready, added = st.sems("skipped gated out_ready added")
        ld_w = [st.sem(f"ld_w{i}") for i in range(2)]
        block = st.block()

        @block.sync
        def _(sp):
            for i in range(2):
                sp.dma_start(w[:, i * EC // 2:(i + 1) * EC // 2, :],
                             io.out_proj[:, i * EC // 2:(i + 1) * EC // 2, :]).then_inc(ld_w[i], 16)

        @block.vector
        def _(dve):
            for e in range(EC):
                nc.vector.scalar_tensor_tensor(xa[:, e, :], xa[:, e, :], d_skip[:, e:e + 1], delta[:, e + 1, :],
                                               ALU.mult, ALU.add).then_inc(skipped, 1)
                dve.wait_ge(skipped, e + 1)
                nc.vector.tensor_tensor(gate[:, e, :], gate[:, e, :], xa[:, e, :], ALU.mult).then_inc(gated, 1)
            for t in range(NT):
                dve.wait_ge(out_ready, t + 1)
                nc.vector.tensor_tensor(x[:, t, :], x[:, t, :], p_out[:, t * BANK:(t + 1) * BANK],
                                        ALU.add).then_inc(added, 1)
            dve.wait_ge(added, NT)

        @block.tensor
        def _(pe):
            for e in range(EC):
                pe.wait_ge(ld_w[2 * e // EC], 16)
                pe.wait_ge(gated, e + 1)
                for t in range(NT):
                    ins = nc.tensor.matmul(p_out[:, t * BANK:(t + 1) * BANK], gate[:, e, t * P:(t + 1) * P], w[:, e, :],
                                           start=(e == 0), stop=(e == EC - 1))
                    if e == EC - 1:
                        ins.then_inc(out_ready, 1)


HID = 4 * D
HC = HID // P
QB = 127.0


def bitnet(nc, io, k, x, xn, xt):
    norm_transpose(nc, "n2", x, xn, xt, k.ident, 1e-5, transpose=False)
    with Stage(nc, "bn") as st:
        w = [st.sb("w1", [P, DC * HID]), st.sb("w2", [P, HC * D])]
        wq = [st.sb("w1q", [P, DC * HID], bf16), st.sb("w2q", [P, HC * D], bf16)]
        b1, b2 = st.sb("b1", [P, HID]), st.sb("b2", [P, D])
        wsum, wscale, winv = st.sb("wsum", [P, 2]), st.sb("wscale", [P, 2]), st.sb("winv", [P, 2])
        amax, inv, oscale = st.sb("amax", [P, 2 * NT]), st.sb("inv", [P, 2 * NT]), st.sb("oscale", [P, 2 * NT])
        xq = st.sb("xq", [P, D], bf16)
        xqt = st.sb("xqt", [P, DC, P], bf16)
        h = st.sb("h", [P, HID])
        hq = st.sb("hq", [P, HID], bf16)
        hqt = st.sb("hqt", [P, HC, P], bf16)
        p_h = st.ps("p_h", 4)
        p_sum = st.ps("p_sum")
        p_out = st.ps("p_out")
        p_t = st.stack.enter_context(nc.psum_tensor("bn_p_t", [P, 2 * 2 * BANK], bf16))
        ld_b, abs_done, sums_ready, winv_ready, rounded, wq_ready, xq_ready, xt_ready, xt_copied, h_ready, biased, \
            gelued, hq_ready, ht_ready, ht_copied, y_ready, chain, added, w_chain = st.sems(
                "ld_b abs_done sums_ready winv_ready rounded wq_ready xq_ready xt_ready xt_copied h_ready biased "
                "gelued hq_ready ht_ready ht_copied y_ready chain added w_chain")
        ld_w = [st.sem(f"ld_w{i}") for i in range(2)]
        block = st.block()

        @block.sync
        def _(sp):
            sp.dma_start(w[0][:, :], io.w1.rearrange("p c n -> p (c n)")).then_inc(ld_w[0], 16)
            sp.dma_start(w[1][:, :], io.w2.rearrange("p c n -> p (c n)")).then_inc(ld_w[1], 16)
            sp.dma_start(b1[:, :], io.b1.partition_broadcast(P)).then_inc(ld_b, 16)
            sp.dma_start(b2[:, :], io.b2.partition_broadcast(P)).then_inc(ld_b, 16)

        @block.scalar
        def _(act):
            for i in range(2):
                act.wait_ge(ld_w[i], 16)
                nc.scalar.activation(wq[i][:, :], w[i][:, :], ACT.Abs, accum_out=wsum[:, i:i + 1]).then_inc(abs_done, 1)
            for i in range(2):
                act.wait_ge(winv_ready, 1)
                nc.scalar.activation(w[i][:, :], w[i][:, :], ACT.Copy, scale=winv[:, i:i + 1],
                                     bias=ROUND).then_inc(rounded, 1)
            for t in range(NT):
                act.wait_ge(xt_ready, t + 1)
                nc.scalar.activation(xqt[:, :, :], p_t[:, 0:D].rearrange("p (c n) -> p c n", n=P),
                                     ACT.Copy).then_inc(xt_copied, 1)
                act.wait_ge(biased, t + 1)
                nc.scalar.activation(h[:, :], h[:, :], ACT.Gelu).then_inc(gelued, 1)
                act.wait_ge(ht_ready, t + 1)
                nc.scalar.activation(hqt[:, :, :], p_t[:, :].rearrange("p (c n) -> p c n", n=P),
                                     ACT.Copy).then_inc(ht_copied, 1)

        @block.vector
        def _(dve):
            c = Chain(dve, chain)

            def quantize(out, v, at, wi):
                c.link(nc.vector.tensor_reduce(amax[:, at:at + 1], v, AX.X, ALU.max, apply_absolute_value=True))
                c.link(nc.vector.tensor_scalar(amax[:, at:at + 1], amax[:, at:at + 1], 1e-5, None, ALU.max))
                c.link(nc.vector.reciprocal(inv[:, at:at + 1], amax[:, at:at + 1]))
                c.link(nc.vector.tensor_scalar(inv[:, at:at + 1], inv[:, at:at + 1], QB, None, ALU.mult))
                c.mark(nc.vector.tensor_scalar(oscale[:, at:at + 1], amax[:, at:at + 1], wscale[:, wi:wi + 1],
                                               1.0 / QB, ALU.mult, ALU.mult))
                c.link(nc.vector.tensor_scalar(v, v, inv[:, at:at + 1], -QB - 1.0, ALU.mult, ALU.max))
                c.link(nc.vector.tensor_scalar(v, v, QB, ROUND, ALU.min, ALU.add))
                return nc.vector.tensor_scalar(out, v, -ROUND, None, ALU.add)

            dve.wait_ge(sums_ready, 1)
            c.link(nc.vector.tensor_scalar(wscale[:, :], p_sum[:, 0:2], 1.0 / (D * HID), 1e-5, ALU.mult, ALU.max))
            nc.vector.reciprocal(winv[:, :], wscale[:, :]).then_inc(winv_ready, 1)
            for i in range(2):
                dve.wait_ge(rounded, i + 1)
                nc.vector.tensor_scalar(w[i][:, :], w[i][:, :], ROUND + 1.0, ROUND - 1.0, ALU.min,
                                        ALU.max).then_inc(w_chain, 1)
                dve.wait_ge(w_chain, i + 1)
                nc.vector.tensor_scalar(wq[i][:, :], w[i][:, :], -ROUND, None, ALU.add).then_inc(wq_ready, 1)
            dve.wait_ge(ld_b, 32)
            for t in range(NT):
                if t:
                    dve.wait_ge(xt_ready, t)
                quantize(xq[:, :], xn[:, t, :], t, 0).then_inc(xq_ready, 1)
                dve.wait_ge(h_ready, t + 1)
                if t:
                    dve.wait_ge(hq_ready, t)
                nc.vector.scalar_tensor_tensor(h[:, :], p_h[:, :], oscale[:, t:t + 1], b1[:, :], ALU.mult,
                                               ALU.add).then_inc(biased, 1)
                dve.wait_ge(gelued, t + 1)
                if t:
                    dve.wait_ge(ht_ready, t)
                quantize(hq[:, :], h[:, :], NT + t, 1).then_inc(hq_ready, 1)
                dve.wait_ge(y_ready, t + 1)
                c.link(nc.vector.scalar_tensor_tensor(xn[:, t, :], p_out[:, :], oscale[:, NT + t:NT + t + 1],
                                                      b2[:, :], ALU.mult, ALU.add))
                nc.vector.tensor_tensor(x[:, t, :], x[:, t, :], xn[:, t, :], ALU.add).then_inc(added, 1)
            dve.wait_ge(added, NT)

        @block.tensor
        def _(pe):
            pe.wait_ge(abs_done, 2)
            nc.tensor.matmul(p_sum[:, 0:2], k.ones[:, :], wsum[:, :], start=True, stop=True).then_inc(sums_ready, 1)
            for t in range(NT):
                pe.wait_ge(xq_ready, t + 1)
                if t:
                    pe.wait_ge(ht_copied, t)
                for c in range(DC):
                    last = nc.tensor.transpose(p_t[:, c * P:(c + 1) * P], xq[:, c * P:(c + 1) * P], k.ident_h[:, :])
                last.then_inc(xt_ready, 1)
                pe.wait_ge(xt_copied, t + 1)
                pe.wait_ge(wq_ready, 1)
                if t:
                    pe.wait_ge(biased, t)
                w1 = wq[0][:, :].rearrange("p (c n) -> p c n", n=HID)
                for j in range(4):
                    for c in range(DC):
                        last = nc.tensor.matmul(p_h[:, j * BANK:(j + 1) * BANK], xqt[:, c, :],
                                                w1[:, c, j * BANK:(j + 1) * BANK], start=(c == 0), stop=(c == DC - 1))
                last.then_inc(h_ready, 1)
                pe.wait_ge(hq_ready, t + 1)
                for c in range(HC):
                    last = nc.tensor.transpose(p_t[:, c * P:(c + 1) * P], hq[:, c * P:(c + 1) * P], k.ident_h[:, :])
                last.then_inc(ht_ready, 1)
                pe.wait_ge(ht_copied, t + 1)
                pe.wait_ge(wq_ready, 2)
                if t:
                    pe.wait_ge(added, t)
                w2 = wq[1][:, :].rearrange("p (c n) -> p c n", n=D)
                for c in range(HC):
                    last = nc.tensor.matmul(p_out[:, :], hqt[:, c, :], w2[:, c, :], start=(c == 0), stop=(c == HC - 1))
                last.then_inc(y_ready, 1)


HEADS, DH = 16, 64
PAIRS = HEADS // 2
GROUPS = 2
GP = PAIRS // GROUPS
CC = CW // P
JT = (CTX + P - 1) // P
KEYS = CTX + 1
LAST = CTX - (JT - 1) * P
CUTS = [0, 401, 802, 1202, KEYS]
W_UP = 64.0
P_UP = 4096.0
ITEMS = 4 * GP + JT


def cross_attention(nc, io, k, x, xn, xt, work):
    norm_transpose(nc, "n3", x, xn, xt, k.ident, 1e-5)
    q_parts = work.bitcast(f16).rearrange("p (b l c s) -> p b l c s", b=B, l=2, c=PAIRS)
    o_t = work.rearrange("p (b c s) -> p b c s", b=B, c=PAIRS)
    with Stage(nc, "cq") as st:
        w = st.sb("w", [P, DC, PAIRS * P])
        q = st.sb("q", [P, 2, PAIRS, TOK], f16)
        p_q = st.ps("p_q", 4)
        ld_w, q_ready, high_done, low_done, moved = st.sems("ld_w q_ready high_done low_done moved")
        block = st.block()

        @block.sync
        def _(sp):
            sp.dma_start(w[:, :, :], io.w_q).then_inc(ld_w, 16)

        @block.tensor
        def _(pe):
            pe.wait_ge(ld_w, 16)
            for f in range(PAIRS):
                if f >= 4:
                    pe.wait_ge(low_done, f - 3)
                for c in range(DC):
                    last = nc.tensor.matmul(p_q[:, (f % 4) * BANK:(f % 4 + 1) * BANK], w[:, c, f * P:(f + 1) * P],
                                            xt[:, c, :], start=(c == 0), stop=(c == DC - 1))
                last.then_inc(q_ready, 1)

        @block.scalar
        def _(act):
            for f in range(PAIRS):
                act.wait_ge(q_ready, f + 1)
                nc.scalar.activation(q[:, 0, f, :], p_q[:, (f % 4) * BANK:(f % 4 + 1) * BANK], ACT.Copy)\
                    .then_inc(high_done, 1)
            act.wait_ge(low_done, PAIRS)
            nc.scalar.activation(q_parts[:, :, 0, :, :], q[:, 0, :, :].rearrange("p c (b s) -> p b c s", b=B),
                                 ACT.Copy).then_inc(moved, 1)
            act.wait_ge(moved, 2)

        @block.vector
        def _(dve):
            for f in range(PAIRS):
                dve.wait_ge(high_done, f + 1)
                nc.vector.tensor_tensor(q[:, 1, f, :], p_q[:, (f % 4) * BANK:(f % 4 + 1) * BANK], q[:, 0, f, :],
                                        ALU.subtract).then_inc(low_done, 1)
            dve.wait_ge(low_done, PAIRS)
            nc.vector.tensor_copy(q_parts[:, :, 1, :, :], q[:, 1, :, :].rearrange("p c (b s) -> p b c s", b=B))\
                .then_inc(moved, 1)

    with Stage(nc, "ca") as st:
        w_kv = [st.sb(f"w_kv{i}", [P, CC, 2 * HEADS * DH], f16) for i in range(2)]
        ctx = [st.sb(f"ctx{i}", [P, CC, CTX], f16) for i in range(2)]
        v_last = [st.sb(f"v_last{i}", [P, GROUPS, GP * P], f16) for i in range(2)]
        keys = [[st.sb(f"keys{s}{i}", [P, KEYS], f16) for i in range(2)] for s in range(2)]
        stage = [st.sb(f"stage{s}", [P, CC * P]) for s in range(2)]
        split_weights(nc, io, w_kv, v_last, keys)
        attend(nc, io, w_kv, ctx, v_last, keys, stage, q_parts, o_t, st, k)
    project_out(nc, io, k, x, o_t)


def split_weights(nc, io, w_kv, v_last, keys):
    with Stage(nc, "cw") as st:
        raw = [st.sb(f"raw{s}", [P, 2 * HEADS * DH]) for s in range(2)]
        nk, nv = st.sb("nk", [P, 1]), st.sb("nv", [1, GP * P])
        nk_high, nk_low = st.sb("nk_high", [P, 1], f16), st.sb("nk_low", [P, 1], f16)
        nv_parts = st.sb("nv_parts", [1, 2, GP * P], f16)
        ld_null, high_done, low_done, null_high, null_low, null_set = st.sems(
            "ld_null high_done low_done null_high null_low null_set")
        ld_w = [st.sem(f"ld_w{s}") for s in range(2)]
        block = st.block()

        @block.sync
        def _(sp):
            sp.dma_start(nk[:, :], io.null_k).then_inc(ld_null, 16)
            sp.dma_start(nv[:, :], io.null_v).then_inc(ld_null, 16)
            for c in range(CC):
                if c >= 2:
                    sp.wait_ge(low_done, c - 1)
                sp.dma_start(raw[c % 2][:, :], io.w_kv[:, c, :]).then_inc(ld_w[c % 2], 16)
            sp.wait_ge(null_low, 2)
            for i in range(2):
                for g in range(GROUPS):
                    sp.dma_start(v_last[i][LAST:LAST + 1, g, :], nv_parts[:, i, :]).then_inc(null_set, 16)
            sp.wait_ge(null_set, 16 * 2 * GROUPS)

        @block.scalar
        def _(act):
            act.wait_ge(ld_null, 32)
            nc.scalar.activation(nk_high[:, :], nk[:, :], ACT.Copy, scale=W_UP).then_inc(null_high, 1)
            nc.scalar.activation(nv_parts[:, 0, :], nv[:, :], ACT.Copy, scale=W_UP).then_inc(null_high, 1)
            for c in range(CC):
                act.wait_ge(ld_w[c % 2], 16 * (c // 2 + 1))
                nc.scalar.activation(w_kv[0][:, c, :], raw[c % 2][:, :], ACT.Copy, scale=W_UP).then_inc(high_done, 1)

        @block.vector
        def _(dve):
            dve.wait_ge(null_high, 2)
            nc.vector.scalar_tensor_tensor(nk_low[:, :], nk[:, :], W_UP, nk_high[:, :], ALU.mult,
                                           ALU.subtract).then_inc(null_low, 1)
            nc.vector.scalar_tensor_tensor(nv_parts[:, 1, :], nv[:, :], W_UP, nv_parts[:, 0, :], ALU.mult,
                                           ALU.subtract).then_inc(null_low, 1)
            dve.wait_ge(null_low, 2)
            for s in range(2):
                nc.vector.tensor_copy(keys[s][0][:, CTX:KEYS], nk_high[:, :])
                last = nc.vector.tensor_copy(keys[s][1][:, CTX:KEYS], nk_low[:, :])
            for c in range(CC):
                dve.wait_ge(high_done, c + 1)
                nc.vector.scalar_tensor_tensor(w_kv[1][:, c, :], raw[c % 2][:, :], W_UP, w_kv[0][:, c, :], ALU.mult,
                                               ALU.subtract).then_inc(low_done, 1)
            dve.wait_ge(low_done, CC)


def attend(nc, io, w_kv, ctx, v_last, keys, stage, q_parts, o_t, st, k):
    probs = st.sb("probs", [P, GP, KEYS])
    q_diag = [st.sb(f"q_diag{i}", [P, PAIRS, P], f16) for i in range(2)]
    vals = [[st.sb(f"vals{s}{i}", [P, GP * P], f16) for i in range(2)] for s in range(2)]
    pt = [[st.sb(f"pt{s}{i}", [P, GP * P], f16) for i in range(2)] for s in range(2)]
    zeros = st.sb("zeros", [1, BANK], f16)
    peak = st.sb("peak", [P, PAIRS, 2])
    nbias = st.sb("nbias", [P, PAIRS])
    rsum = st.sb("rsum", [P, PAIRS, 2])
    rinv = st.sb("rinv", [P, PAIRS])
    p_kv = st.ps("p_kv", 2)
    p_s = st.ps("p_s", 4)
    p_o = st.ps("p_o")
    p_t = st.ps("p_t")
    prod_ready, high_done, low_done, s_ready, max_done, exp_done, norm_done, t_ready, th_done, tl_done, av_done, \
        o_ready, o_copied, ctx_high, ctx_low, q_ready, zeroed, dchain = st.sems(
            "prod_ready high_done low_done s_ready max_done exp_done norm_done t_ready th_done tl_done av_done "
            "o_ready o_copied ctx_high ctx_low q_ready zeroed dchain")
    ld = [st.sem(f"ld{s}") for s in range(2)]
    block = st.block()
    SEQ = GROUPS * ITEMS

    def rows(j):
        return LAST if j == JT - 1 else P

    def chunk(n):
        return CUTS[n], min(CUTS[n + 1], CTX)

    def bank(i):
        return p_kv[:, (i % 2) * BANK:(i % 2 + 1) * BANK]

    def scores(n, n2):
        w = CUTS[n + 1] - CUTS[n]
        return p_s[:, n * BANK:n2 * BANK].rearrange("p (a n) -> p a n", n=BANK)[:, :, 0:w]

    @block.sync
    def _(sp):
        def load(j, seq):
            sp.dma_start(stage[j % 2][:, :], io.ctx_t[bass.ds(seq, 1), j, :, :].rearrange("a p n -> (a p) n"))\
                .then_inc(ld[j % 2], 16)

        for j in range(JT):
            if j >= 2:
                sp.wait_ge(ctx_low, j - 1)
            load(j, 0)
        with sp.Fori(0, B) as b:
            for j in range(JT):
                sp.wait_ge(ctx_low, b * JT + (JT + j - (1 if j else 0)))
                load(j, (b + 1) % B)
        sp.wait_ge(ld[0], 16 * (JT // 2 + 1) * (B + 1))
        sp.wait_ge(ld[1], 16 * (JT // 2) * (B + 1))

    def split_high(act, j, turn):
        n = (JT // 2 + 1) if j % 2 == 0 else JT // 2
        act.wait_ge(ld[j % 2], turn * (16 * n) + 16 * (j // 2 + 1))
        w = rows(j)
        nc.scalar.activation(ctx[0][:, :, j * P:j * P + w],
                             stage[j % 2][:, :].rearrange("p (c n) -> p c n", n=P)[:, :, 0:w],
                             ACT.Copy).then_inc(ctx_high, 1)

    def split_low(dve, j, turn):
        dve.wait_ge(ctx_high, turn * JT + (j + 1))
        w = rows(j)
        nc.vector.tensor_tensor(ctx[1][:, :, j * P:j * P + w],
                                stage[j % 2][:, :].rearrange("p (c n) -> p c n", n=P)[:, :, 0:w],
                                ctx[0][:, :, j * P:j * P + w], ALU.subtract).then_inc(ctx_low, 1)

    @block.gpsimd
    def _(g):
        g.memset(zeros[:, :], 0.0).then_inc(zeroed, 1)
        for i in range(2):
            g.memset(q_diag[i][:, :, :], 0.0).then_inc(zeroed, 1)
        g.wait_ge(zeroed, 3)
        with g.Fori(0, B) as b:
            g.wait_ge(s_ready, b * PAIRS + 2)
            for i in range(2):
                for h in range(2):
                    g.tensor_copy(q_diag[i][h * DH:(h + 1) * DH, :, h * S:(h + 1) * S],
                                  q_parts[h * DH:(h + 1) * DH, bass.ds(b, 1), i, :, :]
                                  .rearrange("p a c s -> p (a c) s")).then_inc(q_ready, 1)

    @block.tensor
    def _(pe):
        pe.wait_ge(zeroed, 1)
        pe.sem_inc(s_ready, 2)
        pe.sem_inc(t_ready, 1)
        pe.sem_inc(av_done, 2)
        with pe.Fori(0, B) as b:
            for g in range(GROUPS):
                def bank_free(m):
                    pe.wait_ge(low_done, b * SEQ + (g * ITEMS + m + 1))

                def keys_of(p):
                    f = (g * GP + p) * P
                    for n in range(4):
                        m = 4 * p + n
                        bank_free(m)
                        lo, hi = chunk(n)
                        pe.wait_ge(ctx_low, b * JT + (hi + P - 1) // P)
                        o = bank(g * ITEMS + m)[:, 0:hi - lo]
                        for c in range(CC):
                            nc.tensor.matmul(o, w_kv[0][:, c, f:f + P], ctx[0][:, c, lo:hi], start=(c == 0), stop=False)
                            nc.tensor.matmul(o, w_kv[0][:, c, f:f + P], ctx[1][:, c, lo:hi], start=False, stop=False)
                            last = nc.tensor.matmul(o, w_kv[1][:, c, f:f + P], ctx[0][:, c, lo:hi], start=False,
                                                    stop=(c == CC - 1))
                        last.then_inc(prod_ready, 1)

                def scores_of(p):
                    pe.wait_ge(low_done, b * SEQ + (g * ITEMS + 4 * p + 6))
                    pe.wait_ge(exp_done, b * PAIRS + (g * GP + p + 1))
                    if p == 0:
                        pe.wait_ge(q_ready, 4 * b + 4)
                    kh, kl = keys[p % 2]
                    f = g * GP + p
                    for n in range(4):
                        o = p_s[:, n * BANK:n * BANK + CUTS[n + 1] - CUTS[n]]
                        kk = slice(CUTS[n], CUTS[n + 1])
                        nc.tensor.matmul(o, q_diag[0][:, f, :], kh[:, kk], start=True, stop=False)
                        nc.tensor.matmul(o, q_diag[0][:, f, :], kl[:, kk], start=False, stop=False)
                        last = nc.tensor.matmul(o, q_diag[1][:, f, :], kh[:, kk], start=False, stop=True)
                    last.then_inc(s_ready, 1)

                def values_of(j):
                    m = 4 * GP + j
                    bank_free(m)
                    w, f = rows(j), HEADS * DH + g * GP * P
                    o = bank(g * ITEMS + m)[0:w, :]
                    cols = slice(j * P, j * P + w)
                    for c in range(CC):
                        nc.tensor.matmul(o, ctx[0][:, c, cols], w_kv[0][:, c, f:f + BANK], start=(c == 0), stop=False)
                        nc.tensor.matmul(o, ctx[0][:, c, cols], w_kv[1][:, c, f:f + BANK], start=False, stop=False)
                        last = nc.tensor.matmul(o, ctx[1][:, c, cols], w_kv[0][:, c, f:f + BANK], start=False,
                                                stop=(c == CC - 1))
                    last.then_inc(prod_ready, 1)

                def transpose_of(j):
                    if j == 0:
                        pe.wait_ge(norm_done, b * PAIRS + (g + 1) * GP)
                    pe.wait_ge(tl_done, b * GROUPS * JT + (g * JT + j + 1))
                    w = rows(j) + (j == JT - 1)
                    for p in range(GP):
                        last = nc.tensor.transpose(p_t[0:w, p * P:(p + 1) * P], probs[:, p, j * P:j * P + w],
                                                   k.ident[:, :])
                    last.then_inc(t_ready, 1)

                def attend_to(j):
                    pe.wait_ge(low_done, b * SEQ + (g * ITEMS + 4 * GP + j + 3))
                    pe.wait_ge(tl_done, b * GROUPS * JT + (g * JT + j + 2))
                    w = rows(j) + (j == JT - 1)
                    for p in range(GP):
                        o, f = p_o[:, p * P:(p + 1) * P], slice(p * P, (p + 1) * P)
                        v = [v_last[i][0:w, g, f] if j == JT - 1 else vals[j % 2][i][:, f] for i in range(2)]
                        a = [pt[j % 2][i][0:w, f] for i in range(2)]
                        nc.tensor.matmul(o, v[0], a[0], start=False, stop=False)
                        nc.tensor.matmul(o, v[0], a[1], start=False, stop=False)
                        last = nc.tensor.matmul(o, v[1], a[0], start=False, stop=(j == JT - 1 and p == GP - 1))
                    last.then_inc(av_done, 1)
                    if j == JT - 1:
                        pe.wait_ge(av_done, b * GROUPS * JT + ((g + 1) * JT + 2))
                        pe.sem_inc(o_ready, 1)

                for p in range(GP):
                    keys_of(p)
                    if p:
                        scores_of(p - 1)
                pe.wait_ge(o_copied, b * GROUPS + (g + 1))
                nc.tensor.matmul(p_o[:, :], zeros[0:1, 0:P], zeros[0:1, :], start=True, stop=False)
                for j in range(JT + 2):
                    if j < JT:
                        values_of(j)
                    if j == 0:
                        scores_of(GP - 1)
                    if 1 <= j <= JT:
                        transpose_of(j - 1)
                    if j >= 2:
                        attend_to(j - 2)

    @block.scalar
    def _(act):
        act.sem_inc(exp_done, 1)
        for j in range(JT):
            split_high(act, j, 0)
        with act.Fori(0, B) as b:
            for g in range(GROUPS):
                def high(m, out, w, parts):
                    act.wait_ge(prod_ready, b * SEQ + (g * ITEMS + m + 1))
                    nc.scalar.activation(out, bank(g * ITEMS + m)[0:parts, 0:w], ACT.Copy).then_inc(high_done, 1)

                def exps(p):
                    f = g * GP + p
                    act.wait_ge(max_done, b * PAIRS + (f + 1))
                    if p == 0:
                        act.wait_ge(t_ready, b * GROUPS * JT + (g * JT + 1))
                    nc.scalar.activation(probs[:, p, 0:CUTS[2]].rearrange("p (a n) -> p a n", a=2), scores(0, 2),
                                         ACT.Exp, bias=nbias[:, f:f + 1], scale=1.0 / (8 * W_UP),
                                         accum_out=rsum[:, f, 0:1])
                    nc.scalar.activation(probs[:, p, CUTS[2]:KEYS].rearrange("p (a n) -> p a n", a=2), scores(2, 4),
                                         ACT.Exp, bias=nbias[:, f:f + 1], scale=1.0 / (8 * W_UP),
                                         accum_out=rsum[:, f, 1:2]).then_inc(exp_done, 1)

                for p in range(GP):
                    act.wait_ge(s_ready, b * PAIRS + (g * GP + p + 1))
                    for n in range(4):
                        lo, hi = chunk(n)
                        high(4 * p + n, keys[p % 2][0][:, lo:hi], hi - lo, P)
                    if p:
                        exps(p - 1)
                for j in range(JT + 1):
                    if j < JT:
                        act.wait_ge(av_done, b * GROUPS * JT + (g * JT + j + 1))
                        w = rows(j)
                        out = v_last[0][0:w, g, :] if j == JT - 1 else vals[j % 2][0][:, :]
                        high(4 * GP + j, out, BANK, w)
                    if j == 0:
                        exps(GP - 1)
                    if j >= 1:
                        jj = j - 1
                        act.wait_ge(t_ready, b * GROUPS * JT + (g * JT + jj + 2))
                        act.wait_ge(av_done, b * GROUPS * JT + (g * JT + jj + (1 if jj else 2)))
                        w = rows(jj) + (jj == JT - 1)
                        nc.scalar.activation(pt[jj % 2][0][0:w, :], p_t[0:w, :], ACT.Copy).then_inc(th_done, 1)
                    if g == GROUPS - 1 and j < JT:
                        split_high(act, j, b + 1)

    @block.vector
    def _(dve):
        dve.sem_inc(low_done, 2)
        dve.sem_inc(tl_done, 1)
        dve.sem_inc(o_copied, 1)
        for j in range(JT):
            split_low(dve, j, 0)
        with dve.Fori(0, B) as b:
            for g in range(GROUPS):
                def low(m, out, high, w, parts):
                    dve.wait_ge(high_done, b * SEQ + (g * ITEMS + m + 1))
                    nc.vector.tensor_tensor(out, bank(g * ITEMS + m)[0:parts, 0:w], high,
                                            ALU.subtract).then_inc(low_done, 1)

                def softmax(p):
                    f = g * GP + p
                    at = 5 * f
                    def step(i):
                        dve.wait_ge(dchain, b * (5 * PAIRS) + (at + i))
                    dve.wait_ge(s_ready, b * PAIRS + (f + 3))
                    nc.vector.tensor_reduce(peak[:, f, 0:1], scores(0, 2), AX.XY, ALU.max).then_inc(dchain, 1)
                    nc.vector.tensor_reduce(peak[:, f, 1:2], scores(2, 4), AX.XY, ALU.max).then_inc(dchain, 1)
                    step(2)
                    nc.vector.tensor_scalar(nbias[:, f:f + 1], peak[:, f, 0:1], peak[:, f, 1:2], -1.0 / (8 * W_UP),
                                            ALU.max, ALU.mult).then_inc(max_done, 1)
                    dve.wait_ge(exp_done, b * PAIRS + (f + 2))
                    nc.vector.tensor_tensor(rinv[:, f:f + 1], rsum[:, f, 0:1], rsum[:, f, 1:2],
                                            ALU.add).then_inc(dchain, 1)
                    step(3)
                    nc.vector.reciprocal(rsum[:, f, 0:1], rinv[:, f:f + 1]).then_inc(dchain, 1)
                    step(4)
                    nc.vector.tensor_scalar(probs[:, p, :], probs[:, p, :], rsum[:, f, 0:1], P_UP, ALU.mult,
                                            ALU.mult).then_inc(norm_done, 1)
                    dve.sem_inc(dchain, 1)

                for p in range(GP):
                    for n in range(4):
                        lo, hi = chunk(n)
                        low(4 * p + n, keys[p % 2][1][:, lo:hi], keys[p % 2][0][:, lo:hi], hi - lo, P)
                    if p:
                        softmax(p - 1)
                for j in range(JT + 1):
                    if j < JT:
                        w = rows(j)
                        out = [v_last[i][0:w, g, :] if j == JT - 1 else vals[j % 2][i][:, :] for i in range(2)]
                        low(4 * GP + j, out[1], out[0], BANK, w)
                    if j == 0:
                        softmax(GP - 1)
                    if j >= 1:
                        jj = j - 1
                        w = rows(jj) + (jj == JT - 1)
                        dve.wait_ge(th_done, b * GROUPS * JT + (g * JT + jj + 1))
                        nc.vector.tensor_tensor(pt[jj % 2][1][0:w, :], p_t[0:w, :], pt[jj % 2][0][0:w, :],
                                                ALU.subtract).then_inc(tl_done, 1)
                    if g == GROUPS - 1 and j < JT:
                        split_low(dve, j, b + 1)
                dve.wait_ge(o_ready, b * GROUPS + (g + 1))
                dve.wait_ge(q_ready, 4 * b + 4)
                for h in range(2):
                    ins = nc.vector.tensor_scalar(
                        o_t[h * DH:(h + 1) * DH, bass.ds(b, 1), g * GP:(g + 1) * GP, :].rearrange("p a c s -> p (a c) s"),
                        p_o[h * DH:(h + 1) * DH, :].rearrange("p (c h s) -> p c h s", h=2, s=S)[:, :, h, :],
                        1.0 / (W_UP * P_UP), None, ALU.mult)
                ins.then_inc(o_copied, 1)


def project_out(nc, io, k, x, o_t):
    with Stage(nc, "co") as st:
        w = st.sb("w", [P, PAIRS, D])
        scale, bias = st.sb("scale", [P, D]), st.sb("bias", [P, D])
        o = st.sb("o", [P, NT, D])
        heads = st.sb("heads", [P, PAIRS, TOK])
        stats, mv = st.sb("stats", [P, NT, 6]), st.sb("mv", [P, NT, 2])
        var, root = st.sb("var", [P, NT]), st.sb("root", [P, NT])
        p_out = st.ps("p_out", NT)
        ld_w, ld_b, moved, out_ready, var_ready, root_ready, chain = st.sems(
            "ld_w ld_b moved out_ready var_ready root_ready chain")
        block = st.block()

        @block.sync
        def _(sp):
            sp.dma_start(w[:, :, :], io.w_out).then_inc(ld_w, 16)
            sp.dma_start(scale[:, :], io.ln_scale.partition_broadcast(P)).then_inc(ld_b, 16)
            sp.dma_start(bias[:, :], io.ln_bias.partition_broadcast(P)).then_inc(ld_b, 16)

        @block.tensor
        def _(pe):
            pe.wait_ge(ld_w, 16)
            for t in range(NT):
                pe.wait_ge(moved, t + 1)
                for f in range(PAIRS):
                    last = nc.tensor.matmul(p_out[:, t * BANK:(t + 1) * BANK], heads[:, f, t * P:(t + 1) * P],
                                            w[:, f, :], start=(f == 0), stop=(f == PAIRS - 1))
                last.then_inc(out_ready, 1)

        @block.scalar
        def _(act):
            act.wait_ge(var_ready, 1)
            nc.scalar.activation(root[:, :], var[:, :], ACT.Sqrt).then_inc(root_ready, 1)

        @block.vector
        def _(dve):
            c = Chain(dve, chain)
            for t in range(NT):
                nc.vector.tensor_copy(heads[:, :, t * P:(t + 1) * P].rearrange("p c (b s) -> p b c s", b=2),
                                      o_t[:, 2 * t:2 * t + 2, :, :]).then_inc(moved, 1)
            for t in range(NT):
                dve.wait_ge(out_ready, t + 1)
                c.link(nc.vector.bn_stats(stats[:, t, :], p_out[:, t * BANK:(t + 1) * BANK]))
                c.mark(nc.vector.bn_aggr(mv[:, t, :], stats[:, t, :]))
            c.settle()
            nc.vector.tensor_scalar(var[:, :], mv[:, :, 1], 1e-6, None, ALU.add).then_inc(var_ready, 1)
            dve.wait_ge(root_ready, 1)
            c.link(nc.vector.reciprocal(var[:, :], root[:, :]))
            dve.wait_ge(ld_b, 32)
            for t in range(NT):
                c.mark(nc.vector.tensor_scalar(o[:, t, :], p_out[:, t * BANK:(t + 1) * BANK], mv[:, t, 0:1],
                                               var[:, t:t + 1], ALU.subtract, ALU.mult))
            c.settle()
            for t in range(NT):
                c.mark(nc.vector.tensor_tensor(o[:, t, :], o[:, t, :], scale[:, :], ALU.mult))
            c.settle()
            for t in range(NT):
                c.mark(nc.vector.tensor_tensor(o[:, t, :], o[:, t, :], bias[:, :], ALU.add))
            c.settle()
            for t in range(NT):
                c.mark(nc.vector.tensor_tensor(x[:, t, :], x[:, t, :], o[:, t, :], ALU.add))
            c.settle()


NH = 8
DEPTH = 3
CIRC = 4
NM = DEPTH * (NH - 1)
A_CT, A_ST, A_CP, A_SP, A_COL, A_2P, A_P, A_QW = (0, NM, 2 * NM, 3 * NM, 4 * NM, 4 * NM + 1, 4 * NM + 1 + DH,
                                                  4 * NM + 1 + 2 * DH)
NA = A_QW + CIRC


def head_attention(nc, io, k, x, xn, xt):
    norm_transpose(nc, "n4", x, xn, xt, k.ident, 1e-5)
    with Stage(nc, "ha") as st:
        h = Namespace()
        h.state = st.sb("state", [P, 2 * NH, TOK])
        h.vhat = st.sb("vhat", [P, NT, NH, DH])
        h.trig = st.sb("trig", [P, NA])
        h.rot = st.sb("rot", [P, NM, P])
        h.same = st.sb("same", [P, P])
        h.turn = st.sb("turn", [P, P])
        h.kappa = st.sb("kappa", [P, CIRC])
        h.sup = st.sb("sup", [P, CIRC])
        head_project(nc, io, k, h, xt)
        entangle(nc, k, h)
        h.pat = st.sb("pat", [P, NT, NH * NH])
        head_scores(nc, k, h)
        head_mix(nc, io, k, h, x, xn, xt)


def head_project(nc, io, k, h, xt):
    HALF_PI, TWO_PI = math.pi / 2, 2 * math.pi
    BIG = 6.28125
    with Stage(nc, "hp") as st:
        w_qk = st.sb("w_qk", [P, DC, 2 * NH, 2, DH])
        w_v = st.sb("w_v", [P, DC, D])
        b_qk = st.sb("b_qk", [P, 2 * NH])
        b_v = st.sb("b_v", [1, D])
        rows = st.sb("rows", [P, 2 * NM + DH + 2 * CIRC])
        phase = st.sb("phase", [P, 1])
        shift = st.sb("shift", [P, 1])
        swap = st.sb("swap", [P, P])
        head_col = st.sb("head_col", [DH, 2 * 2 * NH - 1])
        ang, turns = st.sb("ang", [P, NA]), st.sb("turns", [P, NA])
        coef = st.sb("coef", [P, 6, NM])
        dv = st.sb("dv", [P, NM])
        small = st.sb("small", [P, 4 * CIRC])
        sq = [st.sb(f"sq{i}", [P, TOK]) for i in range(2)]
        root = st.sb("root", [2 * NH, 2, TOK])
        vsq = st.sb("vsq", [P, NT, D])
        vlen = st.sb("vlen", [P, 3, NT * NH])
        p_p, p_n, p_r = st.ps("p_p", 4), st.ps("p_n"), st.ps("p_r", 2)
        ld_w, ld_v, ld_s, made, p_ready, raw_done, sq_done, n_ready, root_done, inv_done, r_ready, scaled, ang_ready, \
            trig_done, v_done, vl_ready, vl_root, chain, gc, sup_max, sup_exp, normed = st.sems(
                "ld_w ld_v ld_s made p_ready raw_done sq_done n_ready root_done inv_done r_ready scaled ang_ready "
                "trig_done v_done vl_ready vl_root chain gc sup_max sup_exp normed")
        block = st.block()

        @block.sync
        def _(sp):
            for i in range(2):
                for c in range(DC):
                    sp.dma_start(w_qk[:, c, :, i, :], io.w_qk[:, c, :].rearrange("p (h d) -> p h d", d=DH))\
                        .then_inc(ld_w, 16)
            sp.dma_start(b_qk[:, :], io.b_qk).then_inc(ld_s, 16)
            sp.dma_start(rows[:, :], io.head_rows.partition_broadcast(P)).then_inc(ld_s, 16)
            sp.dma_start(phase[:, :], io.phase).then_inc(ld_s, 16)
            sp.dma_start(w_v[:, :, :], io.w_v).then_inc(ld_v, 16)
            sp.dma_start(b_v[:, :], io.b_v).then_inc(ld_v, 16)

        @block.gpsimd
        def _(g):
            c = Chain(g, gc)
            for m in (h.same, h.turn, swap, head_col):
                c.mark(g.memset(m[:, :], 0.0))
            c.settle()

            def diagonal(m, offset, value):
                c.link(g.affine_select(out=m[:, :], in_=m[:, :], compare_op=ALU.not_equal, fill=value,
                                       base=offset, pattern=[[-1, m.shape[1]]], channel_multiplier=1))

            for offset in (0, DH, -DH):
                diagonal(h.same, offset, 1.0)
            for offset in (DH, -DH):
                diagonal(swap, offset, 1.0)
            diagonal(h.turn, -DH, 1.0)
            diagonal(h.turn, DH, -1.0)
            c.link(g.memset(head_col[:, 2 * NH - 1:2 * NH], 1.0))
            g.sem_inc(made, 1)

        @block.tensor
        def _(pe):
            def norm_part(u):
                pe.wait_ge(sq_done, u + 1)
                ins = nc.tensor.matmul(p_n[0:2 * NH, :], head_col[:, 2 * NH - 1 - u:4 * NH - 1 - u],
                                       sq[u % 2][0:DH, :], start=(u == 0), stop=(u == 2 * NH - 1))
                ins.then_inc(n_ready, 1)

            pe.wait_ge(ld_w, 16 * 2 * DC)
            pe.wait_ge(made, 1)
            for u in range(2 * NH):
                if u >= 4:
                    pe.wait_ge(raw_done, u - 3)
                for c in range(DC):
                    last = nc.tensor.matmul(p_p[:, (u % 4) * BANK:(u % 4 + 1) * BANK],
                                            w_qk[:, c, u, :, :].rearrange("p i d -> p (i d)"), xt[:, c, :],
                                            start=(c == 0), stop=(c == DC - 1))
                last.then_inc(p_ready, 1)
                if u:
                    norm_part(u - 1)
            norm_part(2 * NH - 1)
            pe.wait_ge(ld_v, 32)
            for t in range(NT):
                pe.wait_ge(raw_done, 2 * NH - 3 + t)
                o = p_p[:, t * BANK:(t + 1) * BANK]
                for c in range(DC):
                    nc.tensor.matmul(o, xt[:, c, t * P:(t + 1) * P], w_v[:, c, :], start=(c == 0), stop=False)
                nc.tensor.matmul(o, k.ones[0:1, :], b_v[0:1, :], start=False, stop=True).then_inc(p_ready, 1)
            pe.wait_ge(inv_done, 1)
            for u in range(2 * NH):
                if u >= 2:
                    pe.wait_ge(scaled, u - 1)
                nc.tensor.matmul(p_r[:, (u % 2) * BANK:(u % 2 + 1) * BANK],
                                 k.ident[0:2 * NH, u:u + 1].to_broadcast([2 * NH, P]), root[:, 1, :],
                                 start=True, stop=True).then_inc(r_ready, 1)

        @block.scalar
        def _(act):
            act.wait_ge(ld_s, 48)
            act.wait_ge(ang_ready, 1)
            nc.scalar.activation(h.trig[:, :], ang[:, :], ACT.Sin).then_inc(trig_done, 1)
            for u in range(2 * NH):
                act.wait_ge(p_ready, u + 1)
                nc.scalar.activation(h.state[:, u, :], p_p[:, (u % 4) * BANK:(u % 4 + 1) * BANK], ACT.Identity,
                                     bias=b_qk[:, u:u + 1]).then_inc(raw_done, 1)
                act.wait_ge(raw_done, u + 1)
                if u >= 2:
                    act.wait_ge(n_ready, u - 1)
                nc.scalar.activation(sq[u % 2][:, :], h.state[:, u, :], ACT.Square).then_inc(sq_done, 1)
            for t in range(NT):
                act.wait_ge(p_ready, 2 * NH + t + 1)
                nc.scalar.activation(h.vhat[:, t, :, :].rearrange("p h d -> p (h d)"),
                                     p_p[:, t * BANK:(t + 1) * BANK], ACT.Copy).then_inc(v_done, 1)
            act.wait_ge(sup_max, 1)
            nc.scalar.activation(small[:, CIRC:2 * CIRC], rows[:, 2 * NM + DH + CIRC:], ACT.Exp,
                                 bias=small[:, 0:1]).then_inc(sup_exp, 1)
            act.wait_ge(n_ready, 2 * NH)
            nc.scalar.activation(root[:, 0, :], p_n[0:2 * NH, :], ACT.Sqrt).then_inc(root_done, 1)
            act.wait_ge(vl_ready, 1)
            nc.scalar.activation(vlen[:, 1, :], vlen[:, 0, :], ACT.Sqrt).then_inc(vl_root, 1)

        @block.vector
        def _(dve):
            c = Chain(dve, chain)
            dve.wait_ge(ld_s, 48)
            dve.wait_ge(made, 1)
            c.mark(nc.vector.memset(shift[0:DH, :], HALF_PI))
            c.mark(nc.vector.memset(shift[DH:P, :], 0.0))
            c.settle()
            th, ph = rows[:, 0:NM], rows[:, NM:2 * NM]
            fr = rows[:, 2 * NM:2 * NM + DH]
            for at, v, n, scale, add in ((A_CT, th, NM, 0.5, HALF_PI), (A_ST, th, NM, 0.5, 0.0),
                                         (A_CP, ph, NM, 1.0, HALF_PI), (A_SP, ph, NM, 1.0, 0.0),
                                         (A_2P, fr, DH, 2.0, HALF_PI), (A_P, fr, DH, 1.0, HALF_PI),
                                         (A_QW, rows[:, 2 * NM + DH:2 * NM + DH + CIRC], CIRC, 1.0, 0.0),
                                         (A_COL, phase[:, :], 1, 1.0, shift[:, 0:1])):
                c.mark(nc.vector.tensor_scalar(ang[:, at:at + n], v, scale, add, ALU.mult, ALU.add))
            c.settle()
            c.link(nc.vector.tensor_scalar(turns[:, :], ang[:, :], 1.0 / TWO_PI, ROUND, ALU.mult, ALU.add))
            c.link(nc.vector.tensor_scalar(turns[:, :], turns[:, :], -ROUND, None, ALU.add))
            c.link(nc.vector.scalar_tensor_tensor(ang[:, :], turns[:, :], -BIG, ang[:, :], ALU.mult, ALU.add))
            c.link(nc.vector.scalar_tensor_tensor(ang[:, :], turns[:, :], BIG - TWO_PI, ang[:, :], ALU.mult, ALU.add))
            nc.vector.tensor_scalar(ang[:, :], ang[:, :], 3.1415925, -3.1415925, ALU.min, ALU.max).then_inc(ang_ready, 1)
            c.link(nc.vector.tensor_reduce(small[:, 0:1], rows[:, 2 * NM + DH + CIRC:], AX.X, ALU.max, negate=True))
            dve.sem_inc(sup_max, 1)
            dve.wait_ge(trig_done, 1)
            tr = h.trig
            st_, cp, sp_ = tr[:, A_ST:A_ST + NM], tr[:, A_CP:A_CP + NM], tr[:, A_SP:A_SP + NM]
            c.mark(nc.vector.tensor_scalar(coef[:, 0, :], tr[:, A_CT:A_CT + NM], -1.0, None, ALU.add))
            c.mark(nc.vector.tensor_tensor(coef[:, 1, :], st_, cp, ALU.mult))
            c.mark(nc.vector.tensor_tensor(coef[:, 2, :], st_, sp_, ALU.mult))
            c.settle()
            c.mark(nc.vector.tensor_tensor(dv[0:DH, :], coef[0:DH, 0, :], coef[0:DH, 1, :], ALU.add))
            c.mark(nc.vector.tensor_tensor(dv[DH:P, :], coef[DH:P, 0, :], coef[DH:P, 1, :], ALU.subtract))
            c.settle()
            for m in range(NM):
                c.mark(nc.vector.tensor_scalar(h.rot[:, m, :], k.ident[:, :], dv[:, m:m + 1], None, ALU.mult))
            c.settle()
            for m in range(NM):
                c.mark(nc.vector.scalar_tensor_tensor(h.rot[:, m, :], swap[:, :], coef[:, 2, m:m + 1], h.rot[:, m, :],
                                                      ALU.mult, ALU.add))
            c.mark(nc.vector.tensor_scalar(small[:, 2 * CIRC:3 * CIRC], tr[:, A_QW:A_QW + CIRC], 0.3, 0.5, ALU.mult, ALU.add))
            c.mark(nc.vector.tensor_scalar(small[:, 3 * CIRC:4 * CIRC], tr[:, A_QW:A_QW + CIRC], -0.3, 0.5, ALU.mult, ALU.add))
            c.settle()
            c.mark(nc.vector.scalar_tensor_tensor(h.kappa[:, :], small[:, 2 * CIRC:3 * CIRC], DH**-0.5,
                                                  small[:, 3 * CIRC:4 * CIRC], ALU.mult, ALU.mult))
            dve.wait_ge(sup_exp, 1)
            c.link(nc.vector.tensor_reduce(small[:, 0:1], small[:, CIRC:2 * CIRC], AX.X, ALU.add))
            c.link(nc.vector.reciprocal(small[:, 1:2], small[:, 0:1]))
            c.mark(nc.vector.tensor_scalar(h.sup[:, :], small[:, CIRC:2 * CIRC], small[:, 1:2], None, ALU.mult))
            for t in range(NT):
                dve.wait_ge(v_done, t + 1)
                v = h.vhat[:, t, :, :].rearrange("p h d -> p (h d)")
                c.mark(nc.vector.tensor_tensor(vsq[:, t, :], v, v, ALU.mult))
            c.settle()
            nc.vector.tensor_reduce(vlen[:, 0, :], vsq[:, :, :].rearrange("p t (h d) -> p (t h) d", d=DH), AX.X,
                                    ALU.add).then_inc(vl_ready, 1)
            dve.wait_ge(root_done, 1)
            c.link(nc.vector.tensor_scalar(root[:, 0, :], root[:, 0, :], 1e-12, None, ALU.max))
            nc.vector.reciprocal(root[:, 1, :], root[:, 0, :]).then_inc(inv_done, 1)
            dve.wait_ge(vl_root, 1)
            c.link(nc.vector.tensor_scalar(vlen[:, 0, :], vlen[:, 1, :], 1e-12, None, ALU.max))
            c.link(nc.vector.reciprocal(vlen[:, 2, :], vlen[:, 0, :]))
            vh = h.vhat[:, :, :, :].rearrange("p t h d -> p (t h) d")
            c.mark(nc.vector.tensor_tensor(vh, vh, vlen[:, 2, :].unsqueeze(2).to_broadcast([P, NT * NH, DH]), ALU.mult))
            for u in range(2 * NH):
                dve.wait_ge(r_ready, u + 1)
                nc.vector.scalar_tensor_tensor(h.state[:, u, :], h.state[:, u, :], h.trig[:, A_COL:A_COL + 1],
                                               p_r[:, (u % 2) * BANK:(u % 2 + 1) * BANK], ALU.mult,
                                               ALU.mult).then_inc(scaled, 1)
            dve.wait_ge(scaled, 2 * NH)
            c.settle()


def entangle(nc, k, h):
    with Stage(nc, "he") as st:
        sq = [st.sb(f"sq{i}", [P, TOK]) for i in range(2)]
        ctrl = [st.sb(f"ctrl{i}", [P, TOK]) for i in range(2)]
        part = [st.sb(f"part{i}", [P, TOK]) for i in range(2)]
        p_c, p_d = st.ps("p_c", 2), st.ps("p_d", 2)
        sq_done, c_ready, d_ready, ctrl_done, part_done, new_done = st.sems(
            "sq_done c_ready d_ready ctrl_done part_done new_done")
        block = st.block()
        units = [(g, i, s * NH + i) for g in range(DEPTH) for i in range(NH - 1) for s in range(2)]

        @block.scalar
        def _(act):
            def square(n):
                u = units[n][2]
                if n >= 2:
                    act.wait_ge(c_ready, n - 1)
                if n >= 2 * (NH - 1):
                    act.wait_ge(new_done, n - 2 * (NH - 1) + 1)
                nc.scalar.activation(sq[n % 2][:, :], h.state[:, u, :], ACT.Square).then_inc(sq_done, 1)

            square(0)
            for n in range(len(units)):
                if n + 1 < len(units):
                    square(n + 1)
                act.wait_ge(c_ready, n + 1)
                if n >= 2:
                    act.wait_ge(part_done, n - 1)
                nc.scalar.activation(ctrl[n % 2][:, :], p_c[:, (n % 2) * BANK:(n % 2 + 1) * BANK],
                                     ACT.Copy).then_inc(ctrl_done, 1)

        @block.tensor
        def _(pe):
            for n, (g, i, u) in enumerate(units):
                o = slice((n % 2) * BANK, (n % 2 + 1) * BANK)
                pe.wait_ge(sq_done, n + 1)
                if n >= 2:
                    pe.wait_ge(part_done, n - 1)
                nc.tensor.matmul(p_c[:, o], h.same[:, :], sq[n % 2][:, :], start=True, stop=True).then_inc(c_ready, 1)
                if i == NH - 2:
                    if g:
                        pass
                elif g:
                    pe.wait_ge(new_done, n - 2 * (NH - 1) + 3)
                nc.tensor.matmul(p_d[:, o], h.rot[:, g * (NH - 1) + i, :], h.state[:, u + 1, :], start=True,
                                 stop=True).then_inc(d_ready, 1)

        @block.vector
        def _(dve):
            for n, (g, i, u) in enumerate(units):
                o = slice((n % 2) * BANK, (n % 2 + 1) * BANK)
                dve.wait_ge(ctrl_done, n + 1)
                dve.wait_ge(d_ready, n + 1)
                if n >= 2:
                    dve.wait_ge(new_done, n - 1)
                nc.vector.tensor_tensor(part[n % 2][:, :], ctrl[n % 2][:, :], p_d[:, o], ALU.mult).then_inc(part_done, 1)
                dve.wait_ge(part_done, n + 1)
                nc.vector.tensor_tensor(h.state[:, u, :], part[n % 2][:, :], h.state[:, u + 1, :],
                                        ALU.add).then_inc(new_done, 1)
            dve.wait_ge(new_done, len(units))


def head_scores(nc, k, h):
    with Stage(nc, "hs") as st:
        turned = st.sb("turned", [P, NH, TOK])
        prod = [st.sb(f"prod{i}", [P, NH, TOK]) for i in range(3)]
        pair_col = st.sb("pair_col", [P, 2 * NH * NH - 1])
        mag = st.sb("mag", [NH * NH, 2, TOK])
        p_k, p_re, p_im, p_t = st.ps("p_k", 2), st.ps("p_re"), st.ps("p_im"), st.ps("p_t")
        made, t_ready, turned_done, prod_done, prod_pool, summed, sq_done, mag_done, pt_ready, gc, summed_pool = st.sems(
            "made t_ready turned_done prod_done prod_pool summed sq_done mag_done pt_ready gc summed_pool")
        block = st.block()
        items = [(i, s) for s in range(2) for i in range(NH)]
        on_pool = [n for n in range(len(items)) if n % 3 == 2]
        on_dve = [n for n in range(len(items)) if n % 3 != 2]

        def product(eng, n, buf):
            i, s = items[n]
            other = turned[:, :, :] if s else h.state[:, NH:, :]
            return eng.tensor_tensor(buf[:, :, :], other, h.state[:, i:i + 1, :].to_broadcast([P, NH, TOK]), ALU.mult)

        @block.gpsimd
        def _(g):
            g.memset(pair_col[:, :], 0.0).then_inc(gc, 1)
            g.wait_ge(gc, 1)
            g.memset(pair_col[:, NH * NH - 1:NH * NH], 1.0).then_inc(made, 1)
            g.wait_ge(turned_done, NH)
            for m, n in enumerate(on_pool):
                if m:
                    g.wait_ge(summed_pool, m)
                product(g, n, prod[2]).then_inc(prod_pool, 1)

        @block.vector
        def _(dve):
            for m, n in enumerate(on_dve):
                if items[n][1]:
                    dve.wait_ge(turned_done, NH)
                if m >= 2:
                    dve.wait_ge(summed, m - 1)
                product(nc.vector, n, prod[m % 2]).then_inc(prod_done, 1)
            dve.wait_ge(sq_done, 2)
            nc.vector.tensor_tensor(mag[:, 0, :], mag[:, 0, :], mag[:, 1, :], ALU.add).then_inc(mag_done, 1)
            dve.wait_ge(pt_ready, 1)
            nc.vector.tensor_copy(h.pat[:, :, :], p_t[:, 0:NT * NH * NH].rearrange("p (t n) -> p t n", t=NT))\
                .then_inc(mag_done, 1)
            dve.wait_ge(mag_done, 2)

        @block.scalar
        def _(act):
            for j in range(NH):
                act.wait_ge(t_ready, j + 1)
                nc.scalar.activation(turned[:, j, :], p_k[:, (j % 2) * BANK:(j % 2 + 1) * BANK],
                                     ACT.Copy).then_inc(turned_done, 1)
            act.wait_ge(summed, len(on_dve))
            act.wait_ge(summed_pool, len(on_pool))
            nc.scalar.activation(mag[:, 0, :], p_re[0:NH * NH, :], ACT.Square).then_inc(sq_done, 1)
            nc.scalar.activation(mag[:, 1, :], p_im[0:NH * NH, :], ACT.Square).then_inc(sq_done, 1)

        @block.tensor
        def _(pe):
            for j in range(NH):
                if j >= 2:
                    pe.wait_ge(turned_done, j - 1)
                nc.tensor.matmul(p_k[:, (j % 2) * BANK:(j % 2 + 1) * BANK], h.turn[:, :], h.state[:, NH + j, :],
                                 start=True, stop=True).then_inc(t_ready, 1)
            pe.wait_ge(made, 1)
            for n, (i, s) in enumerate(items):
                pool = n in on_pool
                m = (on_pool if pool else on_dve).index(n)
                pe.wait_ge(prod_pool if pool else prod_done, m + 1)
                buf = prod[2] if pool else prod[m % 2]
                bank = p_im if s else p_re
                for j in range(NH):
                    r = i * NH + j
                    last = nc.tensor.matmul(bank[0:NH * NH, :], pair_col[:, NH * NH - 1 - r:2 * NH * NH - 1 - r],
                                            buf[:, j, :], start=(i == 0 and j == 0), stop=(i == NH - 1 and j == NH - 1))
                last.then_inc(summed_pool if pool else summed, 1)
            pe.wait_ge(mag_done, 1)
            for t in range(NT):
                last = nc.tensor.transpose(p_t[:, t * NH * NH:(t + 1) * NH * NH], mag[:, 0, t * P:(t + 1) * P],
                                           k.ident[0:NH * NH, 0:NH * NH])
            last.then_inc(pt_ready, 1)


def head_mix(nc, io, k, h, x, xn, xt):
    with Stage(nc, "hm") as st:
        w_o = st.sb("w_o", [P, DC, D])
        b_o = st.sb("b_o", [1, D])
        top = st.sb("top", [P, NT * NH])
        diff = st.sb("diff", [P, NT * NH, NH])
        wgt = st.sb("wgt", [P, CIRC, NT, NH, NH])
        tot = st.sb("tot", [P, 2, CIRC * NT * NH])
        tiny = st.sb("tiny", [P, CIRC])
        vsum, vsign, vsq, face = [st.sb(n, [P, NT, DH]) for n in "vsum vsign vsq face".split()]
        prod = [st.sb(f"prod{i}", [P, NH, NH, DH]) for i in range(3)]
        size, sign, clip, none = [[st.sb(f"{n}{i}", [P, D]) for i in range(2)] for n in "size sign clip none".split()]
        acc, acc_none = st.sb("acc", [P, NT, D]), st.sb("acc_none", [P, NT, D])
        p_w, p_t, p_out = st.ps("p_w", 2), st.ps("p_t", 4), st.ps("p_out", 2)
        ld_w, exp_done, w_ready, root_done, v_ready, signed, prod_done, prod_pool, mixed, sized, clipped, noned, \
            added, y_ready, yt_ready, yt_copied, out_ready, chain, diffed, gc, out_done = st.sems(
                "ld_w exp_done w_ready root_done v_ready signed prod_done prod_pool mixed sized clipped noned "
                "added y_ready yt_ready yt_copied out_ready chain diffed gc out_done")
        block = st.block()
        units = [(t, c) for t in range(NT) for c in range(CIRC)]
        on_pool = [n for n in range(len(units)) if n % 3 == 2]
        on_dve = [n for n in range(len(units)) if n % 3 != 2]

        @block.sync
        def _(sp):
            sp.dma_start(w_o[:, :, :], io.w_o).then_inc(ld_w, 16)
            sp.dma_start(b_o[:, :], io.b_o).then_inc(ld_w, 16)

        def product(eng, n, buf):
            t, c = units[n]
            return eng.tensor_tensor(buf[:, :, :, :],
                                     wgt[:, c, t, :, :].unsqueeze(3).to_broadcast([P, NH, NH, DH]),
                                     h.vhat[:, t, :, :].unsqueeze(1).to_broadcast([P, NH, NH, DH]), ALU.mult)

        @block.vector
        def _(dve):
            c = Chain(dve, chain)
            pat = h.pat[:, :, :].rearrange("p t (i j) -> p (t i) j", j=NH)
            c.link(nc.vector.tensor_reduce(top[:, :], pat, AX.X, ALU.max))
            nc.vector.tensor_tensor(diff[:, :, :], pat, top[:, :].unsqueeze(2).to_broadcast([P, NT * NH, NH]),
                                    ALU.subtract).then_inc(diffed, 1)
            c.mark(nc.vector.tensor_scalar(tiny[:, :], h.sup[:, :], 1e-6, None, ALU.mult))
            for t in range(NT):
                c.mark(nc.vector.tensor_reduce(vsum[:, t, :], h.vhat[:, t, :, :].rearrange("p h d -> p d h"), AX.X,
                                               ALU.add))
            c.settle()
            dve.sem_inc(v_ready, 1)
            dve.wait_ge(exp_done, CIRC)
            wf = wgt[:, :, :, :, :].rearrange("p c t i j -> p (c t i) j")
            c.link(nc.vector.tensor_reduce(tot[:, 0, :], wf, AX.X, ALU.add))
            c.link(nc.vector.reciprocal(tot[:, 1, :], tot[:, 0, :]))
            c.link(nc.vector.tensor_tensor(wf, wf, tot[:, 1, :].unsqueeze(2).to_broadcast([P, CIRC * NT * NH, NH]),
                                           ALU.mult))
            nc.vector.tensor_scalar(wf, wf, 1e-12, None, ALU.add).then_inc(w_ready, 1)
            dve.wait_ge(signed, 2)
            c.link(nc.vector.tensor_tensor(vsum[:, :, :], vsign[:, :, :],
                                           h.trig[:, A_2P:A_2P + DH].unsqueeze(1).to_broadcast([P, NT, DH]), ALU.mult))
            c.link(nc.vector.tensor_scalar(vsq[:, :, :], vsq[:, :, :], -1.0, 1.0, ALU.mult, ALU.add))
            c.link(nc.vector.tensor_tensor(vsq[:, :, :], vsq[:, :, :],
                                           h.trig[:, A_P:A_P + DH].unsqueeze(1).to_broadcast([P, NT, DH]), ALU.mult))
            c.link(nc.vector.tensor_tensor(face[:, :, :], vsum[:, :, :], vsq[:, :, :], ALU.add))
            dve.wait_ge(root_done, 1)

            def finish(n):
                t, ci = units[n]
                dve.wait_ge(sized, 2 * n + 2)
                if n >= 2:
                    dve.wait_ge(added, 2 * n - 2)
                nc.vector.tensor_scalar(none[n % 2][:, :], size[n % 2][:, :], 0.0, tiny[:, ci:ci + 1], ALU.is_equal,
                                        ALU.mult).then_inc(noned, 1)
                c.link(nc.vector.tensor_scalar(clip[n % 2][:, :], size[n % 2][:, :], 1e-6, 1.0, ALU.max, ALU.min))
                nc.vector.scalar_tensor_tensor(clip[n % 2][:, :], clip[n % 2][:, :], h.sup[:, ci:ci + 1],
                                               sign[n % 2][:, :], ALU.mult, ALU.mult).then_inc(clipped, 1)
                if ci == CIRC - 1:
                    dve.wait_ge(added, 2 * n + 2)
                    a = acc[:, t, :].rearrange("p (i d) -> p i d", d=DH)
                    c.link(nc.vector.tensor_tensor(a, a, face[:, t:t + 1, :].to_broadcast([P, NH, DH]), ALU.mult))
                    nc.vector.tensor_tensor(acc[:, t, :], acc[:, t, :], acc_none[:, t, :], ALU.add).then_inc(y_ready, 1)

            m = 0
            for n in range(len(units) + 2):
                if n in on_dve:
                    if m >= 2:
                        dve.wait_ge(mixed, on_dve[m - 2] + 1)
                    product(nc.vector, n, prod[m % 2]).then_inc(prod_done, 1)
                    m += 1
                if n >= 2:
                    finish(n - 2)
            for t in range(NT):
                dve.wait_ge(out_ready, t + 1)
                nc.vector.tensor_tensor(x[:, t, :], x[:, t, :], p_out[:, (t % 2) * BANK:(t % 2 + 1) * BANK],
                                        ALU.add).then_inc(out_done, 1)
            dve.wait_ge(out_done, NT)

        @block.gpsimd
        def _(g):
            g.memset(acc[:, :, :], 0.0).then_inc(gc, 1)
            g.memset(acc_none[:, :, :], 0.0).then_inc(gc, 1)
            g.wait_ge(gc, 2)
            g.wait_ge(root_done, 1)
            m = 0
            for n in range(len(units) + 2):
                if n in on_pool:
                    if m:
                        g.wait_ge(mixed, on_pool[m - 1] + 1)
                    product(g, n, prod[2]).then_inc(prod_pool, 1)
                    m += 1
                if n >= 2:
                    t, b = units[n - 2][0], (n - 2) % 2
                    if n >= 3:
                        g.wait_ge(added, 2 * (n - 2))
                    g.wait_ge(noned, n - 1)
                    g.tensor_tensor(acc_none[:, t, :], acc_none[:, t, :], none[b][:, :], ALU.add).then_inc(added, 1)
                    g.wait_ge(clipped, n - 1)
                    g.tensor_tensor(acc[:, t, :], acc[:, t, :], clip[b][:, :], ALU.add).then_inc(added, 1)

        @block.scalar
        def _(act):
            act.wait_ge(diffed, 1)
            for c in range(CIRC):
                nc.scalar.activation(wgt[:, c, :, :, :].rearrange("p t i j -> p (t i) j"), diff[:, :, :], ACT.Exp,
                                     scale=h.kappa[:, c:c + 1]).then_inc(exp_done, 1)
            act.wait_ge(w_ready, 1)
            wf = wgt[:, :, :, :, :].rearrange("p c t i j -> p (c t i j)")
            nc.scalar.activation(wf, wf, ACT.Sqrt).then_inc(root_done, 1)
            act.wait_ge(v_ready, 1)
            nc.scalar.activation(vsign[:, :, :], vsum[:, :, :], ACT.Sign).then_inc(signed, 1)
            act.wait_ge(signed, 1)
            nc.scalar.activation(vsq[:, :, :], vsign[:, :, :], ACT.Square).then_inc(signed, 1)
            for n in range(len(units)):
                act.wait_ge(mixed, n + 1)
                if n >= 2:
                    act.wait_ge(clipped, n - 1)
                o = p_w[:, (n % 2) * BANK:(n % 2 + 1) * BANK]
                nc.scalar.activation(size[n % 2][:, :], o, ACT.Abs).then_inc(sized, 1)
                nc.scalar.activation(sign[n % 2][:, :], o, ACT.Sign).then_inc(sized, 1)
            act.wait_ge(yt_ready, 1)
            for c in range(DC):
                nc.scalar.activation(xt[:, c, :], p_t[:, c * BANK:(c + 1) * BANK], ACT.Copy).then_inc(yt_copied, 1)

        @block.tensor
        def _(pe):
            for n in range(len(units)):
                pool = n in on_pool
                m = (on_pool if pool else on_dve).index(n)
                pe.wait_ge(prod_pool if pool else prod_done, m + 1)
                if n >= 2:
                    pe.wait_ge(sized, 2 * n - 2)
                buf = prod[2] if pool else prod[m % 2]
                for j in range(NH):
                    last = nc.tensor.matmul(p_w[:, (n % 2) * BANK:(n % 2 + 1) * BANK], k.ident[:, :], buf[:, :, j, :],
                                            start=(j == 0), stop=(j == NH - 1))
                last.then_inc(mixed, 1)
            for t in range(NT):
                pe.wait_ge(y_ready, t + 1)
                for c in range(DC):
                    last = nc.tensor.transpose(p_t[:, c * BANK + t * P:c * BANK + (t + 1) * P],
                                               acc[:, t, c * P:(c + 1) * P], k.ident[:, :])
            last.then_inc(yt_ready, 1)
            pe.wait_ge(ld_w, 32)
            pe.wait_ge(yt_copied, DC)
            for t in range(NT):
                if t >= 2:
                    pe.wait_ge(out_done, t - 1)
                o = p_out[:, (t % 2) * BANK:(t % 2 + 1) * BANK]
                for c in range(DC):
                    nc.tensor.matmul(o, xt[:, c, t * P:(t + 1) * P], w_o[:, c, :], start=(c == 0), stop=False)
                nc.tensor.matmul(o, k.ones[0:1, :], b_o[0:1, :], start=False, stop=True).then_inc(out_ready, 1)


NE = 8
CAP = math.ceil(TOK / NE * 1.25)
HW = 2 * D
WC = HW // P


def experts(nc, io, k, x, xn, xt):
    norm_transpose(nc, "n5", x, xn, xt, k.ident, 1e-5)
    with Stage(nc, "ex") as st:
        RING = 3
        w_g = st.sb("w_g", [P, DC, HW])
        w_r = st.sb("w_r", [P, DC, NE])
        w_d = [st.sb(f"w_d{i}", [P, WC, D]) for i in range(RING)]
        hid = st.sb("hid", [P, NT, HW])
        sel = st.sb("sel", [P, NT, NE, CAP])
        share = st.sb("share", [P, NT, NE, CAP])
        got = st.sb("got", [P, WC, NE * CAP])
        spread = st.sb("spread", [CAP, NE, TOK])
        y = st.sb("y", [CAP, NE, D])
        upto, slots = st.sb("upto", [P, P]), st.sb("slots", [P, CAP])
        before = st.sb("before", [P, NE, NE])
        gate, mask, rank, pos, comb = [st.sb(n, [P, NT, NE]) for n in "gate mask rank pos comb".split()]
        more, same = st.sb("more", [P, NT, NE, NE]), st.sb("same", [P, NT, NE, NE])
        one = st.sb("one", [P, 3, NT])
        p_a, p_b, p_o = st.ps("p_a"), st.ps("p_b", 3), st.ps("p_o", NT)
        ld_g, ld_r, made, gc, l_ready, max_done, exp_done, mask_done, pos_ready, chain, sel_done, h_ready, h_done, \
            g_ready, got_done, s_ready, spread_done, y_ready, y_done, out_ready, added = st.sems(
                "ld_g ld_r made gc l_ready max_done exp_done mask_done pos_ready chain sel_done h_ready h_done "
                "g_ready got_done s_ready spread_done y_ready y_done out_ready added")
        ld_d = [st.sem(f"ld_d{i}") for i in range(RING)]
        block = st.block()
        HALF = NE * CAP // 2
        b3 = lambda n: p_b[:, (n % 3) * BANK:(n % 3 + 1) * BANK]

        @block.sync
        def _(sp):
            sp.dma_start(w_r[:, :, :], io.w_r).then_inc(ld_r, 16)
            sp.dma_start(w_g[:, :, :], io.w_g).then_inc(ld_g, 16)
            for e in range(NE):
                if e >= RING:
                    sp.wait_ge(y_ready, e - RING + 1)
                sp.dma_start(w_d[e % RING][:, :, :], io.w_d[:, e, :, :]).then_inc(ld_d[e % RING], 16)

        @block.gpsimd
        def _(g):
            c = Chain(g, gc)
            c.mark(g.memset(upto[:, :], 1.0))
            c.mark(g.memset(before[:, :, :], 1.0))
            c.mark(g.iota(slots[:, :], [[1, CAP]], base=0, channel_multiplier=0, allow_small_or_imprecise_dtypes=True))
            c.settle()
            c.mark(g.affine_select(out=upto[:, :], in_=upto[:, :], compare_op=ALU.is_ge, fill=0.0, base=0,
                                   pattern=[[1, P]], channel_multiplier=-1))
            c.link(g.affine_select(out=before[:, :, :], in_=before[:, :, :], compare_op=ALU.is_gt, fill=0.0, base=0,
                                   pattern=[[1, NE], [-1, NE]], channel_multiplier=0))
            g.sem_inc(made, 1)

        @block.tensor
        def _(pe):
            pe.wait_ge(ld_r, 16)
            for t in range(NT):
                for c in range(DC):
                    last = nc.tensor.matmul(p_a[:, t * NE:(t + 1) * NE], xt[:, c, t * P:(t + 1) * P], w_r[:, c, :],
                                            start=(c == 0), stop=(c == DC - 1))
            last.then_inc(l_ready, 1)
            pe.wait_ge(ld_g, 16)
            for t in range(NT):
                for i in range(2):
                    n = 2 * t + i
                    if n >= 3:
                        pe.wait_ge(h_done, n - 2)
                    for c in range(DC):
                        last = nc.tensor.matmul(b3(n), xt[:, c, t * P:(t + 1) * P],
                                                w_g[:, c, i * BANK:(i + 1) * BANK], start=(c == 0), stop=(c == DC - 1))
                    last.then_inc(h_ready, 1)
            pe.wait_ge(made, 1)
            pe.wait_ge(mask_done, 1)
            nc.tensor.matmul(p_a[:, 0:NT * NE], upto[:, :], mask[:, :, :].rearrange("p t e -> p (t e)"), start=True,
                             stop=False)
            for t in range(NT - 1):
                rest = NT - 1 - t
                last = nc.tensor.matmul(p_a[:, (t + 1) * NE:NT * NE], k.ones[:, :],
                                        mask[:, t:t + 1, :].to_broadcast([P, rest, NE]), start=False, stop=(rest == 1))
            last.then_inc(pos_ready, 1)
            pe.wait_ge(sel_done, 1)
            for n in range(2 * WC):
                c, i = n // 2, n % 2
                pe.wait_ge(h_done, 2 * NT)
                if n >= 3:
                    pe.wait_ge(got_done, n - 2)
                for t in range(NT):
                    last = nc.tensor.matmul(b3(n)[:, 0:HALF], hid[:, t, c * P:(c + 1) * P],
                                            sel[:, t, :, :].rearrange("p e s -> p (e s)")[:, i * HALF:(i + 1) * HALF],
                                            start=(t == 0), stop=(t == NT - 1))
                last.then_inc(g_ready, 1)
            pe.wait_ge(sel_done, 2)
            for e in range(NE):
                pe.wait_ge(got_done, 2 * WC - 2 + min(e, 2))
                if e >= 3:
                    pe.wait_ge(spread_done, e - 2)
                for t in range(NT):
                    last = nc.tensor.transpose(b3(2 * WC + e)[0:CAP, t * P:(t + 1) * P], share[:, t, e, :], k.ident[:, :])
                last.then_inc(s_ready, 1)
            for e in range(NE + 1):
                if e < NE:
                    n = 2 * WC + NE + e
                    pe.wait_ge(ld_d[e % RING], 16 * (e // RING + 1))
                    if e < 3:
                        pe.wait_ge(spread_done, NE - 2 + e)
                    else:
                        pe.wait_ge(y_done, e - 2)
                    for c in range(WC):
                        last = nc.tensor.matmul(b3(n)[0:CAP, :], got[:, c, e * CAP:(e + 1) * CAP],
                                                w_d[e % RING][:, c, :], start=(c == 0), stop=(c == WC - 1))
                    last.then_inc(y_ready, 1)
                if e:
                    pe.wait_ge(y_done, e)
                    for t in range(NT):
                        ins = nc.tensor.matmul(p_o[:, t * BANK:(t + 1) * BANK], spread[:, e - 1, t * P:(t + 1) * P],
                                               y[:, e - 1, :], start=(e == 1), stop=(e == NE))
                        if e == NE:
                            ins.then_inc(out_ready, 1)

        @block.scalar
        def _(act):
            act.wait_ge(max_done, 1)
            nc.scalar.activation(gate[:, :, :], gate[:, :, :], ACT.Exp).then_inc(exp_done, 1)
            for n in range(2 * NT):
                act.wait_ge(h_ready, n + 1)
                nc.scalar.activation(hid[:, n // 2, (n % 2) * BANK:(n % 2 + 1) * BANK], b3(n), ACT.Silu).then_inc(h_done, 1)
            for n in range(2 * WC):
                act.wait_ge(g_ready, n + 1)
                nc.scalar.activation(got[:, n // 2, (n % 2) * HALF:(n % 2 + 1) * HALF], b3(n)[:, 0:HALF],
                                     ACT.Copy).then_inc(got_done, 1)
            for e in range(NE):
                act.wait_ge(y_ready, e + 1)
                nc.scalar.activation(y[:, e, :], b3(2 * WC + NE + e)[0:CAP, :], ACT.Copy).then_inc(y_done, 1)

        @block.vector
        def _(dve):
            c = Chain(dve, chain)

            def over(v):
                return v.unsqueeze(2).to_broadcast([P, NT, NE])

            dve.wait_ge(l_ready, 1)
            logit = p_a[:, 0:NT * NE].rearrange("p (t e) -> p t e", e=NE)
            c.link(nc.vector.tensor_reduce(one[:, 0, :], logit, AX.X, ALU.max))
            nc.vector.tensor_tensor(gate[:, :, :], logit, over(one[:, 0, :]), ALU.subtract).then_inc(max_done, 1)
            dve.wait_ge(exp_done, 1)
            c.link(nc.vector.tensor_reduce(one[:, 1, :], gate[:, :, :], AX.X, ALU.add))
            c.link(nc.vector.reciprocal(one[:, 2, :], one[:, 1, :]))
            c.link(nc.vector.tensor_tensor(gate[:, :, :], gate[:, :, :], over(one[:, 2, :]), ALU.mult))
            other = gate[:, :, :].unsqueeze(2).to_broadcast([P, NT, NE, NE])
            own = gate[:, :, :].unsqueeze(3).to_broadcast([P, NT, NE, NE])
            c.mark(nc.vector.tensor_tensor(more[:, :, :, :], other, own, ALU.is_gt))
            c.link(nc.vector.tensor_tensor(same[:, :, :, :], other, own, ALU.is_equal))
            dve.wait_ge(made, 1)
            c.link(nc.vector.tensor_tensor(same[:, :, :, :], same[:, :, :, :],
                                           before[:, :, :].unsqueeze(1).to_broadcast([P, NT, NE, NE]), ALU.mult))
            c.link(nc.vector.tensor_tensor(more[:, :, :, :], more[:, :, :, :], same[:, :, :, :], ALU.add))
            c.link(nc.vector.tensor_reduce(rank[:, :, :], more[:, :, :, :], AX.X, ALU.add))
            nc.vector.tensor_scalar(mask[:, :, :], rank[:, :, :], 2.0, None, ALU.is_lt).then_inc(mask_done, 1)
            dve.wait_ge(pos_ready, 1)
            dve.wait_ge(mask_done, 1)
            c.link(nc.vector.tensor_copy(pos[:, :, :], logit))
            c.link(nc.vector.scalar_tensor_tensor(rank[:, :, :], pos[:, :, :], float(CAP), mask[:, :, :], ALU.is_le,
                                                  ALU.mult))
            c.mark(nc.vector.tensor_tensor(comb[:, :, :], gate[:, :, :], rank[:, :, :], ALU.mult))
            c.link(nc.vector.tensor_tensor(pos[:, :, :], pos[:, :, :], rank[:, :, :], ALU.mult))
            c.mark(nc.vector.tensor_scalar(pos[:, :, :], pos[:, :, :], -1.0, None, ALU.add))
            c.link(nc.vector.tensor_reduce(one[:, 0, :], comb[:, :, :], AX.X, ALU.add))
            c.link(nc.vector.tensor_scalar(one[:, 1, :], one[:, 0, :], 1e-6, None, ALU.add))
            c.link(nc.vector.reciprocal(one[:, 2, :], one[:, 1, :]))
            c.link(nc.vector.tensor_tensor(comb[:, :, :], comb[:, :, :], over(one[:, 2, :]), ALU.mult))
            te = "p t e -> p (t e)"
            full = [P, NT * NE, CAP]
            nc.vector.tensor_tensor(sel[:, :, :, :].rearrange("p t e s -> p (t e) s"),
                                    slots[:, :].unsqueeze(1).to_broadcast(full),
                                    pos[:, :, :].rearrange(te).unsqueeze(2).to_broadcast(full),
                                    ALU.is_equal).then_inc(sel_done, 1)
            dve.wait_ge(sel_done, 1)
            nc.vector.tensor_tensor(share[:, :, :, :].rearrange("p t e s -> p (t e) s"),
                                    sel[:, :, :, :].rearrange("p t e s -> p (t e) s"),
                                    comb[:, :, :].rearrange(te).unsqueeze(2).to_broadcast(full),
                                    ALU.mult).then_inc(sel_done, 1)
            for e in range(NE):
                dve.wait_ge(s_ready, e + 1)
                nc.vector.tensor_copy(spread[:, e, :], b3(2 * WC + e)[0:CAP, :]).then_inc(spread_done, 1)
            for t in range(NT):
                dve.wait_ge(out_ready, t + 1)
                nc.vector.tensor_tensor(x[:, t, :], x[:, t, :], p_o[:, t * BANK:(t + 1) * BANK],
                                        ALU.add).then_inc(added, 1)
            dve.wait_ge(added, NT)


STAGES = [depool_stream, mamba, bitnet, cross_attention, head_attention, experts]


class Namespace:
    pass


def build(nc, io):
    with ExitStack() as stack:
        def sb(name, shape, dt=f32):
            return stack.enter_context(nc.sbuf_tensor(name, shape, dt))

        x = sb("x", [P, NT, D])
        work = sb("work", [P, NT * D + DC * TOK])
        xn = work[:, 0:NT * D].rearrange("p (t d) -> p t d", d=D)
        xt = work[:, NT * D:].rearrange("p (c t) -> p c t", t=TOK)
        stored = nc.alloc_semaphore(name="stored")
        k = Namespace()
        k.ident, k.ones = sb("ident", [P, P]), sb("ones", [P, P])
        k.ident_h = sb("ident_h", [P, P], bf16)
        k.cols = sb("cols", [P, io.cols.shape[1]])
        with Stage(nc, "start") as st:
            loaded, made = st.sems("loaded made")
            block = st.block()

            @block.sync
            def _(sp):
                sp.dma_start(x[:, :, :], io.x).then_inc(loaded, 16)
                sp.dma_start(k.cols[:, :], io.cols).then_inc(loaded, 16)
                sp.wait_ge(loaded, 32)

            @block.gpsimd
            def _(g):
                g.memset(k.ones[:, :], 1.0).then_inc(made, 1)
                g.memset(k.ident[:, :], 0.0).then_inc(made, 1)
                g.wait_ge(made, 2)
                g.affine_select(out=k.ident[:, :], in_=k.ident[:, :], compare_op=ALU.not_equal, fill=1.0,
                                base=0, pattern=[[-1, P]], channel_multiplier=1).then_inc(made, 1)
                g.wait_ge(made, 3)
                g.tensor_copy(k.ident_h[:, :], k.ident[:, :]).then_inc(made, 1)
                g.wait_ge(made, 4)
        for stage in STAGES:
            stage(nc, io, k, x, xn, xt, *([work[:, :]] if stage.__name__ == "cross_attention" else []))
        with Stage(nc, "end") as st:
            block = st.block()

            @block.sync
            def _(sp):
                sp.dma_start(io.out, x[:, :, :]).then_inc(stored, 16)
                sp.wait_ge(stored, 16)


def more_data(a, data, rows, columns):
    data["in_proj"] = rows(a["L0_attn_in_proj_w"].T)
    data["x_proj"] = rows(a["L0_attn_x_proj_w"].T)
    data["dt_proj"] = a["L0_attn_dt_proj_w"].T
    data["a_log"] = rows(a["L0_attn_A_log"])
    data["out_proj"] = rows(a["L0_attn_out_proj_w"].T)
    data["w1"] = rows(a["L0_ffn_W1"].T)
    data["w2"] = rows(a["L0_ffn_W2"].T)
    data["b1"] = a["L0_ffn_b1"]
    data["b2"] = a["L0_ffn_b2"]
    data["w_q"] = rows(a["L1_xattn_Wq"])
    data["w_kv"] = rows(a["L1_xattn_Wkv"])
    data["null_k"] = np.tile(a["L1_xattn_null_kv"][0], 2)[:, None]
    data["null_v"] = np.tile(a["L1_xattn_null_kv"][1], P // DH * GP)[None]
    whole = np.zeros((B, JT * P, CW), np.float32)
    whole[:, :CTX] = a["ctx_2048"]
    data["ctx_t"] = whole.reshape(B, JT, P, CC, P).transpose(0, 1, 4, 3, 2).reshape(B, JT, P, CC * P)
    data["w_out"] = rows(a["L1_xattn_Wout"])
    data["ln_scale"] = a["L1_xattn_ln_scale"]
    data["ln_bias"] = a["L1_xattn_ln_bias"]
    wqkv, bqkv = a["L1_attn_W_qkv"], a["L1_attn_b_qkv"]
    data["w_qk"] = rows(wqkv[:2 * D].T)
    data["w_v"] = rows(wqkv[2 * D:].T)
    data["b_qk"] = np.tile(bqkv[:2 * D].reshape(2 * NH, DH).T, (2, 1))
    data["b_v"] = bqkv[2 * D:][None]
    feature = np.arange(DH)
    phase = a["L1_attn_photonic_phases"][feature % 16, feature]
    data["phase"] = np.tile(phase, 2)[:, None]
    data["head_rows"] = np.concatenate([
        a["L1_attn_entanglement_gates"][:, :NH - 1, :2].transpose(2, 0, 1).reshape(-1), phase,
        a["L1_attn_quantum_weights"][:, 0, 0], a["L1_attn_superposition_logits"]])
    data["w_o"] = rows(a["L1_attn_W_out"].T)
    data["b_o"] = a["L1_attn_b_out"][None]
    data["w_r"] = rows(a["L1_ffn_w_router"].T)
    data["w_g"] = rows(a["L1_ffn_w_gate"].T)
    data["w_d"] = a["L1_ffn_w_down"].transpose(0, 2, 1).reshape(NE, WC, P, D).transpose(2, 0, 1, 3)


def kernel(**inputs):
    import concourse.bacc as bacc
    from concourse.bass_utils import run_bass_kernel_spmd

    a = {n: np.ascontiguousarray(v) for n, v in inputs.items()}

    def rows(w):
        return np.ascontiguousarray(w.reshape(-1, P, w.shape[1]).transpose(1, 0, 2))

    def columns(v):
        return v.reshape(-1, P).T

    ctx, lens = a["ctx_2048"], a["mask_BxS2_if0"]
    tiles = -(-CTX // P)
    padded = np.zeros((tiles * P, B), lens.dtype)
    padded[:CTX] = lens.T
    data = {
        "x": a["x"].reshape(NT, P, D).transpose(1, 0, 2),
        "lens": padded.reshape(tiles, P, B).transpose(1, 0, 2),
        "patches": ctx[:, :S, :].reshape(NT, P, CW).transpose(1, 0, 2),
        "w_in": rows(a["L0_xattn_W_in"].T),
        "b_in": a["L0_xattn_b_in"][None],
        "g_init": a["L0_xattn_g_init"][:D],
        "cols": np.concatenate([
            columns(a["L0_xattn_g_res"]), columns(a["L0_attn_conv_b"]), columns(a["L0_attn_D"]),
            columns(a["L0_attn_dt_proj_b"]),
            a["L0_attn_conv_w"].reshape(-1, P, 4).transpose(1, 0, 2).reshape(P, -1)], axis=1),
    }
    more_data(a, data, rows, columns)
    nc = bacc.Bacc("TRN2", target_bir_lowering=False, num_devices=1)
    io = Namespace()
    arrays = {}
    for name, v in data.items():
        v = np.ascontiguousarray(v)
        arrays[f"in_{name}"] = v
        io.__dict__[name] = nc.dram_tensor(f"in_{name}", v.shape, mybir.dt.from_np(v.dtype), kind="ExternalInput").ap()
    io.out = nc.dram_tensor("out", (P, NT, D), f32, kind="ExternalOutput").ap()
    build(nc, io)
    got = run_bass_kernel_spmd(nc, [arrays], core_ids=[0]).results[0]["out"]
    return got.transpose(1, 0, 2).reshape(B, S, D)
```

```python
import math
from contextlib import ExitStack

import numpy as np

import concourse.bass as bass
from concourse import mybir

f32 = mybir.dt.float32
f16 = mybir.dt.float16
bf16 = mybir.dt.bfloat16
i32 = mybir.dt.int32
ALU = mybir.AluOpType
ACT = mybir.ActivationFunctionType
AX = mybir.AxisListType

P = 128
B, S, D = 8, 64, 512
TOK = B * S
NT = TOK // P
DC = D // P
CTX, CW = 1601, 1024
ROUND = 1.5 * 2.0**23
BANK = 512


class Chain:

    def __init__(self, eng, sem):
        self.eng, self.sem, self.n = eng, sem, 0

    def mark(self, ins):
        ins.then_inc(self.sem, 1)
        self.n += 1

    def settle(self):
        self.eng.wait_ge(self.sem, self.n)

    def link(self, ins):
        self.mark(ins)
        self.settle()


class Stage:

    def __init__(self, nc, name):
        self.nc, self.name, self.stack, self.held = nc, name, ExitStack(), []

    def __enter__(self):
        self.stack.__enter__()
        return self

    def __exit__(self, *a):
        self.stack.__exit__(*a)
        if self.held:
            self.nc.clear_and_free_semaphores(self.held)
            self.nc.all_engine_barrier()

    def sb(self, name, shape, dt=f32):
        return self.stack.enter_context(self.nc.sbuf_tensor(f"{self.name}_{name}", shape, dt))

    def ps(self, name, banks=1, dt=f32):
        return self.stack.enter_context(self.nc.psum_tensor(f"{self.name}_{name}", [P, banks * BANK], dt))

    def sem(self, name):
        self.held.append(self.nc.alloc_semaphore(name=f"{self.name}_{name}"))
        return self.held[-1]

    def sems(self, names):
        return [self.sem(n) for n in names.split()]

    def block(self):
        return self.stack.enter_context(self.nc.Block())


def norm_transpose(nc, name, x, xn, xt, ident, eps, rms_eps=None, gain=None, transpose=True, load=None):
    with Stage(nc, name) as st:
        stats = st.sb("stats", [P, NT, 6])
        mv = st.sb("mv", [P, NT, 2])
        root = st.sb("root", [P, 2 * NT])
        rstd = st.sb("rstd", [P, 2 * NT])
        square = st.sb("square", [P, D])
        ssum = st.sb("ssum", [P, NT])
        pt = st.ps("pt", DC)
        var_ready, root_ready, xn_ready, xt_in_psum, done, chain, normed, ss_ready, sq_chain = st.sems(
            "var_ready root_ready xn_ready xt_in_psum done chain normed ss_ready sq_chain")
        block = st.block()
        if load:
            block.sync(load)

        @block.vector
        def _(dve):
            c = Chain(dve, chain)
            for t in range(NT):
                c.mark(nc.vector.bn_stats(stats[:, t, :], x[:, t, :]))
            c.settle()
            for t in range(NT):
                c.mark(nc.vector.bn_aggr(mv[:, t, :], stats[:, t, :]))
            c.settle()
            nc.vector.tensor_scalar(root[:, 0:NT], mv[:, :, 1], eps, None, ALU.add).then_inc(var_ready, 1)
            dve.wait_ge(root_ready, 1)
            c.link(nc.vector.reciprocal(rstd[:, 0:NT], root[:, NT:2 * NT]))
            for t in range(NT):
                nc.vector.tensor_scalar(xn[:, t, :], x[:, t, :], mv[:, t, 0:1], rstd[:, t:t + 1],
                                        ALU.subtract, ALU.mult).then_inc(normed if rms_eps else xn_ready, 1)
            if rms_eps:
                dve.wait_ge(ss_ready, 1)
                c.link(nc.vector.reciprocal(rstd[:, NT:2 * NT], root[:, NT:2 * NT]))
                for t in range(NT):
                    nc.vector.tensor_scalar(xn[:, t, :], xn[:, t, :], rstd[:, NT + t:NT + t + 1], None,
                                            ALU.mult).then_inc(xn_ready, 1)
            if not transpose:
                dve.wait_ge(xn_ready, NT)
                return
            dve.wait_ge(xt_in_psum, 1)
            for k in range(0, DC, 2):
                if gain is None:
                    nc.vector.tensor_copy(xt[:, k, :], pt[:, k * BANK:(k + 1) * BANK]).then_inc(done, 1)
                else:
                    nc.vector.tensor_scalar(xt[:, k, :], pt[:, k * BANK:(k + 1) * BANK], gain[:, k:k + 1],
                                            None, ALU.mult).then_inc(done, 1)
            dve.wait_ge(done, DC)

        @block.scalar
        def _(act):
            act.wait_ge(var_ready, 1)
            nc.scalar.activation(root[:, NT:2 * NT], root[:, 0:NT], ACT.Sqrt).then_inc(root_ready, 1)
            if rms_eps:
                for t in range(NT):
                    act.wait_ge(normed, t + 1)
                    if t:
                        act.wait_ge(sq_chain, t)
                    nc.scalar.activation(square[:, :], xn[:, t, :], ACT.Square,
                                         accum_out=ssum[:, t:t + 1]).then_inc(sq_chain, 1)
                act.wait_ge(sq_chain, NT)
                nc.scalar.activation(root[:, 0:NT], ssum[:, :], ACT.Copy, bias=rms_eps, scale=1.0 / D).then_inc(sq_chain, 1)
                act.wait_ge(sq_chain, NT + 1)
                nc.scalar.activation(root[:, NT:2 * NT], root[:, 0:NT], ACT.Sqrt).then_inc(ss_ready, 1)
            if not transpose:
                return
            act.wait_ge(xt_in_psum, 1)
            for k in range(1, DC, 2):
                if gain is None:
                    nc.scalar.activation(xt[:, k, :], pt[:, k * BANK:(k + 1) * BANK], ACT.Copy).then_inc(done, 1)
                else:
                    nc.scalar.activation(xt[:, k, :], pt[:, k * BANK:(k + 1) * BANK], ACT.Copy,
                                         scale=gain[:, k:k + 1]).then_inc(done, 1)

        @block.tensor
        def _(pe):
            if not transpose:
                return
            for t in range(NT):
                pe.wait_ge(xn_ready, t + 1)
                for k in range(DC):
                    last = nc.tensor.transpose(pt[:, k * BANK + t * P:k * BANK + (t + 1) * P],
                                               xn[:, t, k * P:(k + 1) * P], ident[:, :])
            last.then_inc(xt_in_psum, 1)


COLS = dict(g_res=(0, 4), conv_b=(4, 8), d_skip=(12, 8), dt_b=(20, 8), conv_w=(28, 32))


def col(cols, name, i=0, n=None):
    at, k = COLS[name]
    return cols[:, at + i:at + (k if n is None else i + n)]


def depool_stream(nc, io, k, x, xn, xt):
    EPS = 0.001
    dt = -math.log(-math.expm1(-EPS))
    decay = math.exp(-dt)
    bcoef = math.exp(-EPS)
    PT = (CTX + P - 1) // P
    with Stage(nc, "dp") as st:
        lens_i = st.sb("lens_i", [P, PT, B], i32)
        w_in = st.sb("w_in", [P, DC, D])
        b_row = st.sb("b_row", [1, D])
        ctx = st.sb("ctx", [P, NT, CW])
        g_init = st.sb("g_init", [P, D])
        ld_lens, ld_w = st.sems("ld_lens ld_w")
        ld_ctx = [st.sem(f"ld_ctx{t}") for t in range(NT)]

        def load(sp):
            sp.dma_start(lens_i[:, :, :], io.lens).then_inc(ld_lens, 16)
            for t in range(NT):
                sp.dma_start(ctx[:, t, :], io.patches[:, t, :]).then_inc(ld_ctx[t], 16)
            sp.dma_start(w_in[:, :, :], io.w_in).then_inc(ld_w, 16)
            sp.dma_start(b_row[:, :], io.b_in).then_inc(ld_w, 16)
            sp.dma_start(g_init[:, :], io.g_init.partition_broadcast(P)).then_inc(ld_w, 16)

        norm_transpose(nc, "n0", x, xn, xt, k.ident, 1e-5, rms_eps=1e-5, gain=col(k.cols, "g_res"), load=load)
        lens, ends, wrap = [st.sb(n, [P, PT, B]) for n in "lens ends wrap".split()]
        upto = st.sb("upto", [P, P])
        place = st.sb("place", [P, S])
        hit = st.sb("hit", [P, PT * B, S], bf16)
        ones_h = st.sb("ones_h", [P, P], bf16)
        keep = st.sb("keep", [S, B, S])
        mark = st.sb("mark", [S, TOK])
        plug = st.sb("plug", [S, TOK])
        rowid = st.sb("rowid", [S, 1])
        pick = st.sb("pick", [S, TOK])
        scan = st.sb("scan", [S, 2, S])
        gather = st.sb("gather", [P, NT, P])
        sq = st.sb("sq", [P, CW])
        ss = st.sb("ss", [P, 4 * NT])
        p_ends, p_hits, p_gat = st.ps("p_ends"), st.ps("p_hits"), st.ps("p_gat")
        p_out = st.ps("p_out", NT)
        ready, ends_ready, hit_ready, hits_counted, picked, gat_ready, gat_done, \
            u_ready, out_ready, chain, actc, root_ready, pc = st.sems(
                "ready ends_ready hit_ready hits_counted picked gat_ready gat_done "
                "u_ready out_ready chain actc root_ready pc")
        block = st.block()

        @block.gpsimd
        def _(g):
            c = Chain(g, pc)
            c.mark(g.memset(upto[:, :], 1.0))
            c.mark(g.memset(ones_h[:, :], 1.0))
            c.mark(g.memset(keep[:, :, :], 1.0))
            c.mark(g.memset(scan[:, :, :], 0.0))
            c.mark(g.memset(gather[:, :, :], 0.0))
            c.mark(g.iota(place[:, :], [[1, S]], base=1, channel_multiplier=0,
                          allow_small_or_imprecise_dtypes=True))
            c.mark(g.iota(rowid[:, :], [[0, 1]], base=0, channel_multiplier=1,
                          allow_small_or_imprecise_dtypes=True))
            c.settle()
            c.mark(g.affine_select(out=upto[:, :], in_=upto[:, :], compare_op=ALU.is_ge, fill=0.0,
                                   base=0, pattern=[[1, P]], channel_multiplier=-1))
            c.mark(g.memset(keep[:, :, 0:1], 0.0))
            power = 0
            while decay**power > 1e-38:
                c.link(g.affine_select(out=scan[:, :, :], in_=scan[:, :, :], compare_op=ALU.not_equal,
                                       fill=decay**power, base=-power, pattern=[[0, 2], [-1, S]],
                                       channel_multiplier=1))
                power += 1
            g.sem_inc(ready, 1)

        @block.vector
        def _(dve):
            c = Chain(dve, chain)
            dve.wait_ge(ld_lens, 16)
            nc.vector.tensor_copy(lens[:, :, :], lens_i[:, :, :]).then_inc(hit_ready, 1)
            dve.wait_ge(root_ready, 1)
            c.link(nc.vector.reciprocal(ss[:, 2 * NT:3 * NT], ss[:, NT:2 * NT]))
            c.link(nc.vector.tensor_scalar(ss[:, 3 * NT:4 * NT], ss[:, 2 * NT:3 * NT], bcoef, None, ALU.mult))
            dve.wait_ge(ld_w, 48)
            for t in range(NT):
                nc.vector.scalar_tensor_tensor(ctx[:, t, 0:D], ctx[:, t, 0:D], ss[:, 3 * NT + t:3 * NT + t + 1],
                                               g_init[:, :], ALU.mult, ALU.mult).then_inc(u_ready, 1)
            dve.wait_ge(ends_ready, 1)
            dve.wait_ge(ready, 1)
            e = p_ends[:, 0:PT * B]
            c.link(nc.vector.tensor_scalar(wrap[:, :, :].rearrange("p a b -> p (a b)"), e, 0.0, float(S),
                                           ALU.is_le, ALU.mult))
            c.link(nc.vector.tensor_tensor(ends[:, :, :].rearrange("p a b -> p (a b)"),
                                           wrap[:, :, :].rearrange("p a b -> p (a b)"), e, ALU.add))
            nc.vector.tensor_tensor(
                hit[:, :, :], ends[:, :, :].rearrange("p a b -> p (a b)").unsqueeze(2).to_broadcast([P, PT * B, S]),
                place[:, :].unsqueeze(1).to_broadcast([P, PT * B, S]), ALU.is_equal).then_inc(hit_ready, 1)
            dve.wait_ge(hits_counted, 1)
            c.link(nc.vector.tensor_scalar(mark[:, :], p_hits[0:S, :], 1.0, None, ALU.min))
            c.link(nc.vector.tensor_tensor_scan(plug[:, :], keep[:, :, :].rearrange("p b s -> p (b s)"), mark[:, :],
                                                0.0, ALU.mult, ALU.add))
            c.link(nc.vector.tensor_scalar(plug[:, :], plug[:, :], -1.0, 0.0, ALU.add, ALU.max))
            nc.vector.tensor_scalar(pick[:, :], plug[:, :], rowid[:, 0:1], None, ALU.is_equal).then_inc(picked, 1)
            dve.wait_ge(gat_ready, 1)
            for h in range(2):
                nc.vector.tensor_copy(gather[h * S:(h + 1) * S, :, h * S:(h + 1) * S],
                                      p_gat[h * S:(h + 1) * S, :].rearrange("p (t h s) -> p t h s", h=2, s=S)[:, :, h, :]
                                      ).then_inc(gat_done, 1)
            for t in range(NT):
                dve.wait_ge(out_ready, t + 1)
                c.mark(nc.vector.tensor_tensor(x[:, t, :], x[:, t, :], p_out[:, t * BANK:(t + 1) * BANK], ALU.add))
            c.settle()

        @block.scalar
        def _(act):
            for t in range(NT):
                act.wait_ge(ld_ctx[t], 16)
                if t:
                    act.wait_ge(actc, t)
                nc.scalar.activation(sq[:, :], ctx[:, t, :], ACT.Square,
                                     accum_out=ss[:, t:t + 1]).then_inc(actc, 1)
            act.wait_ge(actc, NT)
            nc.scalar.activation(ss[:, NT:2 * NT], ss[:, 0:NT], ACT.Copy, bias=1e-5, scale=1.0 / CW).then_inc(actc, 1)
            act.wait_ge(actc, NT + 1)
            nc.scalar.activation(ss[:, NT:2 * NT], ss[:, NT:2 * NT], ACT.Sqrt).then_inc(root_ready, 1)

        @block.tensor
        def _(pe):
            pe.wait_ge(hit_ready, 1)
            pe.wait_ge(ready, 1)
            lt = lens[:, :, :]
            nc.tensor.matmul(p_ends[:, 0:PT * B], upto[:, :], lt.rearrange("p a b -> p (a b)"), start=True, stop=False)
            for j in range(PT - 1):
                rest = PT - 1 - j
                last = nc.tensor.matmul(p_ends[:, (j + 1) * B:PT * B], k.ones[:, :],
                                        lt[:, j:j + 1, :].to_broadcast([P, rest, B]), start=False, stop=(rest == 1))
            last.then_inc(ends_ready, 1)
            pe.wait_ge(hit_ready, 2)
            for j in range(PT):
                last = nc.tensor.matmul(p_hits[:, :], ones_h[:, :],
                                        hit[:, j * B:(j + 1) * B, :].rearrange("p b s -> p (b s)"),
                                        start=(j == 0), stop=(j == PT - 1))
            last.then_inc(hits_counted, 1)
            pe.wait_ge(ld_w, 48)
            for t in range(NT):
                o = p_out[:, t * BANK:(t + 1) * BANK]
                for c in range(DC):
                    nc.tensor.matmul(o, xt[:, c, t * P:(t + 1) * P], w_in[:, c, :], start=(c == 0), stop=False)
                nc.tensor.matmul(o, k.ones[0:1, :], b_row[0:1, :], start=False, stop=False)
            pe.wait_ge(picked, 1)
            nc.tensor.matmul(p_gat[:, :], scan[:, :, :].rearrange("p a b -> p (a b)"), pick[:, :],
                             start=True, stop=True).then_inc(gat_ready, 1)
            pe.wait_ge(gat_done, 2)
            pe.wait_ge(u_ready, NT)
            for t in range(NT):
                nc.tensor.matmul(p_out[:, t * BANK:(t + 1) * BANK], gather[:, t, :], ctx[:, t, 0:D],
                                 start=False, stop=True).then_inc(out_ready, 1)


DI, NS, RANK = 2 * D, 16, 32
EC = DI // P
NQ = 4


def mamba(nc, io, k, x, xn, xt):
    conv_b, conv_w = col(k.cols, "conv_b"), col(k.cols, "conv_w").rearrange("p (c j) -> p c j", j=4)
    d_skip, dt_b = col(k.cols, "d_skip"), col(k.cols, "dt_b")
    with Stage(nc, "mb") as keep:
        xa = keep.sb("xa", [P, EC, TOK])
        gate = keep.sb("gate", [P, EC, TOK])
        delta = keep.sb("delta", [P, EC + 1, TOK])
        dbc = keep.sb("dbc", [RANK + 2 * NS, TOK])
        a_neg = keep.sb("a_neg", [P, EC, NS])
        with Stage(nc, "mw") as early:
            w = early.sb("w", [P, DC, 2 * DI])
            ld_wc = [early.sem(f"ld_w{c}") for c in range(DC)]

            def load(sp):
                for c in range(DC):
                    sp.dma_start(w[:, c, :], io.in_proj[:, c, :]).then_inc(ld_wc[c], 16)

            norm_transpose(nc, "n1", x, xn, xt, k.ident, 1e-5, load=load)
            mamba_in(nc, io, k, xt, w, ld_wc, xa, gate, delta, dbc, a_neg, conv_b, conv_w, dt_b)
        mamba_scan(nc, io, k, xa, delta, dbc, a_neg)
        mamba_out(nc, io, x, xa, gate, delta, d_skip)


def mamba_in(nc, io, k, xt, w, ld_wc, xa, gate, delta, dbc, a_neg, conv_b, conv_w, dt_b):
    TAPS = 4
    with Stage(nc, "mi") as st:
        w_x = st.sb("w_x", [P, EC, RANK + 2 * NS])
        w_dt = st.sb("w_dt", [RANK, DI])
        a_log = st.sb("a_log", [P, EC, NS])
        pad = [st.sb(f"pad{i}", [P, B, S + TAPS - 1]) for i in range(2)]
        acc = [st.sb(f"acc{i}", [P, B, S]) for i in range(2)]
        v_abs, v_exp, v_one, v_ln, v_inv, v_max = [st.sb(n, [P, 2, TOK]) for n in
                                                   "v_abs v_exp v_one v_ln v_inv v_max".split()]
        proj = st.ps("proj", 4)
        p_dbc = st.ps("p_dbc")
        p_dt = st.ps("p_dt", 2)
        ld_x, ld_dt, ld_a, padded, conv_out, proj_ready, x_copied, gated, xa_ready, dbc_ready, dbc_copied, \
            dt_ready, exp_ready, one_ready, ln_ready, chain, a_chain, v_maxed, v_copied, v_step = st.sems(
                "ld_x ld_dt ld_a padded conv_out proj_ready x_copied gated xa_ready dbc_ready dbc_copied "
                "dt_ready exp_ready one_ready ln_ready chain a_chain v_maxed v_copied v_step")
        block = st.block()

        @block.sync
        def _(sp):
            sp.dma_start(w_x[:, :, :], io.x_proj).then_inc(ld_x, 16)
            sp.dma_start(w_dt[:, :], io.dt_proj).then_inc(ld_dt, 16)
            sp.dma_start(a_log[:, :, :], io.a_log).then_inc(ld_a, 16)

        @block.gpsimd
        def _(g):
            for i in range(2):
                g.memset(pad[i][:, :, 0:TAPS - 1], 0.0).then_inc(padded, 1)

        @block.tensor
        def _(pe):
            for c in range(DC):
                pe.wait_ge(ld_wc[c], 16)
            for e in range(2 * EC):
                if e >= 4:
                    if e % 2 == 0:
                        pe.wait_ge(x_copied, (e - 4) // 2 + 1)
                    else:
                        pe.wait_ge(gated, (e - 4) // 2 + 1)
                f = (e // 2) * P + (e % 2) * DI
                for c in range(DC):
                    last = nc.tensor.matmul(proj[:, (e % 4) * BANK:(e % 4 + 1) * BANK], w[:, c, f:f + P], xt[:, c, :],
                                            start=(c == 0), stop=(c == DC - 1))
                last.then_inc(proj_ready, 1)
            pe.wait_ge(ld_x, 16)
            for e in range(EC):
                pe.wait_ge(xa_ready, e + 1)
                last = nc.tensor.matmul(p_dbc[0:RANK + 2 * NS, :], w_x[:, e, :], xa[:, e, :],
                                        start=(e == 0), stop=(e == EC - 1))
            last.then_inc(dbc_ready, 1)
            pe.wait_ge(dbc_copied, 1)
            pe.wait_ge(ld_dt, 16)
            for e in range(EC):
                if e >= 2:
                    pe.wait_ge(v_copied, e - 1)
                nc.tensor.matmul(p_dt[:, (e % 2) * BANK:(e % 2 + 1) * BANK], w_dt[:, e * P:(e + 1) * P],
                                 dbc[0:RANK, :], start=True, stop=True).then_inc(dt_ready, 1)

        @block.scalar
        def _(act):
            for e in range(EC):
                act.wait_ge(proj_ready, 2 * e + 1)
                if e < 2:
                    act.wait_ge(padded, 2)
                else:
                    act.wait_ge(conv_out, e - 1)
                nc.scalar.activation(pad[e % 2][:, :, TAPS - 1:], proj[:, (2 * e % 4) * BANK:(2 * e % 4 + 1) * BANK]
                                     .rearrange("p (b s) -> p b s", s=S), ACT.Copy).then_inc(x_copied, 1)
                act.wait_ge(proj_ready, 2 * e + 2)
                o = (2 * e + 1) % 4
                nc.scalar.activation(gate[:, e, :], proj[:, o * BANK:(o + 1) * BANK], ACT.Silu).then_inc(gated, 1)
                act.wait_ge(conv_out, e + 1)
                nc.scalar.activation(xa[:, e, :], acc[e % 2][:, :, :].rearrange("p b s -> p (b s)"),
                                     ACT.Silu).then_inc(xa_ready, 1)
            act.wait_ge(dbc_ready, 1)
            nc.scalar.activation(dbc[:, :], p_dbc[0:RANK + 2 * NS, :], ACT.Copy).then_inc(dbc_copied, 1)
            act.wait_ge(ld_a, 16)
            nc.scalar.activation(a_neg[:, :, :], a_log[:, :, :], ACT.Exp).then_inc(a_chain, 1)
            n = 1
            for e in range(0, EC, 2):
                act.wait_ge(dt_ready, e + 2)
                if e:
                    act.wait_ge(v_step, 2 * e)
                for h in range(2):
                    nc.scalar.activation(v_max[:, h, :], p_dt[:, h * BANK:(h + 1) * BANK], ACT.Identity,
                                         bias=dt_b[:, e + h:e + h + 1]).then_inc(v_copied, 1)
                act.wait_ge(v_copied, e + 2)
                nc.scalar.activation(v_abs[:, :, :], v_max[:, :, :], ACT.Abs).then_inc(a_chain, 1)
                n += 1
                act.wait_ge(a_chain, n)
                nc.scalar.activation(v_exp[:, :, :], v_abs[:, :, :], ACT.Exp, scale=-1.0).then_inc(exp_ready, 1)
                act.wait_ge(one_ready, e // 2 + 1)
                nc.scalar.activation(v_ln[:, :, :], v_one[:, :, :], ACT.Ln).then_inc(a_chain, 1)
                n += 1
                act.wait_ge(a_chain, n)
                nc.scalar.activation(v_inv[:, :, :], v_ln[:, :, :], ACT.Exp, scale=-1.0).then_inc(ln_ready, 1)

        @block.vector
        def _(dve):
            c = Chain(dve, chain)
            for e in range(EC):
                dve.wait_ge(x_copied, e + 1)
                if e >= 2:
                    dve.wait_ge(xa_ready, e - 1)
                o, s = acc[e % 2], pad[e % 2]
                c.link(nc.vector.tensor_scalar(o[:, :, :], s[:, :, 0:S], conv_w[:, e, 0:1], conv_b[:, e:e + 1],
                                               ALU.mult, ALU.add))
                for j in range(1, TAPS):
                    ins = nc.vector.scalar_tensor_tensor(o[:, :, :], s[:, :, j:j + S], conv_w[:, e, j:j + 1],
                                                         o[:, :, :], ALU.mult, ALU.add)
                    if j < TAPS - 1:
                        c.link(ins)
                    else:
                        ins.then_inc(conv_out, 1)
            for e in range(0, EC, 2):
                dve.wait_ge(exp_ready, e // 2 + 1)
                nc.vector.tensor_scalar(v_max[:, :, :], v_max[:, :, :], 0.0, None, ALU.max).then_inc(v_maxed, 1)
                nc.vector.tensor_scalar(v_one[:, :, :], v_exp[:, :, :], 1.0, None, ALU.add).then_inc(one_ready, 1)
                dve.wait_ge(one_ready, e // 2 + 1)
                dve.wait_ge(ln_ready, e // 2 + 1)
                nc.vector.scalar_tensor_tensor(v_exp[:, :, :], v_one[:, :, :], -1.0, v_exp[:, :, :], ALU.add,
                                               ALU.subtract).then_inc(v_step, 1)
                dve.wait_ge(v_step, 4 * (e // 2) + 1)
                nc.vector.tensor_tensor(v_exp[:, :, :], v_exp[:, :, :], v_inv[:, :, :], ALU.mult).then_inc(v_step, 1)
                dve.wait_ge(v_step, 4 * (e // 2) + 2)
                nc.vector.tensor_tensor(v_ln[:, :, :], v_ln[:, :, :], v_exp[:, :, :], ALU.subtract).then_inc(v_step, 1)
                dve.wait_ge(v_step, 4 * (e // 2) + 3)
                dve.wait_ge(v_maxed, e // 2 + 1)
                nc.vector.tensor_tensor(delta[:, e + 1:e + 3, :], v_ln[:, :, :], v_max[:, :, :],
                                        ALU.add).then_inc(v_step, 1)
            dve.wait_ge(a_chain, 1)
            nc.vector.tensor_scalar(a_neg[:, :, :], a_neg[:, :, :], -1.0, None, ALU.mult).then_inc(v_step, 1)


def mamba_scan(nc, io, k, xa, delta, dbc, a_neg):
    with Stage(nc, "ms") as st:
        b_all = st.sb("b_all", [P, NS, TOK])
        c_all = st.sb("c_all", [P, NS, TOK])
        da = [st.sb(f"da{i}", [P, NQ, B, S]) for i in range(2)]
        h = [st.sb(f"h{i}", [P, NQ, TOK]) for i in range(2)]
        hc = [st.sb(f"hc{i}", [P, NQ, TOK]) for i in range(2)]
        du = st.sb("du", [P, TOK])
        ROWS = RANK + 2 * NS
        parts = st.sb("parts", [ROWS, 3, TOK], bf16)
        p_bc = st.ps("p_bc", 4)
        p_y = st.ps("p_y")
        bc_ready, b_copied, c_copied, first_zero, da_ready, du_ready, h_set, scanned, hc_ready, summed, y_copied, split = \
            st.sems("bc_ready b_copied c_copied first_zero da_ready du_ready h_set scanned hc_ready summed y_copied split")
        block = st.block()
        STEPS = NS // NQ
        flat = "p n t -> p (n t)"

        @block.gpsimd
        def _(g):
            for i in range(2):
                g.memset(da[i][:, :, :, 0:1], 0.0).then_inc(first_zero, 1)
            g.wait_ge(c_copied, NS)
            with g.Fori(0, EC) as e:
                for q in range(STEPS):
                    g.wait_ge(scanned, e * STEPS + (q + 3))
                    g.wait_ge(summed, e * STEPS + (q + 1))
                    g.tensor_tensor(hc[q % 2][:, :, :], h[q % 2][:, :, :], c_all[:, q * NQ:(q + 1) * NQ, :],
                                    ALU.mult).then_inc(hc_ready, 1)

        @block.tensor
        def _(pe):
            pe.wait_ge(split, 5)
            for n in range(2 * NS):
                if n >= 4:
                    pe.wait_ge(b_copied if n % 2 == 0 else c_copied, (n - 4) // 2 + 1)
                r = RANK + n // 2 + (n % 2) * NS
                for i in range(3):
                    last = nc.tensor.matmul(p_bc[:, (n % 4) * BANK:(n % 4 + 1) * BANK],
                                            k.ident_h[0:ROWS, r:r + 1].to_broadcast([ROWS, P]), parts[:, i, :],
                                            start=(i == 0), stop=(i == 2))
                last.then_inc(bc_ready, 1)
            nc.tensor.matmul(p_y[:, :], k.ident_h[0:ROWS, :], parts[:, 0, :], start=True, stop=True)\
                .then_inc(summed, 2)
            with pe.Fori(0, EC) as e:
                pe.wait_ge(y_copied, e + 1)
                for q in range(STEPS):
                    pe.wait_ge(hc_ready, e * STEPS + (q + 3))
                    for n in range(NQ):
                        last = nc.tensor.matmul(p_y[:, :], k.ident[:, :], hc[q % 2][:, n, :],
                                                start=(q == 0 and n == 0), stop=(q == STEPS - 1 and n == NQ - 1))
                    last.then_inc(summed, 1)

        @block.scalar
        def _(act):
            for n in range(NS):
                act.wait_ge(bc_ready, 2 * n + 2)
                o = (2 * n + 1) % 4
                nc.scalar.activation(c_all[:, n, :], p_bc[:, o * BANK:(o + 1) * BANK], ACT.Copy)\
                    .then_inc(c_copied, 1)
            act.wait_ge(first_zero, 2)
            with act.Fori(0, EC) as e:
                for q in range(STEPS):
                    act.wait_ge(scanned, e * STEPS + (q + 1))
                    for n in range(NQ):
                        ins = nc.scalar.activation(
                            da[q % 2][:, n, :, 1:],
                            delta[:, bass.ds(e + 1, 1), :].rearrange("p a (b s) -> p (a b) s", s=S)[:, :, 1:],
                            ACT.Exp, scale=a_neg[:, bass.ds(e, 1), q * NQ + n:q * NQ + n + 1]
                            .rearrange("p a n -> p (a n)"))
                    ins.then_inc(da_ready, 1)
                    if q == 1:
                        act.wait_ge(summed, e * STEPS + 2)
                        act.wait_ge(du_ready, e + 1)
                        nc.scalar.activation(delta[:, bass.ds(e, 1), :].rearrange("p a t -> p (a t)"), p_y[:, :],
                                             ACT.Copy).then_inc(y_copied, 1)
            act.wait_ge(summed, EC * STEPS + 2)
            nc.scalar.activation(delta[:, EC, :], p_y[:, :], ACT.Copy).then_inc(y_copied, 1)

        @block.vector
        def _(dve):
            dve.sem_inc(scanned, 2)
            dve.sem_inc(hc_ready, 2)
            dve.sem_inc(h_set, 1)
            for i in range(3):
                if i:
                    nc.vector.tensor_tensor(dbc[:, :], dbc[:, :], parts[:, i - 1, :], ALU.subtract).then_inc(split, 1)
                    dve.wait_ge(split, 2 * i)
                nc.vector.tensor_copy(parts[:, i, :], dbc[:, :]).then_inc(split, 1)
                dve.wait_ge(split, 2 * i + 1)
            for n in range(NS):
                dve.wait_ge(bc_ready, 2 * n + 1)
                o = (2 * n) % 4
                nc.vector.tensor_copy(b_all[:, n, :], p_bc[:, o * BANK:(o + 1) * BANK]).then_inc(b_copied, 1)
            dve.wait_ge(b_copied, NS)
            with dve.Fori(0, EC) as e:
                dve.wait_ge(h_set, e * STEPS + 1)
                nc.vector.tensor_tensor(du[:, :], delta[:, bass.ds(e + 1, 1), :].rearrange("p a t -> p (a t)"),
                                        xa[:, bass.ds(e, 1), :].rearrange("p a t -> p (a t)"),
                                        ALU.mult).then_inc(du_ready, 1)
                dve.wait_ge(du_ready, e + 1)
                for q in range(STEPS):
                    dve.wait_ge(hc_ready, e * STEPS + (q + 1))
                    nc.vector.tensor_tensor(h[q % 2][:, :, :], b_all[:, q * NQ:(q + 1) * NQ, :],
                                            du[:, :].unsqueeze(1).to_broadcast([P, NQ, TOK]),
                                            ALU.mult).then_inc(h_set, 1)
                    dve.wait_ge(h_set, e * STEPS + (q + 2))
                    dve.wait_ge(da_ready, e * STEPS + (q + 1))
                    hf = h[q % 2][:, :, :].rearrange(flat)
                    nc.vector.tensor_tensor_scan(hf, da[q % 2][:, :, :, :].rearrange("p n b s -> p (n b s)"), hf,
                                                 0.0, ALU.mult, ALU.add).then_inc(scanned, 1)


def mamba_out(nc, io, x, xa, gate, delta, d_skip):
    with Stage(nc, "mo") as st:
        w = st.sb("w", [P, EC, D])
        p_out = st.ps("p_out", NT)
        skipped, gated, out_ready, added = st.sems("skipped gated out_ready added")
        ld_w = [st.sem(f"ld_w{i}") for i in range(2)]
        block = st.block()

        @block.sync
        def _(sp):
            for i in range(2):
                sp.dma_start(w[:, i * EC // 2:(i + 1) * EC // 2, :],
                             io.out_proj[:, i * EC // 2:(i + 1) * EC // 2, :]).then_inc(ld_w[i], 16)

        @block.vector
        def _(dve):
            for e in range(EC):
                nc.vector.scalar_tensor_tensor(xa[:, e, :], xa[:, e, :], d_skip[:, e:e + 1], delta[:, e + 1, :],
                                               ALU.mult, ALU.add).then_inc(skipped, 1)
                dve.wait_ge(skipped, e + 1)
                nc.vector.tensor_tensor(gate[:, e, :], gate[:, e, :], xa[:, e, :], ALU.mult).then_inc(gated, 1)
            for t in range(NT):
                dve.wait_ge(out_ready, t + 1)
                nc.vector.tensor_tensor(x[:, t, :], x[:, t, :], p_out[:, t * BANK:(t + 1) * BANK],
                                        ALU.add).then_inc(added, 1)
            dve.wait_ge(added, NT)

        @block.tensor
        def _(pe):
            for e in range(EC):
                pe.wait_ge(ld_w[2 * e // EC], 16)
                pe.wait_ge(gated, e + 1)
                for t in range(NT):
                    ins = nc.tensor.matmul(p_out[:, t * BANK:(t + 1) * BANK], gate[:, e, t * P:(t + 1) * P], w[:, e, :],
                                           start=(e == 0), stop=(e == EC - 1))
                    if e == EC - 1:
                        ins.then_inc(out_ready, 1)


HID = 4 * D
HC = HID // P
QB = 127.0


def bitnet(nc, io, k, x, xn, xt):
    with Stage(nc, "bn") as st:
        w = [st.sb("w1", [P, DC * HID]), st.sb("w2", [P, HC * D])]
        ld_w = [st.sem(f"ld_w{i}") for i in range(2)]

        def load(sp):
            sp.dma_start(w[0][:, :], io.w1.rearrange("p c n -> p (c n)")).then_inc(ld_w[0], 16)
            sp.dma_start(w[1][:, :], io.w2.rearrange("p c n -> p (c n)")).then_inc(ld_w[1], 16)

        norm_transpose(nc, "n2", x, xn, xt, k.ident, 1e-5, transpose=False, load=load)
        wq = [st.sb("w1q", [P, DC * HID], bf16), st.sb("w2q", [P, HC * D], bf16)]
        b1, b2 = st.sb("b1", [P, HID]), st.sb("b2", [P, D])
        wsum, wscale, winv = st.sb("wsum", [P, 2]), st.sb("wscale", [P, 2]), st.sb("winv", [P, 2])
        amax, inv, oscale = st.sb("amax", [P, 2 * NT]), st.sb("inv", [P, 2 * NT]), st.sb("oscale", [P, 2 * NT])
        xq = st.sb("xq", [P, NT, D], bf16)
        xqt = st.sb("xqt", [P, NT, DC, P], bf16)
        h = [st.sb(f"h{i}", [P, HID]) for i in range(2)]
        hq = [st.sb(f"hq{i}", [P, HID], bf16) for i in range(2)]
        hqt = st.sb("hqt", [P, HC, P], bf16)
        p_h = st.ps("p_h", 4)
        p_sum = st.ps("p_sum")
        p_out = st.ps("p_out")
        p_t = st.stack.enter_context(nc.psum_tensor("bn_p_t", [P, 2 * 2 * BANK], bf16))
        ld_b, abs_done, sums_ready, winv_ready, rounded, wq_ready, xq_ready, xt_ready, xt_copied, h_ready, biased, \
            gelued, hq_ready, ht_ready, ht_copied, y_ready, chain, added = st.sems(
                "ld_b abs_done sums_ready winv_ready rounded wq_ready xq_ready xt_ready xt_copied h_ready biased "
                "gelued hq_ready ht_ready ht_copied y_ready chain added")
        block = st.block()

        @block.sync
        def _(sp):
            sp.dma_start(b1[:, :], io.b1.partition_broadcast(P)).then_inc(ld_b, 16)
            sp.dma_start(b2[:, :], io.b2.partition_broadcast(P)).then_inc(ld_b, 16)

        @block.scalar
        def _(act):
            for i in range(2):
                act.wait_ge(ld_w[i], 16)
                nc.scalar.activation(wq[i][:, :], w[i][:, :], ACT.Abs, accum_out=wsum[:, i:i + 1]).then_inc(abs_done, 1)
                if i == 0:
                    act.wait_ge(xt_ready, 1)
                    nc.scalar.activation(xqt[:, :, :, :], p_t[:, :].rearrange("p (t c n) -> p t c n", c=DC, n=P),
                                         ACT.Copy).then_inc(xt_copied, 1)
                act.wait_ge(winv_ready, i + 1)
                nc.scalar.activation(w[i][:, :], w[i][:, :], ACT.Copy, scale=winv[:, i:i + 1],
                                     bias=ROUND).then_inc(rounded, 1)
            for t in range(NT + 1):
                if t < NT:
                    act.wait_ge(biased, t + 1)
                    nc.scalar.activation(h[t % 2][:, :], h[t % 2][:, :], ACT.Gelu).then_inc(gelued, 1)
                if t:
                    act.wait_ge(ht_ready, t)
                    if t >= 2:
                        act.wait_ge(y_ready, t - 1)
                    nc.scalar.activation(hqt[:, :, :], p_t[:, :].rearrange("p (c n) -> p c n", n=P),
                                         ACT.Copy).then_inc(ht_copied, 1)

        @block.vector
        def _(dve):
            c = Chain(dve, chain)

            def quantize(out, v, at):
                c.link(nc.vector.tensor_reduce(amax[:, at:at + 1], v, AX.X, ALU.max, apply_absolute_value=True))
                c.link(nc.vector.tensor_scalar(amax[:, at:at + 1], amax[:, at:at + 1], 1e-5, None, ALU.max))
                c.link(nc.vector.reciprocal(inv[:, at:at + 1], amax[:, at:at + 1]))
                c.link(nc.vector.tensor_scalar(inv[:, at:at + 1], inv[:, at:at + 1], QB, None, ALU.mult))
                c.link(nc.vector.tensor_scalar(v, v, inv[:, at:at + 1], -QB - 1.0, ALU.mult, ALU.max))
                c.link(nc.vector.tensor_scalar(v, v, QB, ROUND, ALU.min, ALU.add))
                return nc.vector.tensor_scalar(out, v, -ROUND, None, ALU.add)

            for t in range(NT):
                quantize(xq[:, t, :], xn[:, t, :], t).then_inc(xq_ready, 1)
            def bias(t):
                dve.wait_ge(h_ready, t + 1)
                if t >= 2:
                    dve.wait_ge(hq_ready, t - 1)
                nc.vector.scalar_tensor_tensor(h[t % 2][:, :], p_h[:, :], oscale[:, t:t + 1], b1[:, :], ALU.mult,
                                               ALU.add).then_inc(biased, 1)

            def leave(t):
                dve.wait_ge(y_ready, t + 1)
                c.link(nc.vector.scalar_tensor_tensor(xn[:, t, :], p_out[:, :], oscale[:, NT + t:NT + t + 1],
                                                      b2[:, :], ALU.mult, ALU.add))
                nc.vector.tensor_tensor(x[:, t, :], x[:, t, :], xn[:, t, :], ALU.add).then_inc(added, 1)

            for i in range(2):
                dve.wait_ge(sums_ready, i + 1)
                c.link(nc.vector.tensor_scalar(wscale[:, i:i + 1], p_sum[:, i:i + 1], 1.0 / (D * HID), 1e-5, ALU.mult,
                                               ALU.max))
                nc.vector.reciprocal(winv[:, i:i + 1], wscale[:, i:i + 1]).then_inc(winv_ready, 1)
                if i == 0:
                    c.link(nc.vector.tensor_scalar(oscale[:, 0:NT], amax[:, 0:NT], wscale[:, 0:1], 1.0 / QB, ALU.mult,
                                                   ALU.mult))
                dve.wait_ge(rounded, i + 1)
                c.link(nc.vector.tensor_scalar(w[i][:, :], w[i][:, :], ROUND + 1.0, ROUND - 1.0, ALU.min, ALU.max))
                nc.vector.tensor_scalar(wq[i][:, :], w[i][:, :], -ROUND, None, ALU.add).then_inc(wq_ready, 1)
                if i == 0:
                    dve.wait_ge(ld_b, 32)
                    bias(0)
            for t in range(NT):
                if t + 1 < NT:
                    bias(t + 1)
                dve.wait_ge(gelued, t + 1)
                if t >= 2:
                    dve.wait_ge(ht_ready, t - 1)
                quantize(hq[t % 2][:, :], h[t % 2][:, :], NT + t).then_inc(hq_ready, 1)
                c.link(nc.vector.tensor_scalar(oscale[:, NT + t:NT + t + 1], amax[:, NT + t:NT + t + 1],
                                               wscale[:, 1:2], 1.0 / QB, ALU.mult, ALU.mult))
                if t:
                    leave(t - 1)
            leave(NT - 1)
            dve.wait_ge(added, NT)

        @block.tensor
        def _(pe):
            pe.wait_ge(xq_ready, NT)
            for t in range(NT):
                for c in range(DC):
                    at = (t * DC + c) * P
                    last = nc.tensor.transpose(p_t[:, at:at + P], xq[:, t, c * P:(c + 1) * P], k.ident_h[:, :])
            last.then_inc(xt_ready, 1)
            for i in range(2):
                pe.wait_ge(abs_done, i + 1)
                if i:
                    pe.wait_ge(winv_ready, 1)
                nc.tensor.matmul(p_sum[:, i:i + 1], k.ones[:, :], wsum[:, i:i + 1], start=True, stop=True)\
                    .then_inc(sums_ready, 1)
            pe.wait_ge(xt_copied, 1)
            pe.wait_ge(wq_ready, 1)

            def first(t):
                if t:
                    pe.wait_ge(biased, t)
                w1 = wq[0][:, :].rearrange("p (c n) -> p c n", n=HID)
                for j in range(4):
                    for c in range(DC):
                        last = nc.tensor.matmul(p_h[:, j * BANK:(j + 1) * BANK], xqt[:, t, c, :],
                                                w1[:, c, j * BANK:(j + 1) * BANK], start=(c == 0), stop=(c == DC - 1))
                last.then_inc(h_ready, 1)

            def second(t):
                pe.wait_ge(hq_ready, t + 1)
                if t:
                    pe.wait_ge(ht_copied, t)
                for c in range(HC):
                    last = nc.tensor.transpose(p_t[:, c * P:(c + 1) * P], hq[t % 2][:, c * P:(c + 1) * P],
                                               k.ident_h[:, :])
                last.then_inc(ht_ready, 1)
                pe.wait_ge(ht_copied, t + 1)
                pe.wait_ge(wq_ready, 2)
                if t:
                    pe.wait_ge(added, t)
                w2 = wq[1][:, :].rearrange("p (c n) -> p c n", n=D)
                for c in range(HC):
                    last = nc.tensor.matmul(p_out[:, :], hqt[:, c, :], w2[:, c, :], start=(c == 0), stop=(c == HC - 1))
                last.then_inc(y_ready, 1)

            first(0)
            first(1)
            for t in range(NT):
                if t + 2 < NT:
                    first(t + 2)
                second(t)


HEADS, DH = 16, 64
PAIRS = HEADS // 2
GROUPS = 2
GP = PAIRS // GROUPS
CC = CW // P
JT = (CTX + P - 1) // P
KEYS = CTX + 1
LAST = CTX - (JT - 1) * P
CUTS = [0, 401, 802, 1202, KEYS]
W_UP = 64.0
P_UP = 4096.0
ITEMS = 4 * GP + JT


def cross_attention(nc, io, k, x, xn, xt, work):
    q_parts = work.bitcast(f16).rearrange("p (b l c s) -> p b l c s", b=B, l=2, c=PAIRS)
    o_t = work.rearrange("p (b c s) -> p b c s", b=B, c=PAIRS)
    with Stage(nc, "ca") as st:
        w_kv = [st.sb(f"w_kv{i}", [P, CC, 2 * HEADS * DH], f16) for i in range(2)]
        v_last = [st.sb(f"v_last{i}", [P, GROUPS, GP * P], f16) for i in range(2)]
        keys = [[st.sb(f"keys{s}{i}", [P, KEYS], f16) for i in range(2)] for s in range(2)]
        queries_and_weights(nc, io, k, x, xn, xt, w_kv, v_last, keys, q_parts)
        ctx = [st.sb(f"ctx{i}", [P, CC, CTX], f16) for i in range(2)]
        stage = [st.sb(f"stage{s}", [P, CC * P]) for s in range(2)]
        attend(nc, io, w_kv, ctx, v_last, keys, stage, q_parts, o_t, st, k)
    project_out(nc, io, k, x, o_t)


def queries_and_weights(nc, io, k, x, xn, xt, w_kv, v_last, keys, q_parts):
    RAWS = 4
    with Stage(nc, "cq") as st:
        w = st.sb("w", [P, DC, PAIRS * P])
        raw = [st.sb(f"raw{s}", [P, 2 * HEADS * DH]) for s in range(RAWS)]
        ld_w = st.sem("ld_w")
        ld_raw = [st.sem(f"ld_raw{s}") for s in range(RAWS)]

        def load_raw(sp, c):
            sp.dma_start(raw[c % RAWS][:, :], io.w_kv[:, c, :]).then_inc(ld_raw[c % RAWS], 16)

        def load(sp):
            sp.dma_start(w[:, :, :], io.w_q).then_inc(ld_w, 16)
            for c in range(RAWS):
                load_raw(sp, c)

        norm_transpose(nc, "n3", x, xn, xt, k.ident, 1e-5, load=load)
        q = st.sb("q", [P, 2, PAIRS, TOK], f16)
        nk, nv = st.sb("nk", [P, 1]), st.sb("nv", [1, GP * P])
        nk_high, nk_low = st.sb("nk_high", [P, 1], f16), st.sb("nk_low", [P, 1], f16)
        nv_parts = st.sb("nv_parts", [1, 2, GP * P], f16)
        p_q = st.ps("p_q", 4)
        q_ready, q_high, q_low, moved, ld_null, w_high, w_low, null_high, null_low, null_set = st.sems(
            "q_ready q_high q_low moved ld_null w_high w_low null_high null_low null_set")
        block = st.block()

        @block.sync
        def _(sp):
            sp.dma_start(nk[:, :], io.null_k).then_inc(ld_null, 16)
            sp.dma_start(nv[:, :], io.null_v).then_inc(ld_null, 16)
            for c in range(RAWS, CC):
                sp.wait_ge(w_low, c - RAWS + 1)
                load_raw(sp, c)
            sp.wait_ge(null_low, 2)
            for i in range(2):
                for g in range(GROUPS):
                    sp.dma_start(v_last[i][LAST:LAST + 1, g, :], nv_parts[:, i, :]).then_inc(null_set, 16)
            sp.wait_ge(null_set, 16 * 2 * GROUPS)

        @block.tensor
        def _(pe):
            pe.wait_ge(ld_w, 16)
            for f in range(PAIRS):
                if f >= 4:
                    pe.wait_ge(q_low, f - 3)
                for c in range(DC):
                    last = nc.tensor.matmul(p_q[:, (f % 4) * BANK:(f % 4 + 1) * BANK], w[:, c, f * P:(f + 1) * P],
                                            xt[:, c, :], start=(c == 0), stop=(c == DC - 1))
                last.then_inc(q_ready, 1)

        @block.scalar
        def _(act):
            act.wait_ge(ld_null, 32)
            nc.scalar.activation(nk_high[:, :], nk[:, :], ACT.Copy, scale=W_UP).then_inc(null_high, 1)
            nc.scalar.activation(nv_parts[:, 0, :], nv[:, :], ACT.Copy, scale=W_UP).then_inc(null_high, 1)
            for f in range(PAIRS):
                act.wait_ge(q_ready, f + 1)
                nc.scalar.activation(q[:, 0, f, :], p_q[:, (f % 4) * BANK:(f % 4 + 1) * BANK], ACT.Copy)\
                    .then_inc(q_high, 1)
                c = f
                act.wait_ge(ld_raw[c % RAWS], 16 * (c // RAWS + 1))
                nc.scalar.activation(w_kv[0][:, c, :], raw[c % RAWS][:, :], ACT.Copy, scale=W_UP).then_inc(w_high, 1)
            act.wait_ge(q_low, PAIRS)
            nc.scalar.activation(q_parts[:, :, 0, :, :], q[:, 0, :, :].rearrange("p c (b s) -> p b c s", b=B),
                                 ACT.Copy).then_inc(moved, 1)
            act.wait_ge(moved, 2)

        @block.vector
        def _(dve):
            dve.wait_ge(null_high, 2)
            nc.vector.scalar_tensor_tensor(nk_low[:, :], nk[:, :], W_UP, nk_high[:, :], ALU.mult,
                                           ALU.subtract).then_inc(null_low, 1)
            nc.vector.scalar_tensor_tensor(nv_parts[:, 1, :], nv[:, :], W_UP, nv_parts[:, 0, :], ALU.mult,
                                           ALU.subtract).then_inc(null_low, 1)
            dve.wait_ge(null_low, 2)
            for s in range(2):
                nc.vector.tensor_copy(keys[s][0][:, CTX:KEYS], nk_high[:, :])
                nc.vector.tensor_copy(keys[s][1][:, CTX:KEYS], nk_low[:, :])
            for f in range(PAIRS):
                dve.wait_ge(q_high, f + 1)
                nc.vector.tensor_tensor(q[:, 1, f, :], p_q[:, (f % 4) * BANK:(f % 4 + 1) * BANK], q[:, 0, f, :],
                                        ALU.subtract).then_inc(q_low, 1)
                c = f
                dve.wait_ge(w_high, c + 1)
                nc.vector.scalar_tensor_tensor(w_kv[1][:, c, :], raw[c % RAWS][:, :], W_UP, w_kv[0][:, c, :], ALU.mult,
                                               ALU.subtract).then_inc(w_low, 1)
            dve.wait_ge(q_low, PAIRS)
            nc.vector.tensor_copy(q_parts[:, :, 1, :, :], q[:, 1, :, :].rearrange("p c (b s) -> p b c s", b=B))\
                .then_inc(moved, 1)
            dve.wait_ge(w_low, CC)


def attend(nc, io, w_kv, ctx, v_last, keys, stage, q_parts, o_t, st, k):
    probs = st.sb("probs", [P, KEYS])
    parts = st.sb("parts", [P, 2, GP, KEYS], f16)
    q_diag = [st.sb(f"q_diag{i}", [P, PAIRS, P], f16) for i in range(2)]
    vals = [[st.sb(f"vals{s}{i}", [P, GP * P], f16) for i in range(2)] for s in range(2)]
    pt = [st.sb(f"pt{s}", [P, 2 * GP * P], f16) for s in range(2)]
    small = st.sb("small", [P, 6])
    peak, nbias, rsum, rinv = small[:, 0:2], small[:, 2:3], small[:, 3:5], small[:, 5:6]
    p_kv = st.ps("p_kv", 2)
    p_s = st.ps("p_s", 4)
    p_o = st.ps("p_o")
    p_t = st.ps("p_t")[:, :].bitcast(f16)
    prod_ready, high_done, low_done, s_ready, max_done, exp_done, inv_done, wh_done, wl_done, t_ready, pt_done, \
        av_done, o_ready, o_copied, ctx_high, ctx_low, q_ready, zeroed, dchain = st.sems(
            "prod_ready high_done low_done s_ready max_done exp_done inv_done wh_done wl_done t_ready pt_done av_done "
            "o_ready o_copied ctx_high ctx_low q_ready zeroed dchain")
    ld = [st.sem(f"ld{s}") for s in range(2)]
    block = st.block()
    SEQ = GROUPS * ITEMS

    def rows(j):
        return LAST if j == JT - 1 else P

    def chunk(n):
        return CUTS[n], min(CUTS[n + 1], CTX)

    def bank(i):
        return p_kv[:, (i % 2) * BANK:(i % 2 + 1) * BANK]

    def scores(n, n2):
        w = CUTS[n + 1] - CUTS[n]
        return p_s[:, n * BANK:n2 * BANK].rearrange("p (a n) -> p a n", n=BANK)[:, :, 0:w]

    @block.sync
    def _(sp):
        def load(j, seq):
            sp.dma_start(stage[j % 2][:, :], io.ctx_t[bass.ds(seq, 1), j, :, :].rearrange("a p n -> (a p) n"))\
                .then_inc(ld[j % 2], 16)

        for j in range(JT):
            if j >= 2:
                sp.wait_ge(ctx_low, j - 1)
            load(j, 0)
        with sp.Fori(0, B) as b:
            for j in range(JT):
                sp.wait_ge(ctx_low, b * JT + (JT + j - (1 if j else 0)))
                load(j, (b + 1) % B)
        sp.wait_ge(ld[0], 16 * (JT // 2 + 1) * (B + 1))
        sp.wait_ge(ld[1], 16 * (JT // 2) * (B + 1))

    def split_high(act, j, turn):
        n = (JT // 2 + 1) if j % 2 == 0 else JT // 2
        act.wait_ge(ld[j % 2], turn * (16 * n) + 16 * (j // 2 + 1))
        w = rows(j)
        nc.scalar.activation(ctx[0][:, :, j * P:j * P + w],
                             stage[j % 2][:, :].rearrange("p (c n) -> p c n", n=P)[:, :, 0:w],
                             ACT.Copy).then_inc(ctx_high, 1)

    def split_low(dve, j, turn):
        dve.wait_ge(ctx_high, turn * JT + (j + 1))
        w = rows(j)
        nc.vector.tensor_tensor(ctx[1][:, :, j * P:j * P + w],
                                stage[j % 2][:, :].rearrange("p (c n) -> p c n", n=P)[:, :, 0:w],
                                ctx[0][:, :, j * P:j * P + w], ALU.subtract).then_inc(ctx_low, 1)

    @block.gpsimd
    def _(g):
        for i in range(2):
            g.memset(q_diag[i][:, :, :], 0.0).then_inc(zeroed, 1)
        g.wait_ge(zeroed, 2)
        with g.Fori(0, B) as b:
            g.wait_ge(s_ready, b * PAIRS + 2)
            for i in range(2):
                for h in range(2):
                    g.tensor_copy(q_diag[i][h * DH:(h + 1) * DH, :, h * S:(h + 1) * S],
                                  q_parts[h * DH:(h + 1) * DH, bass.ds(b, 1), i, :, :]
                                  .rearrange("p a c s -> p (a c) s")).then_inc(q_ready, 1)

    @block.tensor
    def _(pe):
        pe.sem_inc(s_ready, 2)
        pe.sem_inc(t_ready, 1)
        pe.sem_inc(av_done, 2)
        with pe.Fori(0, B) as b:
            for g in range(GROUPS):
                def bank_free(m):
                    pe.wait_ge(low_done, b * SEQ + (g * ITEMS + m + 1))

                def keys_of(p):
                    f = (g * GP + p) * P
                    for n in range(4):
                        m = 4 * p + n
                        bank_free(m)
                        lo, hi = chunk(n)
                        pe.wait_ge(ctx_low, b * JT + (hi + P - 1) // P)
                        o = bank(g * ITEMS + m)[:, 0:hi - lo]
                        for c in range(CC):
                            nc.tensor.matmul(o, w_kv[0][:, c, f:f + P], ctx[0][:, c, lo:hi], start=(c == 0), stop=False)
                            nc.tensor.matmul(o, w_kv[0][:, c, f:f + P], ctx[1][:, c, lo:hi], start=False, stop=False)
                            last = nc.tensor.matmul(o, w_kv[1][:, c, f:f + P], ctx[0][:, c, lo:hi], start=False,
                                                    stop=(c == CC - 1))
                        last.then_inc(prod_ready, 1)
                        if n == 1 and p:
                            scores_of(p - 1)

                def scores_of(p):
                    pe.wait_ge(low_done, b * SEQ + (g * ITEMS + 4 * p + 6))
                    pe.wait_ge(exp_done, b * PAIRS + (g * GP + p + 1))
                    if p == 0:
                        pe.wait_ge(q_ready, 4 * b + 4)
                    kh, kl = keys[p % 2]
                    f = g * GP + p
                    for n in range(4):
                        o = p_s[:, n * BANK:n * BANK + CUTS[n + 1] - CUTS[n]]
                        kk = slice(CUTS[n], CUTS[n + 1])
                        nc.tensor.matmul(o, q_diag[0][:, f, :], kh[:, kk], start=True, stop=False)
                        nc.tensor.matmul(o, q_diag[0][:, f, :], kl[:, kk], start=False, stop=False)
                        last = nc.tensor.matmul(o, q_diag[1][:, f, :], kh[:, kk], start=False, stop=True)
                    last.then_inc(s_ready, 1)

                def values_of(j):
                    m = 4 * GP + j
                    bank_free(m)
                    w, f = rows(j), HEADS * DH + g * GP * P
                    o = bank(g * ITEMS + m)[0:w, :]
                    cols = slice(j * P, j * P + w)
                    for c in range(CC):
                        nc.tensor.matmul(o, ctx[0][:, c, cols], w_kv[0][:, c, f:f + BANK], start=(c == 0), stop=False)
                        nc.tensor.matmul(o, ctx[0][:, c, cols], w_kv[1][:, c, f:f + BANK], start=False, stop=False)
                        last = nc.tensor.matmul(o, ctx[1][:, c, cols], w_kv[0][:, c, f:f + BANK], start=False,
                                                stop=(c == CC - 1))
                        if j == 0 and c == 1:
                            scores_of(GP - 1)
                    last.then_inc(prod_ready, 1)

                def transpose_of(j):
                    if j == 0:
                        pe.wait_ge(wl_done, b * PAIRS + ((g + 1) * GP + 1))
                    pe.wait_ge(pt_done, b * GROUPS * JT + (g * JT + j + 1))
                    w = rows(j) + (j == JT - 1)
                    for i in range(2):
                        for p in range(GP):
                            at = (i * GP + p) * P
                            last = nc.tensor.transpose(p_t[0:w, at:at + P], parts[:, i, p, j * P:j * P + w],
                                                       k.ident_f[:, :])
                    last.then_inc(t_ready, 1)

                def attend_to(j):
                    pe.wait_ge(low_done, b * SEQ + (g * ITEMS + 4 * GP + j + 3))
                    pe.wait_ge(pt_done, b * GROUPS * JT + (g * JT + j + 2))
                    w = rows(j) + (j == JT - 1)
                    for p in range(GP):
                        o, f = p_o[:, p * P:(p + 1) * P], slice(p * P, (p + 1) * P)
                        v = [v_last[i][0:w, g, f] if j == JT - 1 else vals[j % 2][i][:, f] for i in range(2)]
                        a = [pt[j % 2][0:w, (i * GP + p) * P:(i * GP + p + 1) * P] for i in range(2)]
                        nc.tensor.matmul(o, v[0], a[0], start=False, stop=False)
                        nc.tensor.matmul(o, v[0], a[1], start=False, stop=False)
                        last = nc.tensor.matmul(o, v[1], a[0], start=False, stop=(j == JT - 1 and p == GP - 1))
                    last.then_inc(av_done, 1)
                    if j == JT - 1:
                        pe.wait_ge(av_done, b * GROUPS * JT + ((g + 1) * JT + 2))
                        pe.sem_inc(o_ready, 1)

                for p in range(GP):
                    keys_of(p)
                pe.wait_ge(o_copied, b * GROUPS + (g + 1))
                nc.tensor.matmul(p_o[:, :], k.ident_f[0:1, :], k.ident_f[0:1, 1:2].to_broadcast([1, BANK]), start=True,
                                 stop=False)
                for j in range(JT + 2):
                    if j < JT:
                        values_of(j)
                    if 1 <= j <= JT:
                        transpose_of(j - 1)
                    if j >= 2:
                        attend_to(j - 2)

    @block.scalar
    def _(act):
        act.sem_inc(exp_done, 1)
        for j in range(JT):
            split_high(act, j, 0)
        with act.Fori(0, B) as b:
            for g in range(GROUPS):
                def high(m, out, w, parts):
                    act.wait_ge(prod_ready, b * SEQ + (g * ITEMS + m + 1))
                    nc.scalar.activation(out, bank(g * ITEMS + m)[0:parts, 0:w], ACT.Copy).then_inc(high_done, 1)

                def exps(p):
                    f = g * GP + p
                    act.wait_ge(max_done, b * PAIRS + (f + 1))
                    act.wait_ge(wl_done, b * PAIRS + (f + 1))
                    nc.scalar.activation(probs[:, 0:CUTS[2]].rearrange("p (a n) -> p a n", a=2), scores(0, 2),
                                         ACT.Exp, bias=nbias, scale=1.0 / (8 * W_UP),
                                         accum_out=rsum[:, 0:1])
                    nc.scalar.activation(probs[:, CUTS[2]:KEYS].rearrange("p (a n) -> p a n", a=2), scores(2, 4),
                                         ACT.Exp, bias=nbias, scale=1.0 / (8 * W_UP),
                                         accum_out=rsum[:, 1:2]).then_inc(exp_done, 1)

                def weights_high(p):
                    f = g * GP + p
                    if p == 0:
                        act.wait_ge(t_ready, b * GROUPS * JT + (g * JT + 1))
                    act.wait_ge(exp_done, b * PAIRS + (f + 2))
                    act.wait_ge(inv_done, b * PAIRS + (f + 1))
                    nc.scalar.activation(parts[:, 0, p, :], probs[:, :], ACT.Copy,
                                         scale=rinv).then_inc(wh_done, 1)

                for p in range(GP):
                    act.wait_ge(s_ready, b * PAIRS + (g * GP + p + 1))
                    for n in range(4):
                        lo, hi = chunk(n)
                        high(4 * p + n, keys[p % 2][0][:, lo:hi], hi - lo, P)
                        if n == 1 and p:
                            exps(p - 1)
                        if n == 3 and p:
                            weights_high(p - 1)
                exps(GP - 1)
                for j in range(JT):
                    act.wait_ge(av_done, b * GROUPS * JT + (g * JT + j + 1))
                    w = rows(j)
                    out = v_last[0][0:w, g, :] if j == JT - 1 else vals[j % 2][0][:, :]
                    high(4 * GP + j, out, BANK, w)
                    if j == 0:
                        weights_high(GP - 1)
                    if g == GROUPS - 1:
                        split_high(act, j, b + 1)

    @block.vector
    def _(dve):
        dve.sem_inc(low_done, 2)
        dve.sem_inc(wl_done, 1)
        dve.sem_inc(pt_done, 1)
        dve.sem_inc(o_copied, 1)
        for j in range(JT):
            split_low(dve, j, 0)
        with dve.Fori(0, B) as b:
            for g in range(GROUPS):
                def low(m, out, high, w, parts):
                    dve.wait_ge(high_done, b * SEQ + (g * ITEMS + m + 1))
                    nc.vector.tensor_tensor(out, bank(g * ITEMS + m)[0:parts, 0:w], high,
                                            ALU.subtract).then_inc(low_done, 1)

                def softmax(p):
                    f = g * GP + p
                    at = 3 * f
                    def step(i):
                        dve.wait_ge(dchain, b * (3 * PAIRS) + (at + i))
                    dve.wait_ge(s_ready, b * PAIRS + (f + 3))
                    nc.vector.tensor_reduce(peak[:, 0:1], scores(0, 2), AX.XY, ALU.max).then_inc(dchain, 1)
                    nc.vector.tensor_reduce(peak[:, 1:2], scores(2, 4), AX.XY, ALU.max).then_inc(dchain, 1)
                    step(2)
                    nc.vector.tensor_scalar(nbias, peak[:, 0:1], peak[:, 1:2], -1.0 / (8 * W_UP),
                                            ALU.max, ALU.mult).then_inc(max_done, 1)
                    dve.wait_ge(exp_done, b * PAIRS + (f + 2))
                    nc.vector.tensor_scalar(rsum[:, 0:1], rsum[:, 0:1], rsum[:, 1:2], 1.0 / P_UP, ALU.add,
                                            ALU.mult).then_inc(dchain, 1)
                    step(3)
                    nc.vector.reciprocal(rinv, rsum[:, 0:1]).then_inc(inv_done, 1)

                def weights_low(p):
                    f = g * GP + p
                    dve.wait_ge(inv_done, b * PAIRS + (f + 1))
                    dve.wait_ge(wh_done, b * PAIRS + (f + 1))
                    nc.vector.scalar_tensor_tensor(parts[:, 1, p, :], probs[:, :], rinv,
                                                   parts[:, 0, p, :], ALU.mult, ALU.subtract).then_inc(wl_done, 1)

                for p in range(GP):
                    for n in range(4):
                        lo, hi = chunk(n)
                        low(4 * p + n, keys[p % 2][1][:, lo:hi], keys[p % 2][0][:, lo:hi], hi - lo, P)
                        if n == 1 and p:
                            softmax(p - 1)
                        if n == 3 and p:
                            weights_low(p - 1)
                softmax(GP - 1)
                for j in range(JT + 1):
                    if j:
                        jj = j - 1
                        w = rows(jj) + (jj == JT - 1)
                        dve.wait_ge(t_ready, b * GROUPS * JT + (g * JT + jj + 2))
                        dve.wait_ge(av_done, b * GROUPS * JT + (g * JT + jj + (1 if jj else 2)))
                        nc.vector.tensor_copy(pt[jj % 2][0:w, :], p_t[0:w, :]).then_inc(pt_done, 1)
                    if j < JT:
                        w = rows(j)
                        out = [v_last[i][0:w, g, :] if j == JT - 1 else vals[j % 2][i][:, :] for i in range(2)]
                        low(4 * GP + j, out[1], out[0], BANK, w)
                    if j == 0:
                        weights_low(GP - 1)
                    if g == GROUPS - 1 and j < JT:
                        split_low(dve, j, b + 1)
                dve.wait_ge(o_ready, b * GROUPS + (g + 1))
                dve.wait_ge(q_ready, 4 * b + 4)
                for h in range(2):
                    ins = nc.vector.tensor_scalar(
                        o_t[h * DH:(h + 1) * DH, bass.ds(b, 1), g * GP:(g + 1) * GP, :].rearrange("p a c s -> p (a c) s"),
                        p_o[h * DH:(h + 1) * DH, :].rearrange("p (c h s) -> p c h s", h=2, s=S)[:, :, h, :],
                        1.0 / (W_UP * P_UP), None, ALU.mult)
                ins.then_inc(o_copied, 1)


def project_out(nc, io, k, x, o_t):
    with Stage(nc, "co") as st:
        w = st.sb("w", [P, PAIRS, D])
        scale, bias = st.sb("scale", [P, D]), st.sb("bias", [P, D])
        o = st.sb("o", [P, NT, D])
        heads = st.sb("heads", [P, PAIRS, TOK])
        stats, mv = st.sb("stats", [P, NT, 6]), st.sb("mv", [P, NT, 2])
        var, root = st.sb("var", [P, NT]), st.sb("root", [P, NT])
        p_out = st.ps("p_out", NT)
        ld_w, ld_b, moved, out_ready, var_ready, root_ready, chain = st.sems(
            "ld_w ld_b moved out_ready var_ready root_ready chain")
        block = st.block()

        @block.sync
        def _(sp):
            sp.dma_start(w[:, :, :], io.w_out).then_inc(ld_w, 16)
            sp.dma_start(scale[:, :], io.ln_scale.partition_broadcast(P)).then_inc(ld_b, 16)
            sp.dma_start(bias[:, :], io.ln_bias.partition_broadcast(P)).then_inc(ld_b, 16)

        @block.tensor
        def _(pe):
            pe.wait_ge(ld_w, 16)
            for t in range(NT):
                pe.wait_ge(moved, t + 1)
                for f in range(PAIRS):
                    last = nc.tensor.matmul(p_out[:, t * BANK:(t + 1) * BANK], heads[:, f, t * P:(t + 1) * P],
                                            w[:, f, :], start=(f == 0), stop=(f == PAIRS - 1))
                last.then_inc(out_ready, 1)

        @block.scalar
        def _(act):
            act.wait_ge(var_ready, 1)
            nc.scalar.activation(root[:, :], var[:, :], ACT.Sqrt).then_inc(root_ready, 1)

        @block.vector
        def _(dve):
            c = Chain(dve, chain)
            for t in range(NT):
                nc.vector.tensor_copy(heads[:, :, t * P:(t + 1) * P].rearrange("p c (b s) -> p b c s", b=2),
                                      o_t[:, 2 * t:2 * t + 2, :, :]).then_inc(moved, 1)
            for t in range(NT):
                dve.wait_ge(out_ready, t + 1)
                c.link(nc.vector.bn_stats(stats[:, t, :], p_out[:, t * BANK:(t + 1) * BANK]))
                c.mark(nc.vector.bn_aggr(mv[:, t, :], stats[:, t, :]))
            c.settle()
            nc.vector.tensor_scalar(var[:, :], mv[:, :, 1], 1e-6, None, ALU.add).then_inc(var_ready, 1)
            dve.wait_ge(root_ready, 1)
            c.link(nc.vector.reciprocal(var[:, :], root[:, :]))
            dve.wait_ge(ld_b, 32)
            for t in range(NT):
                c.mark(nc.vector.tensor_scalar(o[:, t, :], p_out[:, t * BANK:(t + 1) * BANK], mv[:, t, 0:1],
                                               var[:, t:t + 1], ALU.subtract, ALU.mult))
            c.settle()
            for t in range(NT):
                c.mark(nc.vector.tensor_tensor(o[:, t, :], o[:, t, :], scale[:, :], ALU.mult))
            c.settle()
            for t in range(NT):
                c.mark(nc.vector.tensor_tensor(o[:, t, :], o[:, t, :], bias[:, :], ALU.add))
            c.settle()
            for t in range(NT):
                c.mark(nc.vector.tensor_tensor(x[:, t, :], x[:, t, :], o[:, t, :], ALU.add))
            c.settle()


NH = 8
DEPTH = 3
CIRC = 4
NM = DEPTH * (NH - 1)
A_CT, A_ST, A_CP, A_SP, A_COL, A_2P, A_P, A_QW = (0, NM, 2 * NM, 3 * NM, 4 * NM, 4 * NM + 1, 4 * NM + 1 + DH,
                                                  4 * NM + 1 + 2 * DH)
NA = A_QW + CIRC
GT = P // NH
NG = TOK // GT
GB = BANK // P
OG = BANK // DH


def head_of(state, u):
    return state[:, u // NH, :, u % NH, :]


def grouped(v):
    return v.rearrange("p (g t) -> p g t", t=GT)


def head_attention(nc, io, k, x, xn, xt):
    with Stage(nc, "ha") as st:
        h = Namespace()
        h.state = st.sb("state", [P, 2, NG, NH, GT])
        h.vhat = st.sb("vhat", [P, NG, DH])
        h.trig = st.sb("trig", [P, NA])
        h.rot = st.sb("rot", [P, NM, P])
        h.same = st.sb("same", [P, P])
        h.turn = st.sb("turn", [P, P])
        h.kappa = st.sb("kappa", [P, CIRC])
        h.sup = st.sb("sup", [P, CIRC])
        with Stage(nc, "hw") as early:
            w_qk = early.sb("w_qk", [P, DC, 2 * NH, 2, DH])
            ld_w = early.sem("ld_w")

            def load(sp):
                for c in range(DC):
                    sp.dma_start(w_qk[:, c, :, :, :], io.w_qk[:, c, :, :, :]).then_inc(ld_w, 16)

            norm_transpose(nc, "n4", x, xn, xt, k.ident, 1e-5, load=load)
            head_project(nc, io, k, h, xt, w_qk, ld_w)
        entangle(nc, k, h)
        h.own = st.sb("own", [P, GT])
        h.own_all = st.sb("own_all", [P, P])
        h.pat = st.sb("pat", [P, NG, NH])
        head_scores(nc, k, h)
        head_mix(nc, io, k, h, x, xn, xt)


def head_project(nc, io, k, h, xt, w_qk, ld_w):
    HALF_PI, TWO_PI = math.pi / 2, 2 * math.pi
    BIG = 6.28125
    with Stage(nc, "hp") as st:
        w_v = st.sb("w_v", [P, DC, D])
        vt = st.sb("vt", [DH, NG, NH, GT])
        b_qk = st.sb("b_qk", [P, 2 * NH])
        b_v = st.sb("b_v", [DH, NH])
        rows = st.sb("rows", [P, 2 * NM + DH + 2 * CIRC])
        phase = st.sb("phase", [P, 1])
        shift = st.sb("shift", [P, 1])
        swap = st.sb("swap", [P, P])
        head_col = st.sb("head_col", [DH, 2 * 2 * NH - 1])
        ang, turns = st.sb("ang", [P, NA]), st.sb("turns", [P, NA])
        coef = st.sb("coef", [P, 6, NM])
        dv = st.sb("dv", [P, NM])
        small = st.sb("small", [P, 4 * CIRC])
        sq = [st.sb(f"sq{i}", [P, TOK]) for i in range(2)]
        root = st.sb("root", [2 * NH, 2, TOK])
        inv = st.sb("inv", [2 * NH, 3, TOK], bf16)
        vsq = st.sb("vsq", [P, NG, DH])
        vlen = st.sb("vlen", [P, 3, NG])
        p_p, p_n, p_r = st.ps("p_p", 4), st.ps("p_n"), st.ps("p_r", 2)
        ld_v, ld_s, made, p_ready, raw_done, sq_done, n_ready, root_done, split, r_ready, scaled, ang_ready, \
            trig_done, v_done, vt_ready, v_copied, vl_ready, vl_root, chain, gc, sup_max, sup_exp = st.sems(
                "ld_v ld_s made p_ready raw_done sq_done n_ready root_done split r_ready scaled ang_ready "
                "trig_done v_done vt_ready v_copied vl_ready vl_root chain gc sup_max sup_exp")
        block = st.block()

        @block.sync
        def _(sp):
            sp.dma_start(b_qk[:, :], io.b_qk).then_inc(ld_s, 16)
            sp.dma_start(rows[:, :], io.head_rows.partition_broadcast(P)).then_inc(ld_s, 16)
            sp.dma_start(phase[:, :], io.phase).then_inc(ld_s, 16)
            sp.dma_start(w_v[:, :, :], io.w_v).then_inc(ld_v, 16)
            sp.dma_start(b_v[:, :], io.b_v).then_inc(ld_v, 16)

        @block.gpsimd
        def _(g):
            c = Chain(g, gc)
            for m in (h.same, h.turn, swap, head_col):
                c.mark(g.memset(m[:, :], 0.0))
            c.settle()

            def diagonal(m, offset, value):
                c.link(g.affine_select(out=m[:, :], in_=m[:, :], compare_op=ALU.not_equal, fill=value,
                                       base=offset, pattern=[[-1, m.shape[1]]], channel_multiplier=1))

            for offset in (0, DH, -DH):
                diagonal(h.same, offset, 1.0)
            for offset in (DH, -DH):
                diagonal(swap, offset, 1.0)
            diagonal(h.turn, -DH, 1.0)
            diagonal(h.turn, DH, -1.0)
            c.link(g.memset(head_col[:, 2 * NH - 1:2 * NH], 1.0))
            g.sem_inc(made, 1)

        @block.tensor
        def _(pe):
            def norm_part(u):
                pe.wait_ge(sq_done, u + 1)
                ins = nc.tensor.matmul(p_n[0:2 * NH, :], head_col[:, 2 * NH - 1 - u:4 * NH - 1 - u],
                                       sq[u % 2][0:DH, :], start=(u == 0), stop=(u == 2 * NH - 1))
                ins.then_inc(n_ready, 1)

            pe.wait_ge(ld_w, 16 * DC)
            pe.wait_ge(made, 1)
            for u in range(2 * NH):
                if u >= 4:
                    pe.wait_ge(raw_done, u - 3)
                for c in range(DC):
                    last = nc.tensor.matmul(p_p[:, (u % 4) * BANK:(u % 4 + 1) * BANK],
                                            w_qk[:, c, u, :, :].rearrange("p i d -> p (i d)"), xt[:, c, :],
                                            start=(c == 0), stop=(c == DC - 1))
                last.then_inc(p_ready, 1)
                if u:
                    norm_part(u - 1)
            norm_part(2 * NH - 1)
            pe.wait_ge(ld_v, 32)
            for j in range(NH):
                if j < 4:
                    pe.wait_ge(raw_done, 2 * NH - 3 + j)
                else:
                    pe.wait_ge(v_done, j - 3)
                for c in range(DC):
                    last = nc.tensor.matmul(p_p[0:DH, (j % 4) * BANK:(j % 4 + 1) * BANK],
                                            w_v[:, c, j * DH:(j + 1) * DH], xt[:, c, :],
                                            start=(c == 0), stop=(c == DC - 1))
                last.then_inc(p_ready, 1)
            pe.wait_ge(v_done, NH)
            for g in range(NG):
                ins = nc.tensor.transpose(p_p[:, g * DH:(g + 1) * DH], vt[:, g, :, :].rearrange("p h t -> p (h t)"),
                                          k.ident[0:DH, 0:DH])
                if g % OG == OG - 1:
                    ins.then_inc(vt_ready, 1)
            pe.wait_ge(split, 5)
            for u in range(2 * NH):
                if u >= 2:
                    pe.wait_ge(scaled, u - 1)
                for i in range(3):
                    last = nc.tensor.matmul(p_r[:, (u % 2) * BANK:(u % 2 + 1) * BANK],
                                            k.ident_h[0:2 * NH, u:u + 1].to_broadcast([2 * NH, P]), inv[:, i, :],
                                            start=(i == 0), stop=(i == 2))
                last.then_inc(r_ready, 1)

        @block.scalar
        def _(act):
            act.wait_ge(ld_s, 48)
            act.wait_ge(ang_ready, 1)
            nc.scalar.activation(h.trig[:, :], ang[:, :], ACT.Sin).then_inc(trig_done, 1)
            for u in range(2 * NH):
                act.wait_ge(p_ready, u + 1)
                nc.scalar.activation(head_of(h.state, u), grouped(p_p[:, (u % 4) * BANK:(u % 4 + 1) * BANK]), ACT.Identity,
                                     bias=b_qk[:, u:u + 1]).then_inc(raw_done, 1)
                act.wait_ge(raw_done, u + 1)
                if u >= 2:
                    act.wait_ge(n_ready, u - 1)
                nc.scalar.activation(grouped(sq[u % 2][:, :]), head_of(h.state, u), ACT.Square).then_inc(sq_done, 1)
            for j in range(NH):
                act.wait_ge(p_ready, 2 * NH + j + 1)
                nc.scalar.activation(vt[:, :, j, :], grouped(p_p[0:DH, (j % 4) * BANK:(j % 4 + 1) * BANK]), ACT.Identity,
                                     bias=b_v[:, j:j + 1]).then_inc(v_done, 1)
            for q in range(NG // OG):
                act.wait_ge(vt_ready, q + 1)
                nc.scalar.activation(h.vhat[:, q * OG:(q + 1) * OG, :].rearrange("p g d -> p (g d)"),
                                     p_p[:, q * BANK:(q + 1) * BANK], ACT.Copy).then_inc(v_copied, 1)
            act.wait_ge(sup_max, 1)
            nc.scalar.activation(small[:, CIRC:2 * CIRC], rows[:, 2 * NM + DH + CIRC:], ACT.Exp,
                                 bias=small[:, 0:1]).then_inc(sup_exp, 1)
            act.wait_ge(n_ready, 2 * NH)
            nc.scalar.activation(root[:, 0, :], p_n[0:2 * NH, :], ACT.Sqrt).then_inc(root_done, 1)
            act.wait_ge(vl_ready, 1)
            nc.scalar.activation(vlen[:, 1, :], vlen[:, 0, :], ACT.Sqrt).then_inc(vl_root, 1)

        @block.vector
        def _(dve):
            c = Chain(dve, chain)
            dve.wait_ge(ld_s, 48)
            dve.wait_ge(made, 1)
            c.mark(nc.vector.memset(shift[0:DH, :], HALF_PI))
            c.mark(nc.vector.memset(shift[DH:P, :], 0.0))
            c.settle()
            th, ph = rows[:, 0:NM], rows[:, NM:2 * NM]
            fr = rows[:, 2 * NM:2 * NM + DH]
            for at, v, n, scale, add in ((A_CT, th, NM, 0.5, HALF_PI), (A_ST, th, NM, 0.5, 0.0),
                                         (A_CP, ph, NM, 1.0, HALF_PI), (A_SP, ph, NM, 1.0, 0.0),
                                         (A_2P, fr, DH, 2.0, HALF_PI), (A_P, fr, DH, 1.0, HALF_PI),
                                         (A_QW, rows[:, 2 * NM + DH:2 * NM + DH + CIRC], CIRC, 1.0, 0.0),
                                         (A_COL, phase[:, :], 1, 1.0, shift[:, 0:1])):
                c.mark(nc.vector.tensor_scalar(ang[:, at:at + n], v, scale, add, ALU.mult, ALU.add))
            c.settle()
            c.link(nc.vector.tensor_scalar(turns[:, :], ang[:, :], 1.0 / TWO_PI, ROUND, ALU.mult, ALU.add))
            c.link(nc.vector.tensor_scalar(turns[:, :], turns[:, :], -ROUND, None, ALU.add))
            c.link(nc.vector.scalar_tensor_tensor(ang[:, :], turns[:, :], -BIG, ang[:, :], ALU.mult, ALU.add))
            c.link(nc.vector.scalar_tensor_tensor(ang[:, :], turns[:, :], BIG - TWO_PI, ang[:, :], ALU.mult, ALU.add))
            nc.vector.tensor_scalar(ang[:, :], ang[:, :], 3.1415925, -3.1415925, ALU.min, ALU.max).then_inc(ang_ready, 1)
            c.link(nc.vector.tensor_reduce(small[:, 0:1], rows[:, 2 * NM + DH + CIRC:], AX.X, ALU.max, negate=True))
            dve.sem_inc(sup_max, 1)
            dve.wait_ge(trig_done, 1)
            tr = h.trig
            st_, cp, sp_ = tr[:, A_ST:A_ST + NM], tr[:, A_CP:A_CP + NM], tr[:, A_SP:A_SP + NM]
            c.mark(nc.vector.tensor_scalar(coef[:, 0, :], tr[:, A_CT:A_CT + NM], -1.0, None, ALU.add))
            c.mark(nc.vector.tensor_tensor(coef[:, 1, :], st_, cp, ALU.mult))
            c.mark(nc.vector.tensor_tensor(coef[:, 2, :], st_, sp_, ALU.mult))
            c.settle()
            c.mark(nc.vector.tensor_tensor(dv[0:DH, :], coef[0:DH, 0, :], coef[0:DH, 1, :], ALU.add))
            c.mark(nc.vector.tensor_tensor(dv[DH:P, :], coef[DH:P, 0, :], coef[DH:P, 1, :], ALU.subtract))
            c.settle()
            for m in range(NM):
                c.mark(nc.vector.tensor_scalar(h.rot[:, m, :], k.ident[:, :], dv[:, m:m + 1], None, ALU.mult))
            c.settle()
            for m in range(NM):
                c.mark(nc.vector.scalar_tensor_tensor(h.rot[:, m, :], swap[:, :], coef[:, 2, m:m + 1], h.rot[:, m, :],
                                                      ALU.mult, ALU.add))
            c.mark(nc.vector.tensor_scalar(small[:, 2 * CIRC:3 * CIRC], tr[:, A_QW:A_QW + CIRC], 0.3, 0.5, ALU.mult, ALU.add))
            c.mark(nc.vector.tensor_scalar(small[:, 3 * CIRC:4 * CIRC], tr[:, A_QW:A_QW + CIRC], -0.3, 0.5, ALU.mult, ALU.add))
            c.settle()
            c.mark(nc.vector.scalar_tensor_tensor(h.kappa[:, :], small[:, 2 * CIRC:3 * CIRC], DH**-0.5,
                                                  small[:, 3 * CIRC:4 * CIRC], ALU.mult, ALU.mult))
            dve.wait_ge(sup_exp, 1)
            c.link(nc.vector.tensor_reduce(small[:, 0:1], small[:, CIRC:2 * CIRC], AX.X, ALU.add))
            c.link(nc.vector.reciprocal(small[:, 1:2], small[:, 0:1]))
            c.mark(nc.vector.tensor_scalar(h.sup[:, :], small[:, CIRC:2 * CIRC], small[:, 1:2], None, ALU.mult))
            for q in range(NG // OG):
                dve.wait_ge(v_copied, q + 1)
                v = h.vhat[:, q * OG:(q + 1) * OG, :]
                c.mark(nc.vector.tensor_tensor(vsq[:, q * OG:(q + 1) * OG, :], v, v, ALU.mult))
            c.settle()
            nc.vector.tensor_reduce(vlen[:, 0, :], vsq[:, :, :], AX.X, ALU.add).then_inc(vl_ready, 1)
            dve.wait_ge(root_done, 1)
            c.link(nc.vector.tensor_scalar(root[:, 0, :], root[:, 0, :], 1e-12, None, ALU.max))
            c.link(nc.vector.reciprocal(root[:, 1, :], root[:, 0, :]))
            for i in range(3):
                if i:
                    nc.vector.tensor_tensor(root[:, 1, :], root[:, 1, :], inv[:, i - 1, :],
                                            ALU.subtract).then_inc(split, 1)
                    dve.wait_ge(split, 2 * i)
                nc.vector.tensor_copy(inv[:, i, :], root[:, 1, :]).then_inc(split, 1)
                dve.wait_ge(split, 2 * i + 1)
            dve.wait_ge(vl_root, 1)
            c.link(nc.vector.tensor_scalar(vlen[:, 0, :], vlen[:, 1, :], 1e-12, None, ALU.max))
            c.link(nc.vector.reciprocal(vlen[:, 2, :], vlen[:, 0, :]))
            vh = h.vhat[:, :, :]
            c.mark(nc.vector.tensor_tensor(vh, vh, vlen[:, 2, :].unsqueeze(2).to_broadcast([P, NG, DH]), ALU.mult))
            for u in range(2 * NH):
                dve.wait_ge(r_ready, u + 1)
                nc.vector.scalar_tensor_tensor(head_of(h.state, u), head_of(h.state, u), h.trig[:, A_COL:A_COL + 1],
                                               grouped(p_r[:, (u % 2) * BANK:(u % 2 + 1) * BANK]), ALU.mult,
                                               ALU.mult).then_inc(scaled, 1)
            dve.wait_ge(scaled, 2 * NH)
            c.settle()


def entangle(nc, k, h):
    with Stage(nc, "he") as st:
        sq = [st.sb(f"sq{i}", [P, TOK]) for i in range(2)]
        ctrl = [st.sb(f"ctrl{i}", [P, TOK]) for i in range(2)]
        part = [st.sb(f"part{i}", [P, TOK]) for i in range(2)]
        p_c, p_d = st.ps("p_c", 2), st.ps("p_d", 2)
        sq_done, c_ready, d_ready, ctrl_done, part_done, new_done = st.sems(
            "sq_done c_ready d_ready ctrl_done part_done new_done")
        block = st.block()
        units = [(g, i, s * NH + i) for g in range(DEPTH) for i in range(NH - 1) for s in range(2)]

        @block.scalar
        def _(act):
            def square(n):
                u = units[n][2]
                if n >= 2:
                    act.wait_ge(c_ready, n - 1)
                if n >= 2 * (NH - 1):
                    act.wait_ge(new_done, n - 2 * (NH - 1) + 1)
                nc.scalar.activation(grouped(sq[n % 2][:, :]), head_of(h.state, u), ACT.Square).then_inc(sq_done, 1)

            square(0)
            for n in range(len(units)):
                if n + 1 < len(units):
                    square(n + 1)
                act.wait_ge(c_ready, n + 1)
                if n >= 2:
                    act.wait_ge(part_done, n - 1)
                nc.scalar.activation(ctrl[n % 2][:, :], p_c[:, (n % 2) * BANK:(n % 2 + 1) * BANK],
                                     ACT.Copy).then_inc(ctrl_done, 1)

        @block.tensor
        def _(pe):
            for n, (g, i, u) in enumerate(units):
                o = slice((n % 2) * BANK, (n % 2 + 1) * BANK)
                pe.wait_ge(sq_done, n + 1)
                if n >= 2:
                    pe.wait_ge(part_done, n - 1)
                nc.tensor.matmul(p_c[:, o], h.same[:, :], sq[n % 2][:, :], start=True, stop=True).then_inc(c_ready, 1)
                if g and i < NH - 2:
                    pe.wait_ge(new_done, n - 2 * (NH - 1) + 3)
                nc.tensor.matmul(p_d[:, o], h.rot[:, g * (NH - 1) + i, :], head_of(h.state, u + 1), start=True,
                                 stop=True).then_inc(d_ready, 1)

        @block.vector
        def _(dve):
            for n, (g, i, u) in enumerate(units):
                o = slice((n % 2) * BANK, (n % 2 + 1) * BANK)
                dve.wait_ge(ctrl_done, n + 1)
                dve.wait_ge(d_ready, n + 1)
                if n >= 2:
                    dve.wait_ge(new_done, n - 1)
                nc.vector.tensor_tensor(part[n % 2][:, :], ctrl[n % 2][:, :], p_d[:, o], ALU.mult).then_inc(part_done, 1)
                dve.wait_ge(part_done, n + 1)
                nc.vector.tensor_tensor(head_of(h.state, u), grouped(part[n % 2][:, :]), head_of(h.state, u + 1),
                                        ALU.add).then_inc(new_done, 1)
            dve.wait_ge(new_done, len(units))


def head_scores(nc, k, h):
    with Stage(nc, "hs") as st:
        turned = st.sb("turned", [P, NG, NH, GT])
        picked = [st.sb(f"picked{i}", [P, GB, NH, GT]) for i in range(2)]
        part = st.sb("part", [P, 2, NG, NH])
        p_k, p_s = st.ps("p_k", 2), st.ps("p_s", 4)
        made, t_ready, turned_done, s_ready, picked_done, summed, sq_done, gc = st.sems(
            "made t_ready turned_done s_ready picked_done summed sq_done gc")
        block = st.block()
        units = [(s, n) for s in range(2) for n in range(NG // GB)]

        @block.gpsimd
        def _(g):
            c = Chain(g, gc)
            c.link(g.memset(h.own[:, :], 0.0))
            for i in range(NH):
                c.link(g.affine_select(out=h.own[:, :], in_=h.own[:, :], compare_op=ALU.not_equal, fill=1.0,
                                       base=-i * GT, pattern=[[-1, GT]], channel_multiplier=1))
            g.sem_inc(made, 1)
            c.link(g.tensor_copy(h.own_all[:, :].rearrange("p (i t) -> p i t", t=GT),
                                 h.own[:, :].unsqueeze(1).to_broadcast([P, NH, GT])))

        @block.tensor
        def _(pe):
            def score(n):
                s, q = units[n]
                if n >= 4:
                    pe.wait_ge(picked_done, n - 3)
                for g in range(q * GB, (q + 1) * GB):
                    keys = turned[:, g, :, :] if s else h.state[:, 1, g, :, :]
                    at = (n % 4) * BANK + g % GB * P
                    last = nc.tensor.matmul(p_s[:, at:at + P], h.state[:, 0, g, :, :].rearrange("p h t -> p (h t)"),
                                            keys.rearrange("p h t -> p (h t)"), start=True, stop=True)
                last.then_inc(s_ready, 1)

            for n in range(NH):
                if n >= 2:
                    pe.wait_ge(turned_done, n - 1)
                nc.tensor.matmul(p_k[:, (n % 2) * BANK:(n % 2 + 1) * BANK], h.turn[:, :], head_of(h.state, NH + n),
                                 start=True, stop=True).then_inc(t_ready, 1)
                score(n)
            pe.wait_ge(turned_done, NH)
            for n in range(NH, len(units)):
                score(n)

        @block.scalar
        def _(act):
            for j in range(NH):
                act.wait_ge(t_ready, j + 1)
                nc.scalar.activation(turned[:, :, j, :], grouped(p_k[:, (j % 2) * BANK:(j % 2 + 1) * BANK]),
                                     ACT.Copy).then_inc(turned_done, 1)
            act.wait_ge(summed, len(units))
            nc.scalar.activation(part[:, :, :, :], part[:, :, :, :], ACT.Square).then_inc(sq_done, 1)

        @block.vector
        def _(dve):
            dve.wait_ge(made, 1)
            for n, (s, q) in enumerate(units):
                dve.wait_ge(s_ready, n + 1)
                if n >= 2:
                    dve.wait_ge(summed, n - 1)
                nc.vector.tensor_tensor(picked[n % 2][:, :, :, :].rearrange("p g j t -> p (g j) t"),
                                        p_s[:, (n % 4) * BANK:(n % 4 + 1) * BANK].rearrange("p (n t) -> p n t", t=GT),
                                        h.own[:, :].unsqueeze(1).to_broadcast([P, GB * NH, GT]),
                                        ALU.mult).then_inc(picked_done, 1)
                dve.wait_ge(picked_done, n + 1)
                nc.vector.tensor_reduce(part[:, s, q * GB:(q + 1) * GB, :], picked[n % 2][:, :, :, :], AX.X,
                                        ALU.add).then_inc(summed, 1)
            dve.wait_ge(sq_done, 1)
            nc.vector.tensor_tensor(h.pat[:, :, :], part[:, 0, :, :], part[:, 1, :, :], ALU.add).then_inc(sq_done, 1)
            dve.wait_ge(sq_done, 2)


def head_mix(nc, io, k, h, x, xn, xt):
    with Stage(nc, "hm") as st:
        w_o = st.sb("w_o", [DH, NH, D])
        b_o = st.sb("b_o", [1, D])
        top = st.sb("top", [P, NG])
        diff = st.sb("diff", [P, NG, NH])
        wgt = st.sb("wgt", [P, CIRC, NG, NH])
        tot = st.sb("tot", [P, 2, CIRC * NG])
        tiny = st.sb("tiny", [P, CIRC])
        vsum, vsign, vsq, face = [st.sb(n, [P, NG, DH]) for n in "vsum vsign vsq face".split()]
        wide = [st.sb(f"wide{i}", [P, GB, NH, GT]) for i in range(3)]
        wide_t = [st.sb(f"wide_t{i}", [P, GB, P]) for i in range(2)]
        size, sign, clip, none = [[st.sb(f"{n}{i}", [P, D]) for i in range(2)] for n in "size sign clip none".split()]
        acc, acc_none = st.sb("acc", [P, NT, D]), st.sb("acc_none", [P, NT, D])
        y_t = st.sb("y_t", [DH, NH, TOK])
        p_w, p_x, p_t, p_out = st.ps("p_w", 2), st.ps("p_x", 2), st.ps("p_t", 2), st.ps("p_out", 2)
        ld_w, exp_done, w_ready, root_done, vs_ready, vs_copied, signed, squared, faced, wide_done, wt_ready, wt_done, mixed, \
            sized, clipped, noned, added, y_ready, yt_ready, yt_copied, out_ready, chain, diffed, gc, out_done, \
            tiny_done = st.sems(
                "ld_w exp_done w_ready root_done vs_ready vs_copied signed squared faced wide_done wt_ready wt_done mixed "
                "sized clipped noned added y_ready yt_ready yt_copied out_ready chain diffed gc out_done tiny_done")
        wide_pool, half_mixed = st.sems("wide_pool half_mixed")
        block = st.block()
        units = [(t, c) for t in range(NT) for c in range(CIRC)]
        HALVES = OG // GB
        halves = [(t, c, a) for t, c in units for a in range(HALVES)]
        on_pool = [m for m in range(len(halves)) if m % 4 == 3]
        on_dve = [m for m in range(len(halves)) if m % 4 != 3]

        @block.sync
        def _(sp):
            sp.dma_start(w_o[:, :, :], io.w_o).then_inc(ld_w, 16)
            sp.dma_start(b_o[:, :], io.b_o).then_inc(ld_w, 16)

        def spread(eng, m, out):
            t, c, a = halves[m]
            g = t * OG + a * GB
            return eng.tensor_tensor(out[:, :, :, :].rearrange("p g j t -> p (g j) t"),
                                     wgt[:, c, g:g + GB, :].rearrange("p g j -> p (g j)").unsqueeze(2)
                                     .to_broadcast([P, GB * NH, GT]),
                                     h.own[:, :].unsqueeze(1).to_broadcast([P, GB * NH, GT]), ALU.mult)

        def wide_of(m):
            return wide[2] if m in on_pool else wide[on_dve.index(m) % 2]

        @block.vector
        def _(dve):
            c = Chain(dve, chain)
            c.link(nc.vector.tensor_reduce(top[:, :], h.pat[:, :, :], AX.X, ALU.max))
            nc.vector.tensor_tensor(diff[:, :, :], h.pat[:, :, :], top[:, :].unsqueeze(2).to_broadcast([P, NG, NH]),
                                    ALU.subtract).then_inc(diffed, 1)
            nc.vector.tensor_scalar(tiny[:, :], h.sup[:, :], 1e-6, None, ALU.mult).then_inc(tiny_done, 1)
            dve.wait_ge(tiny_done, 1)
            dve.wait_ge(exp_done, CIRC)
            wf = wgt[:, :, :, :].rearrange("p c g j -> p (c g) j")
            c.link(nc.vector.tensor_reduce(tot[:, 0, :], wf, AX.X, ALU.add))
            c.link(nc.vector.reciprocal(tot[:, 1, :], tot[:, 0, :]))
            c.link(nc.vector.tensor_tensor(wf, wf, tot[:, 1, :].unsqueeze(2).to_broadcast([P, CIRC * NG, NH]), ALU.mult))
            nc.vector.tensor_scalar(wf, wf, 1e-12, None, ALU.add).then_inc(w_ready, 1)
            dve.wait_ge(root_done, 1)

            def finish(n):
                t, ci = units[n]
                dve.wait_ge(sized, 2 * n + 2)
                if n >= 2:
                    dve.wait_ge(added, 2 * n - 2)
                nc.vector.tensor_scalar(none[n % 2][:, :], size[n % 2][:, :], 0.0, tiny[:, ci:ci + 1], ALU.is_equal,
                                        ALU.mult).then_inc(noned, 1)
                c.link(nc.vector.tensor_scalar(clip[n % 2][:, :], size[n % 2][:, :], 1e-6, 1.0, ALU.max, ALU.min))
                nc.vector.scalar_tensor_tensor(clip[n % 2][:, :], clip[n % 2][:, :], h.sup[:, ci:ci + 1],
                                               sign[n % 2][:, :], ALU.mult, ALU.mult).then_inc(clipped, 1)
                if ci == CIRC - 1:
                    dve.wait_ge(added, 2 * n + 2)
                    dve.wait_ge(faced, 4)
                    a = acc[:, t, :].rearrange("p (g d) -> p g d", d=DH)
                    c.link(nc.vector.tensor_tensor(a, a, face[:, t * OG:(t + 1) * OG, :], ALU.mult))
                    nc.vector.tensor_tensor(acc[:, t, :], acc[:, t, :], acc_none[:, t, :], ALU.add).then_inc(y_ready, 1)

            for m in range(len(halves)):
                if m in on_dve:
                    if on_dve.index(m) >= 2:
                        dve.wait_ge(wt_ready, on_dve[on_dve.index(m) - 2] + 1)
                    spread(nc.vector, m, wide_of(m)).then_inc(wide_done, 1)
                if m % HALVES == HALVES - 1 and m >= 3 * HALVES:
                    finish(m // HALVES - 3)
            for n in range(len(units) - 3, len(units)):
                finish(n)
            for t in range(NT):
                dve.wait_ge(out_ready, t + 1)
                nc.vector.tensor_tensor(x[:, t, :], x[:, t, :], p_out[:, (t % 2) * BANK:(t % 2 + 1) * BANK],
                                        ALU.add).then_inc(out_done, 1)
            dve.wait_ge(out_done, NT)

        def total(g, n):
            t, b = units[n][0], n % 2
            if n >= 1:
                g.wait_ge(added, 2 * n)
            g.wait_ge(noned, n + 1)
            g.tensor_tensor(acc_none[:, t, :], acc_none[:, t, :], none[b][:, :], ALU.add).then_inc(added, 1)
            g.wait_ge(clipped, n + 1)
            g.tensor_tensor(acc[:, t, :], acc[:, t, :], clip[b][:, :], ALU.add).then_inc(added, 1)

        @block.gpsimd
        def _(g):
            g.memset(acc[:, :, :], 0.0).then_inc(gc, 1)
            g.memset(acc_none[:, :, :], 0.0).then_inc(gc, 1)
            g.wait_ge(gc, 2)
            g.wait_ge(root_done, 1)

            def spread_next(m):
                i = on_pool.index(m)
                if i:
                    g.wait_ge(wt_ready, on_pool[i - 1] + 1)
                spread(g, m, wide_of(m)).then_inc(wide_pool, 1)

            def face_step(i):
                if i == 0:
                    g.wait_ge(signed, 1)
                    g.tensor_tensor(vsum[:, :, :], vsign[:, :, :],
                                    h.trig[:, A_2P:A_2P + DH].unsqueeze(1).to_broadcast([P, NG, DH]), ALU.mult)\
                        .then_inc(faced, 1)
                elif i == 1:
                    g.wait_ge(squared, 1)
                    g.tensor_scalar(vsq[:, :, :], vsq[:, :, :], -1.0, 1.0, ALU.mult, ALU.add).then_inc(faced, 1)
                elif i == 2:
                    g.wait_ge(faced, 2)
                    g.tensor_tensor(vsq[:, :, :], vsq[:, :, :],
                                    h.trig[:, A_P:A_P + DH].unsqueeze(1).to_broadcast([P, NG, DH]), ALU.mult)\
                        .then_inc(faced, 1)
                elif i == 3:
                    g.wait_ge(faced, 3)
                    g.tensor_tensor(face[:, :, :], vsum[:, :, :], vsq[:, :, :], ALU.add).then_inc(faced, 1)

            for n in range(len(units)):
                for m in range(n * HALVES, (n + 1) * HALVES):
                    if m in on_pool:
                        spread_next(m)
                face_step(n)
                if n >= 3:
                    total(g, n - 3)
            for n in range(len(units) - 3, len(units)):
                total(g, n)

        @block.scalar
        def _(act):
            act.wait_ge(diffed, 1)
            for c in range(CIRC):
                nc.scalar.activation(wgt[:, c, :, :], diff[:, :, :], ACT.Exp,
                                     scale=h.kappa[:, c:c + 1]).then_inc(exp_done, 1)
            for q in range(NT):
                act.wait_ge(vs_ready, q + 1)
                nc.scalar.activation(vsign[:, q * OG:(q + 1) * OG, :].rearrange("p g d -> p (g d)"),
                                     p_x[:, (q % 2) * BANK:(q % 2 + 1) * BANK], ACT.Sign).then_inc(vs_copied, 1)
            act.wait_ge(vs_copied, NT)
            nc.scalar.activation(vsq[:, :, :], vsign[:, :, :], ACT.Square).then_inc(squared, 1)
            act.sem_inc(signed, 1)
            act.wait_ge(w_ready, 1)
            wf = wgt[:, :, :, :].rearrange("p c g j -> p (c g j)")
            nc.scalar.activation(wf, wf, ACT.Sqrt).then_inc(root_done, 1)

            def sizes(n):
                act.wait_ge(mixed, n + 1)
                if n >= 2:
                    act.wait_ge(clipped, n - 1)
                o = p_w[:, (n % 2) * BANK:(n % 2 + 1) * BANK]
                nc.scalar.activation(size[n % 2][:, :], o, ACT.Abs).then_inc(sized, 1)
                nc.scalar.activation(sign[n % 2][:, :], o, ACT.Sign).then_inc(sized, 1)

            for m in range(len(halves)):
                act.wait_ge(wt_ready, m + 1)
                if m >= 2:
                    act.wait_ge(half_mixed, m - 1)
                nc.scalar.activation(wide_t[m % 2][:, :, :], p_x[:, (m % 2) * BANK:(m % 2 + 1) * BANK]
                                     .rearrange("p (g n) -> p g n", n=P), ACT.Copy).then_inc(wt_done, 1)
                if m % HALVES == 1 and m >= HALVES:
                    sizes(m // HALVES - 1)
            sizes(len(units) - 1)
            for q in range(NG // GB):
                act.wait_ge(yt_ready, q + 1)
                nc.scalar.activation(y_t[:, :, q * GB * GT:(q + 1) * GB * GT].rearrange("p i (g t) -> p g i t", t=GT),
                                     p_t[0:DH, (q % 2) * BANK:(q % 2 + 1) * BANK]
                                     .rearrange("p (g i t) -> p g i t", i=NH, t=GT), ACT.Copy).then_inc(yt_copied, 1)

        @block.tensor
        def _(pe):
            for q in range(NT):
                if q >= 2:
                    pe.wait_ge(vs_copied, q - 1)
                nc.tensor.matmul(p_x[:, (q % 2) * BANK:(q % 2 + 1) * BANK], h.own_all[:, :],
                                 h.vhat[:, q * OG:(q + 1) * OG, :].rearrange("p g d -> p (g d)"), start=True,
                                 stop=True).then_inc(vs_ready, 1)
            pe.wait_ge(vs_copied, NT)

            def transpose(m):
                if m in on_pool:
                    pe.wait_ge(wide_pool, on_pool.index(m) + 1)
                else:
                    pe.wait_ge(wide_done, on_dve.index(m) + 1)
                if m >= 2:
                    pe.wait_ge(wt_done, m - 1)
                for g in range(GB):
                    at = (m % 2) * BANK + g * P
                    last = nc.tensor.transpose(p_x[:, at:at + P], wide_of(m)[:, g, :, :].rearrange("p j t -> p (j t)"),
                                               k.ident[:, :])
                last.then_inc(wt_ready, 1)

            def mix(m):
                n, a = m // HALVES, m % HALVES
                t = units[n][0]
                pe.wait_ge(wt_done, m + 1)
                if n >= 2:
                    pe.wait_ge(sized, 2 * n - 2)
                for g in range(GB):
                    at = (n % 2) * BANK + (a * GB + g) * DH
                    last = nc.tensor.matmul(p_w[:, at:at + DH], wide_t[m % 2][:, g, :], h.vhat[:, t * OG + a * GB + g, :],
                                            start=True, stop=True)
                last.then_inc(half_mixed, 1)
                if a == HALVES - 1:
                    pe.wait_ge(half_mixed, m + 1)
                    pe.sem_inc(mixed, 1)

            for m in range(len(halves) + 1):
                if m < len(halves):
                    transpose(m)
                if m:
                    mix(m - 1)
            for q in range(NG // GB):
                if q % 2 == 0:
                    pe.wait_ge(y_ready, q // 2 + 1)
                if q >= 2:
                    pe.wait_ge(yt_copied, q - 1)
                for g in range(GB):
                    at = (q % 2) * BANK + g * P
                    f = (q % 2 * GB + g) * DH
                    last = nc.tensor.transpose(p_t[0:DH, at:at + P], acc[:, q // 2, f:f + DH], k.ident[:, :])
                last.then_inc(yt_ready, 1)
            pe.wait_ge(ld_w, 32)
            for t in range(NT):
                pe.wait_ge(yt_copied, 2 * t + 2)
                if t >= 2:
                    pe.wait_ge(out_done, t - 1)
                o = p_out[:, (t % 2) * BANK:(t % 2 + 1) * BANK]
                for i in range(NH):
                    nc.tensor.matmul(o, y_t[:, i, t * P:(t + 1) * P], w_o[:, i, :], start=(i == 0), stop=False)
                nc.tensor.matmul(o, k.ones[0:1, :], b_o[0:1, :], start=False, stop=True).then_inc(out_ready, 1)


NE = 8
CAP = math.ceil(TOK / NE * 1.25)
HW = 2 * D
WC = HW // P


def experts(nc, io, k, x, xn, xt):
    with Stage(nc, "ex") as st:
        RING = 3
        w_g = st.sb("w_g", [P, DC, HW])
        w_r = st.sb("w_r", [P, DC, NE])
        w_d = [st.sb(f"w_d{i}", [P, WC, D]) for i in range(RING)]
        ld_r, ld_g = st.sems("ld_r ld_g")
        ld_d = [st.sem(f"ld_d{i}") for i in range(RING)]

        def load_down(sp, e):
            sp.dma_start(w_d[e % RING][:, :, :], io.w_d[:, e, :, :]).then_inc(ld_d[e % RING], 16)

        def load(sp):
            sp.dma_start(w_r[:, :, :], io.w_r).then_inc(ld_r, 16)
            sp.dma_start(w_g[:, :, :], io.w_g).then_inc(ld_g, 16)
            for e in range(RING):
                load_down(sp, e)

        norm_transpose(nc, "n5", x, xn, xt, k.ident, 1e-5, load=load)
        hid = st.sb("hid", [P, NT, HW])
        sel = st.sb("sel", [P, NT, NE, CAP])
        share = st.sb("share", [P, NT, NE, CAP])
        got = st.sb("got", [P, WC, NE * CAP])
        spread = st.sb("spread", [CAP, NE, TOK])
        y = st.sb("y", [CAP, NE, D])
        upto, slots = st.sb("upto", [P, P]), st.sb("slots", [P, CAP])
        before = st.sb("before", [P, NE, NE])
        gate, mask, rank, pos, comb = [st.sb(n, [P, NT, NE]) for n in "gate mask rank pos comb".split()]
        more, same = st.sb("more", [P, NT, NE, NE]), st.sb("same", [P, NT, NE, NE])
        one = st.sb("one", [P, 3, NT])
        p_a, p_b, p_o = st.ps("p_a"), st.ps("p_b", 3), st.ps("p_o", NT)
        made, gc, l_ready, max_done, exp_done, mask_done, pos_ready, chain, sel_done, h_ready, h_done, \
            g_ready, got_done, s_ready, spread_done, y_ready, y_done, out_ready, added = st.sems(
                "made gc l_ready max_done exp_done mask_done pos_ready chain sel_done h_ready h_done "
                "g_ready got_done s_ready spread_done y_ready y_done out_ready added")
        block = st.block()
        HALF = NE * CAP // 2
        b3 = lambda n: p_b[:, (n % 3) * BANK:(n % 3 + 1) * BANK]

        @block.sync
        def _(sp):
            for e in range(RING, NE):
                sp.wait_ge(y_ready, e - RING + 1)
                load_down(sp, e)

        @block.gpsimd
        def _(g):
            c = Chain(g, gc)
            c.mark(g.memset(upto[:, :], 1.0))
            c.mark(g.memset(before[:, :, :], 1.0))
            c.mark(g.iota(slots[:, :], [[1, CAP]], base=0, channel_multiplier=0, allow_small_or_imprecise_dtypes=True))
            c.settle()
            c.mark(g.affine_select(out=upto[:, :], in_=upto[:, :], compare_op=ALU.is_ge, fill=0.0, base=0,
                                   pattern=[[1, P]], channel_multiplier=-1))
            c.link(g.affine_select(out=before[:, :, :], in_=before[:, :, :], compare_op=ALU.is_gt, fill=0.0, base=0,
                                   pattern=[[1, NE], [-1, NE]], channel_multiplier=0))
            g.sem_inc(made, 1)

        @block.tensor
        def _(pe):
            pe.wait_ge(ld_r, 16)
            for t in range(NT):
                for c in range(DC):
                    last = nc.tensor.matmul(p_a[:, t * NE:(t + 1) * NE], xt[:, c, t * P:(t + 1) * P], w_r[:, c, :],
                                            start=(c == 0), stop=(c == DC - 1))
            last.then_inc(l_ready, 1)
            pe.wait_ge(ld_g, 16)
            for t in range(NT):
                for i in range(2):
                    n = 2 * t + i
                    if n >= 3:
                        pe.wait_ge(h_done, n - 2)
                    for c in range(DC):
                        last = nc.tensor.matmul(b3(n), xt[:, c, t * P:(t + 1) * P],
                                                w_g[:, c, i * BANK:(i + 1) * BANK], start=(c == 0), stop=(c == DC - 1))
                    last.then_inc(h_ready, 1)
            pe.wait_ge(made, 1)
            pe.wait_ge(mask_done, 1)
            nc.tensor.matmul(p_a[:, 0:NT * NE], upto[:, :], mask[:, :, :].rearrange("p t e -> p (t e)"), start=True,
                             stop=False)
            for t in range(NT - 1):
                rest = NT - 1 - t
                last = nc.tensor.matmul(p_a[:, (t + 1) * NE:NT * NE], k.ones[:, :],
                                        mask[:, t:t + 1, :].to_broadcast([P, rest, NE]), start=False, stop=(rest == 1))
            last.then_inc(pos_ready, 1)
            pe.wait_ge(sel_done, 1)
            for n in range(2 * WC):
                c, i = n // 2, n % 2
                pe.wait_ge(h_done, 2 * NT)
                if n >= 3:
                    pe.wait_ge(got_done, n - 2)
                for t in range(NT):
                    last = nc.tensor.matmul(b3(n)[:, 0:HALF], hid[:, t, c * P:(c + 1) * P],
                                            sel[:, t, :, :].rearrange("p e s -> p (e s)")[:, i * HALF:(i + 1) * HALF],
                                            start=(t == 0), stop=(t == NT - 1))
                last.then_inc(g_ready, 1)
            pe.wait_ge(sel_done, 2)
            for e in range(NE):
                pe.wait_ge(got_done, 2 * WC - 2 + min(e, 2))
                if e >= 3:
                    pe.wait_ge(spread_done, e - 2)
                for t in range(NT):
                    last = nc.tensor.transpose(b3(2 * WC + e)[0:CAP, t * P:(t + 1) * P], share[:, t, e, :], k.ident[:, :])
                last.then_inc(s_ready, 1)
            for e in range(NE + 1):
                if e < NE:
                    n = 2 * WC + NE + e
                    pe.wait_ge(ld_d[e % RING], 16 * (e // RING + 1))
                    if e < 3:
                        pe.wait_ge(spread_done, NE - 2 + e)
                    else:
                        pe.wait_ge(y_done, e - 2)
                    for c in range(WC):
                        last = nc.tensor.matmul(b3(n)[0:CAP, :], got[:, c, e * CAP:(e + 1) * CAP],
                                                w_d[e % RING][:, c, :], start=(c == 0), stop=(c == WC - 1))
                    last.then_inc(y_ready, 1)
                if e:
                    pe.wait_ge(y_done, e)
                    for t in range(NT):
                        ins = nc.tensor.matmul(p_o[:, t * BANK:(t + 1) * BANK], spread[:, e - 1, t * P:(t + 1) * P],
                                               y[:, e - 1, :], start=(e == 1), stop=(e == NE))
                        if e == NE:
                            ins.then_inc(out_ready, 1)

        @block.scalar
        def _(act):
            act.wait_ge(max_done, 1)
            nc.scalar.activation(gate[:, :, :], gate[:, :, :], ACT.Exp).then_inc(exp_done, 1)
            for n in range(2 * NT):
                act.wait_ge(h_ready, n + 1)
                nc.scalar.activation(hid[:, n // 2, (n % 2) * BANK:(n % 2 + 1) * BANK], b3(n), ACT.Silu).then_inc(h_done, 1)
            for n in range(2 * WC):
                act.wait_ge(g_ready, n + 1)
                nc.scalar.activation(got[:, n // 2, (n % 2) * HALF:(n % 2 + 1) * HALF], b3(n)[:, 0:HALF],
                                     ACT.Copy).then_inc(got_done, 1)
            for e in range(NE):
                act.wait_ge(y_ready, e + 1)
                nc.scalar.activation(y[:, e, :], b3(2 * WC + NE + e)[0:CAP, :], ACT.Copy).then_inc(y_done, 1)

        @block.vector
        def _(dve):
            c = Chain(dve, chain)

            def over(v):
                return v.unsqueeze(2).to_broadcast([P, NT, NE])

            dve.wait_ge(l_ready, 1)
            logit = p_a[:, 0:NT * NE].rearrange("p (t e) -> p t e", e=NE)
            c.link(nc.vector.tensor_reduce(one[:, 0, :], logit, AX.X, ALU.max))
            nc.vector.tensor_tensor(gate[:, :, :], logit, over(one[:, 0, :]), ALU.subtract).then_inc(max_done, 1)
            dve.wait_ge(exp_done, 1)
            c.link(nc.vector.tensor_reduce(one[:, 1, :], gate[:, :, :], AX.X, ALU.add))
            c.link(nc.vector.reciprocal(one[:, 2, :], one[:, 1, :]))
            c.link(nc.vector.tensor_tensor(gate[:, :, :], gate[:, :, :], over(one[:, 2, :]), ALU.mult))
            other = gate[:, :, :].unsqueeze(2).to_broadcast([P, NT, NE, NE])
            own = gate[:, :, :].unsqueeze(3).to_broadcast([P, NT, NE, NE])
            c.mark(nc.vector.tensor_tensor(more[:, :, :, :], other, own, ALU.is_gt))
            c.link(nc.vector.tensor_tensor(same[:, :, :, :], other, own, ALU.is_equal))
            dve.wait_ge(made, 1)
            c.link(nc.vector.tensor_tensor(same[:, :, :, :], same[:, :, :, :],
                                           before[:, :, :].unsqueeze(1).to_broadcast([P, NT, NE, NE]), ALU.mult))
            c.link(nc.vector.tensor_tensor(more[:, :, :, :], more[:, :, :, :], same[:, :, :, :], ALU.add))
            c.link(nc.vector.tensor_reduce(rank[:, :, :], more[:, :, :, :], AX.X, ALU.add))
            nc.vector.tensor_scalar(mask[:, :, :], rank[:, :, :], 2.0, None, ALU.is_lt).then_inc(mask_done, 1)
            dve.wait_ge(pos_ready, 1)
            dve.wait_ge(mask_done, 1)
            c.link(nc.vector.tensor_copy(pos[:, :, :], logit))
            c.link(nc.vector.scalar_tensor_tensor(rank[:, :, :], pos[:, :, :], float(CAP), mask[:, :, :], ALU.is_le,
                                                  ALU.mult))
            c.mark(nc.vector.tensor_tensor(comb[:, :, :], gate[:, :, :], rank[:, :, :], ALU.mult))
            c.link(nc.vector.tensor_tensor(pos[:, :, :], pos[:, :, :], rank[:, :, :], ALU.mult))
            c.mark(nc.vector.tensor_scalar(pos[:, :, :], pos[:, :, :], -1.0, None, ALU.add))
            c.link(nc.vector.tensor_reduce(one[:, 0, :], comb[:, :, :], AX.X, ALU.add))
            c.link(nc.vector.tensor_scalar(one[:, 1, :], one[:, 0, :], 1e-6, None, ALU.add))
            c.link(nc.vector.reciprocal(one[:, 2, :], one[:, 1, :]))
            c.link(nc.vector.tensor_tensor(comb[:, :, :], comb[:, :, :], over(one[:, 2, :]), ALU.mult))
            te = "p t e -> p (t e)"
            full = [P, NT * NE, CAP]
            nc.vector.tensor_tensor(sel[:, :, :, :].rearrange("p t e s -> p (t e) s"),
                                    slots[:, :].unsqueeze(1).to_broadcast(full),
                                    pos[:, :, :].rearrange(te).unsqueeze(2).to_broadcast(full),
                                    ALU.is_equal).then_inc(sel_done, 1)
            dve.wait_ge(sel_done, 1)
            nc.vector.tensor_tensor(share[:, :, :, :].rearrange("p t e s -> p (t e) s"),
                                    sel[:, :, :, :].rearrange("p t e s -> p (t e) s"),
                                    comb[:, :, :].rearrange(te).unsqueeze(2).to_broadcast(full),
                                    ALU.mult).then_inc(sel_done, 1)
            for e in range(NE):
                dve.wait_ge(s_ready, e + 1)
                nc.vector.tensor_copy(spread[:, e, :], b3(2 * WC + e)[0:CAP, :]).then_inc(spread_done, 1)
            for t in range(NT):
                dve.wait_ge(out_ready, t + 1)
                nc.vector.tensor_tensor(x[:, t, :], x[:, t, :], p_o[:, t * BANK:(t + 1) * BANK],
                                        ALU.add).then_inc(added, 1)
            dve.wait_ge(added, NT)


STAGES = [depool_stream, mamba, bitnet, cross_attention, head_attention, experts]


class Namespace:
    pass


def build(nc, io):
    with ExitStack() as stack:
        def sb(name, shape, dt=f32):
            return stack.enter_context(nc.sbuf_tensor(name, shape, dt))

        x = sb("x", [P, NT, D])
        work = sb("work", [P, NT * D + DC * TOK])
        xn = work[:, 0:NT * D].rearrange("p (t d) -> p t d", d=D)
        xt = work[:, NT * D:].rearrange("p (c t) -> p c t", t=TOK)
        stored = nc.alloc_semaphore(name="stored")
        k = Namespace()
        k.ident, k.ones = sb("ident", [P, P]), sb("ones", [P, P])
        k.ident_h, k.ident_f = sb("ident_h", [P, P], bf16), sb("ident_f", [P, P], f16)
        k.cols = sb("cols", [P, io.cols.shape[1]])
        with Stage(nc, "start") as st:
            loaded, made = st.sems("loaded made")
            block = st.block()

            @block.sync
            def _(sp):
                sp.dma_start(x[:, :, :], io.x).then_inc(loaded, 16)
                sp.dma_start(k.cols[:, :], io.cols).then_inc(loaded, 16)
                sp.wait_ge(loaded, 32)

            @block.gpsimd
            def _(g):
                g.memset(k.ones[:, :], 1.0).then_inc(made, 1)
                g.memset(k.ident[:, :], 0.0).then_inc(made, 1)
                g.wait_ge(made, 2)
                g.affine_select(out=k.ident[:, :], in_=k.ident[:, :], compare_op=ALU.not_equal, fill=1.0,
                                base=0, pattern=[[-1, P]], channel_multiplier=1).then_inc(made, 1)
                g.wait_ge(made, 3)
                g.tensor_copy(k.ident_h[:, :], k.ident[:, :]).then_inc(made, 1)
                g.tensor_copy(k.ident_f[:, :], k.ident[:, :]).then_inc(made, 1)
                g.wait_ge(made, 5)
        for stage in STAGES:
            stage(nc, io, k, x, xn, xt, *([work[:, :]] if stage.__name__ == "cross_attention" else []))
        with Stage(nc, "end") as st:
            block = st.block()

            @block.sync
            def _(sp):
                sp.dma_start(io.out, x[:, :, :]).then_inc(stored, 16)
                sp.wait_ge(stored, 16)


def more_data(a, data, rows, columns):
    data["in_proj"] = rows(a["L0_attn_in_proj_w"].T)
    data["x_proj"] = rows(a["L0_attn_x_proj_w"].T)
    data["dt_proj"] = a["L0_attn_dt_proj_w"].T
    data["a_log"] = rows(a["L0_attn_A_log"])
    data["out_proj"] = rows(a["L0_attn_out_proj_w"].T)
    data["w1"] = rows(a["L0_ffn_W1"].T)
    data["w2"] = rows(a["L0_ffn_W2"].T)
    data["b1"] = a["L0_ffn_b1"]
    data["b2"] = a["L0_ffn_b2"]
    data["w_q"] = rows(a["L1_xattn_Wq"])
    data["w_kv"] = rows(a["L1_xattn_Wkv"])
    data["null_k"] = np.tile(a["L1_xattn_null_kv"][0], 2)[:, None]
    data["null_v"] = np.tile(a["L1_xattn_null_kv"][1], P // DH * GP)[None]
    whole = np.zeros((B, JT * P, CW), np.float32)
    whole[:, :CTX] = a["ctx_2048"]
    data["ctx_t"] = whole.reshape(B, JT, P, CC, P).transpose(0, 1, 4, 3, 2).reshape(B, JT, P, CC * P)
    data["w_out"] = rows(a["L1_xattn_Wout"])
    data["ln_scale"] = a["L1_xattn_ln_scale"]
    data["ln_bias"] = a["L1_xattn_ln_bias"]
    wqkv, bqkv = a["L1_attn_W_qkv"], a["L1_attn_b_qkv"]
    data["w_qk"] = np.repeat(rows(wqkv[:2 * D].T).reshape(P, DC, 2 * NH, 1, DH), 2, axis=3)
    data["w_v"] = rows(wqkv[2 * D:].T)
    data["b_qk"] = np.tile(bqkv[:2 * D].reshape(2 * NH, DH).T, (2, 1))
    data["b_v"] = bqkv[2 * D:].reshape(NH, DH).T
    feature = np.arange(DH)
    phase = a["L1_attn_photonic_phases"][feature % 16, feature]
    data["phase"] = np.tile(phase, 2)[:, None]
    data["head_rows"] = np.concatenate([
        a["L1_attn_entanglement_gates"][:, :NH - 1, :2].transpose(2, 0, 1).reshape(-1), phase,
        a["L1_attn_quantum_weights"][:, 0, 0], a["L1_attn_superposition_logits"]])
    data["w_o"] = a["L1_attn_W_out"].T.reshape(NH, DH, D).transpose(1, 0, 2)
    data["b_o"] = a["L1_attn_b_out"][None]
    data["w_r"] = rows(a["L1_ffn_w_router"].T)
    data["w_g"] = rows(a["L1_ffn_w_gate"].T)
    data["w_d"] = a["L1_ffn_w_down"].transpose(0, 2, 1).reshape(NE, WC, P, D).transpose(2, 0, 1, 3)


def kernel(**inputs):
    import concourse.bacc as bacc
    from concourse.bass_utils import run_bass_kernel_spmd

    a = {n: np.ascontiguousarray(v) for n, v in inputs.items()}

    def rows(w):
        return np.ascontiguousarray(w.reshape(-1, P, w.shape[1]).transpose(1, 0, 2))

    def columns(v):
        return v.reshape(-1, P).T

    ctx, lens = a["ctx_2048"], a["mask_BxS2_if0"]
    tiles = -(-CTX // P)
    padded = np.zeros((tiles * P, B), lens.dtype)
    padded[:CTX] = lens.T
    data = {
        "x": a["x"].reshape(NT, P, D).transpose(1, 0, 2),
        "lens": padded.reshape(tiles, P, B).transpose(1, 0, 2),
        "patches": ctx[:, :S, :].reshape(NT, P, CW).transpose(1, 0, 2),
        "w_in": rows(a["L0_xattn_W_in"].T),
        "b_in": a["L0_xattn_b_in"][None],
        "g_init": a["L0_xattn_g_init"][:D],
        "cols": np.concatenate([
            columns(a["L0_xattn_g_res"]), columns(a["L0_attn_conv_b"]), columns(a["L0_attn_D"]),
            columns(a["L0_attn_dt_proj_b"]),
            a["L0_attn_conv_w"].reshape(-1, P, 4).transpose(1, 0, 2).reshape(P, -1)], axis=1),
    }
    more_data(a, data, rows, columns)
    nc = bacc.Bacc("TRN2", target_bir_lowering=False, num_devices=1)
    io = Namespace()
    arrays = {}
    for name, v in data.items():
        v = np.ascontiguousarray(v)
        arrays[f"in_{name}"] = v
        io.__dict__[name] = nc.dram_tensor(f"in_{name}", v.shape, mybir.dt.from_np(v.dtype), kind="ExternalInput").ap()
    io.out = nc.dram_tensor("out", (P, NT, D), f32, kind="ExternalOutput").ap()
    build(nc, io)
    got = run_bass_kernel_spmd(nc, [arrays], core_ids=[0]).results[0]["out"]
    return got.transpose(1, 0, 2).reshape(B, S, D)
```
